# Optimizing a Trainium2 kernel written in Bass

```python
import numpy as np
import jax
import jax.numpy as jnp

def _softmax(x, axis=-1):
    return jax.nn.softmax(x, axis=axis)

def _gelu(x):
    return jax.nn.gelu(x, approximate=True)

def _silu(x):
    return jax.nn.silu(x)

def _sigmoid(x):
    return jax.nn.sigmoid(x)

def _layernorm(x, axis=-1, eps=1e-05):
    m = jnp.mean(x, axis=axis, keepdims=True)
    v = jnp.var(x, axis=axis, keepdims=True)
    return (x - m) / jnp.sqrt(v + eps)

def _scatter_add(tgt, idx, src, axis=0):
    return tgt.at[idx].add(src)

def _segment_sum(src, seg, n):
    return jax.ops.segment_sum(src, seg, n)
kernel_name = 'mk_sandwich_d1_jaxref_r8_712bd5'

def setup_inputs(seed: int=0):
    np.random.seed(seed)
    _w = jnp.asarray

    def _L0_attn_setup():
        import jax, jax.numpy as jnp
        import numpy as np
        WINDOWP = 64
        LN_EPS = 1e-05

        def _layer_norm(y, g, b):
            mu = jnp.mean(y, axis=-1, keepdims=True)
            var = jnp.mean((y - mu) ** 2, axis=-1, keepdims=True)
            return (y - mu) * jax.lax.rsqrt(var + LN_EPS) * g + b
        key = jax.random.key(seed)
        ks = jax.random.split(key, 4)
        B, T, D = (8, 256, 128)
        feature = jax.random.normal(ks[0], (B, T, D), dtype=jnp.float32)
        wq_w = jax.random.normal(ks[1], (D, D), dtype=jnp.float32) * 0.02
        wq_b = jnp.zeros((D,), dtype=jnp.float32)
        w2_w = jax.random.normal(ks[2], (D,), dtype=jnp.float32) * 0.02
        w2_b = jnp.zeros((1,), dtype=jnp.float32)
        ln_g = jnp.ones((D,), dtype=jnp.float32)
        ln_b = jnp.zeros((D,), dtype=jnp.float32)
        return {'feature': feature, 'wq_w': wq_w, 'wq_b': wq_b, 'w2_w': w2_w, 'w2_b': w2_b, 'ln_g': ln_g, 'ln_b': ln_b}
    _L0_attn_in = _L0_attn_setup()

    def _L0_ffn_setup():
        import jax, jax.numpy as jnp
        import numpy as np
        from math import sqrt
        B, S, D, H, E, K, FF = (2, 128, 128, 16, 8, 2, 512)
        HD = D // H
        EPS = 1e-05

        def _rope_cache(seq_len, hd):
            inv_freq = 1.0 / 10000.0 ** (jnp.arange(0, hd, 2, dtype=jnp.float32) / hd)
            t = jnp.arange(seq_len, dtype=jnp.float32)
            freqs = t[:, None] * inv_freq[None, :]
            emb = jnp.concatenate([freqs, freqs], axis=-1)
            return (jnp.cos(emb), jnp.sin(emb))

        def _rotate_half(x):
            x1, x2 = jnp.split(x, 2, axis=-1)
            return jnp.concatenate([-x2, x1], axis=-1)

        def _layernorm(x, g, b):
            m = jnp.mean(x, axis=-1, keepdims=True)
            v = jnp.var(x, axis=-1, keepdims=True)
            return (x - m) * jax.lax.rsqrt(v + EPS) * g + b

        def _forward(x, Wq, bq, Wk, bk, Wv, bv, Wo, bo, Wg, bg, W1, b1, W2, b2, g1, be1, g2, be2):
            bsz, seq, d = x.shape
            q = (x @ Wq + bq).reshape(bsz, seq, H, HD).transpose(0, 2, 1, 3)
            k = (x @ Wk + bk).reshape(bsz, seq, H, HD).transpose(0, 2, 1, 3)
            v = (x @ Wv + bv).reshape(bsz, seq, H, HD).transpose(0, 2, 1, 3)
            cos, sin = _rope_cache(seq, HD)
            cos = cos[None, None]
            sin = sin[None, None]
            q = q * cos + _rotate_half(q) * sin
            k = k * cos + _rotate_half(k) * sin
            scores = jnp.einsum('bhqd,bhkd->bhqk', q, k) / sqrt(HD)
            attn = jax.nn.softmax(scores, axis=-1)
            ao = jnp.einsum('bhqk,bhkd->bhqd', attn, v)
            ao = ao.transpose(0, 2, 1, 3).reshape(bsz, seq, d)
            attn_out = ao @ Wo + bo
            x1 = _layernorm(x + attn_out, g1, be1)
            gate_logits = x1 @ Wg + bg
            gate_probs = jax.nn.softmax(gate_logits, axis=-1)
            topk_p, topk_i = jax.lax.top_k(gate_probs, K)
            topk_p = topk_p / jnp.sum(topk_p, axis=-1, keepdims=True)
            comb = jnp.sum(jax.nn.one_hot(topk_i, E, dtype=x.dtype) * topk_p[..., None], axis=-2)
            h = jax.nn.gelu(jnp.einsum('bsd,edf->bsef', x1, W1) + b1, approximate=False)
            y = jnp.einsum('bsef,efd->bsed', h, W2) + b2
            moe_out = jnp.einsum('bse,bsed->bsd', comb, y)
            return _layernorm(x1 + moe_out, g2, be2)
        key = jax.random.key(seed)
        ks = jax.random.split(key, 20)
        std = 0.02
        p = lambda k, sh: jax.random.normal(k, sh, dtype=jnp.float32) * std
        return {'x': jax.random.normal(ks[0], (B, S, D), dtype=jnp.float32), 'Wq': p(ks[1], (D, D)), 'bq': jnp.zeros((D,), jnp.float32), 'Wk': p(ks[2], (D, D)), 'bk': jnp.zeros((D,), jnp.float32), 'Wv': p(ks[3], (D, D)), 'bv': jnp.zeros((D,), jnp.float32), 'Wo': p(ks[4], (D, D)), 'bo': jnp.zeros((D,), jnp.float32), 'Wg': p(ks[5], (D, E)), 'bg': jnp.zeros((E,), jnp.float32), 'W1': p(ks[6], (E, D, FF)), 'b1': jnp.zeros((E, FF), jnp.float32), 'W2': p(ks[7], (E, FF, D)), 'b2': jnp.zeros((E, D), jnp.float32), 'g1': jnp.ones((D,), jnp.float32), 'be1': jnp.zeros((D,), jnp.float32), 'g2': jnp.ones((D,), jnp.float32), 'be2': jnp.zeros((D,), jnp.float32)}
    _L0_ffn_in = _L0_ffn_setup()
    _d = {'L0_attn_feature': _L0_attn_in['feature'], 'L0_attn_wq_w': _L0_attn_in['wq_w'], 'L0_attn_wq_b': _L0_attn_in['wq_b'], 'L0_attn_w2_w': _L0_attn_in['w2_w'], 'L0_attn_w2_b': _L0_attn_in['w2_b'], 'L0_attn_ln_g': _L0_attn_in['ln_g'], 'L0_attn_ln_b': _L0_attn_in['ln_b'], 'L0_ffn_Wq': _L0_ffn_in['Wq'], 'L0_ffn_bq': _L0_ffn_in['bq'], 'L0_ffn_Wk': _L0_ffn_in['Wk'], 'L0_ffn_bk': _L0_ffn_in['bk'], 'L0_ffn_Wv': _L0_ffn_in['Wv'], 'L0_ffn_bv': _L0_ffn_in['bv'], 'L0_ffn_Wo': _L0_ffn_in['Wo'], 'L0_ffn_bo': _L0_ffn_in['bo'], 'L0_ffn_Wg': _L0_ffn_in['Wg'], 'L0_ffn_bg': _L0_ffn_in['bg'], 'L0_ffn_W1': _L0_ffn_in['W1'], 'L0_ffn_b1': _L0_ffn_in['b1'], 'L0_ffn_W2': _L0_ffn_in['W2'], 'L0_ffn_b2': _L0_ffn_in['b2'], 'L0_ffn_g1': _L0_ffn_in['g1'], 'L0_ffn_be1': _L0_ffn_in['be1'], 'L0_ffn_g2': _L0_ffn_in['g2'], 'L0_ffn_be2': _L0_ffn_in['be2']}
    _x0 = _d['L0_attn_feature']
    _d['L0_attn_feature'] = jax.random.normal(jax.random.fold_in(jax.random.key(seed), 1), (4, 1024, 128), dtype=_x0.dtype)
    del _x0
    return _d

def reference(L0_attn_feature, L0_attn_wq_w, L0_attn_wq_b, L0_attn_w2_w, L0_attn_w2_b, L0_attn_ln_g, L0_attn_ln_b, L0_ffn_Wq, L0_ffn_bq, L0_ffn_Wk, L0_ffn_bk, L0_ffn_Wv, L0_ffn_bv, L0_ffn_Wo, L0_ffn_bo, L0_ffn_Wg, L0_ffn_bg, L0_ffn_W1, L0_ffn_b1, L0_ffn_W2, L0_ffn_b2, L0_ffn_g1, L0_ffn_be1, L0_ffn_g2, L0_ffn_be2):

    def _L0_attn_ref(feature, wq_w, wq_b, w2_w, w2_b, ln_g, ln_b):
        import jax, jax.numpy as jnp
        import numpy as np
        WINDOWP = 64
        LN_EPS = 1e-05

        def _layer_norm(y, g, b):
            mu = jnp.mean(y, axis=-1, keepdims=True)
            var = jnp.mean((y - mu) ** 2, axis=-1, keepdims=True)
            return (y - mu) * jax.lax.rsqrt(var + LN_EPS) * g + b
        B, T, D = feature.shape
        W = WINDOWP
        q_local = feature @ wq_w + wq_b
        init_buf = feature[:, :W, :]

        def step(buf, q_i):
            ki = jnp.concatenate([buf, jnp.zeros((B, 1, D), feature.dtype)], axis=1)
            scores = jnp.einsum('bwd,d->bw', q_i[:, None, :] * ki, w2_w) + w2_b[0]
            alpha = jax.nn.softmax(scores, axis=1)
            v_i = jnp.einsum('bwd,bw->bd', ki, alpha)
            new_buf = jnp.concatenate([buf[:, 1:, :], v_i[:, None, :]], axis=1)
            return (new_buf, v_i)
        qs = jnp.transpose(q_local[:, W:, :], (1, 0, 2))
        _, vs = jax.lax.scan(step, init_buf, qs)
        v_local = jnp.concatenate([feature[:, :W, :], jnp.transpose(vs, (1, 0, 2))], axis=1)
        y = jnp.tanh(v_local) * feature + feature
        return _layer_norm(y, ln_g, ln_b)

    def _L0_ffn_ref(x, Wq, bq, Wk, bk, Wv, bv, Wo, bo, Wg, bg, W1, b1, W2, b2, g1, be1, g2, be2):
        import jax, jax.numpy as jnp
        import numpy as np
        from math import sqrt
        B, S, D, H, E, K, FF = (2, 128, 128, 16, 8, 2, 512)
        HD = D // H
        EPS = 1e-05

        def _rope_cache(seq_len, hd):
            inv_freq = 1.0 / 10000.0 ** (jnp.arange(0, hd, 2, dtype=jnp.float32) / hd)
            t = jnp.arange(seq_len, dtype=jnp.float32)
            freqs = t[:, None] * inv_freq[None, :]
            emb = jnp.concatenate([freqs, freqs], axis=-1)
            return (jnp.cos(emb), jnp.sin(emb))

        def _rotate_half(x):
            x1, x2 = jnp.split(x, 2, axis=-1)
            return jnp.concatenate([-x2, x1], axis=-1)

        def _layernorm(x, g, b):
            m = jnp.mean(x, axis=-1, keepdims=True)
            v = jnp.var(x, axis=-1, keepdims=True)
            return (x - m) * jax.lax.rsqrt(v + EPS) * g + b

        def _forward(x, Wq, bq, Wk, bk, Wv, bv, Wo, bo, Wg, bg, W1, b1, W2, b2, g1, be1, g2, be2):
            bsz, seq, d = x.shape
            q = (x @ Wq + bq).reshape(bsz, seq, H, HD).transpose(0, 2, 1, 3)
            k = (x @ Wk + bk).reshape(bsz, seq, H, HD).transpose(0, 2, 1, 3)
            v = (x @ Wv + bv).reshape(bsz, seq, H, HD).transpose(0, 2, 1, 3)
            cos, sin = _rope_cache(seq, HD)
            cos = cos[None, None]
            sin = sin[None, None]
            q = q * cos + _rotate_half(q) * sin
            k = k * cos + _rotate_half(k) * sin
            scores = jnp.einsum('bhqd,bhkd->bhqk', q, k) / sqrt(HD)
            attn = jax.nn.softmax(scores, axis=-1)
            ao = jnp.einsum('bhqk,bhkd->bhqd', attn, v)
            ao = ao.transpose(0, 2, 1, 3).reshape(bsz, seq, d)
            attn_out = ao @ Wo + bo
            x1 = _layernorm(x + attn_out, g1, be1)
            gate_logits = x1 @ Wg + bg
            gate_probs = jax.nn.softmax(gate_logits, axis=-1)
            topk_p, topk_i = jax.lax.top_k(gate_probs, K)
            topk_p = topk_p / jnp.sum(topk_p, axis=-1, keepdims=True)
            comb = jnp.sum(jax.nn.one_hot(topk_i, E, dtype=x.dtype) * topk_p[..., None], axis=-2)
            h = jax.nn.gelu(jnp.einsum('bsd,edf->bsef', x1, W1) + b1, approximate=False)
            y = jnp.einsum('bsef,efd->bsed', h, W2) + b2
            moe_out = jnp.einsum('bse,bsed->bsd', comb, y)
            return _layernorm(x1 + moe_out, g2, be2)
        return _forward(x, Wq, bq, Wk, bk, Wv, bv, Wo, bo, Wg, bg, W1, b1, W2, b2, g1, be1, g2, be2)
    x = L0_attn_feature
    x = x + _layernorm(_L0_attn_ref(_layernorm(x, axis=-1), L0_attn_wq_w, L0_attn_wq_b, L0_attn_w2_w, L0_attn_w2_b, L0_attn_ln_g, L0_attn_ln_b), axis=-1)
    x = x + _layernorm(_L0_ffn_ref(_layernorm(x, axis=-1), L0_ffn_Wq, L0_ffn_bq, L0_ffn_Wk, L0_ffn_bk, L0_ffn_Wv, L0_ffn_bv, L0_ffn_Wo, L0_ffn_bo, L0_ffn_Wg, L0_ffn_bg, L0_ffn_W1, L0_ffn_b1, L0_ffn_W2, L0_ffn_b2, L0_ffn_g1, L0_ffn_be1, L0_ffn_g2, L0_ffn_be2), axis=-1)
    return x

_drawn_inputs = setup_inputs


def setup_inputs(seed=0):
    import zlib

    import numpy as np

    out = dict(_drawn_inputs(seed))
    spreads = {'L0_attn_wq_b': (0.0, 0.8),
     'L0_attn_ln_g': (1.0, 0.2),
     'L0_attn_ln_b': (0.0, 0.1),
     'L0_ffn_bq': (0.0, 0.8),
     'L0_ffn_bk': (0.0, 0.8),
     'L0_ffn_bv': (0.0, 0.8),
     'L0_ffn_bo': (0.0, 0.337),
     'L0_ffn_bg': (0.0, 0.574),
     'L0_ffn_b1': (0.0, 0.8),
     'L0_ffn_b2': (0.0, 0.362),
     'L0_ffn_g1': (1.0, 0.2),
     'L0_ffn_be1': (0.0, 0.1),
     'L0_ffn_g2': (1.0, 0.2),
     'L0_ffn_be2': (0.0, 0.1)}
    factors = {'L0_attn_wq_w': 8.0,
     'L0_attn_w2_w': 8.0,
     'L0_ffn_Wq': 8.0,
     'L0_ffn_Wk': 8.0,
     'L0_ffn_Wv': 8.0,
     'L0_ffn_Wo': 7.044,
     'L0_ffn_W1': 4.494,
     'L0_ffn_W2': 4.019}
    for name, (base, spread) in spreads.items():
        noise = np.random.default_rng([zlib.crc32(name.encode()), seed]).standard_normal(out[name].shape)
        drawn = base * np.exp(spread * noise) if base else spread * noise
        out[name] = jnp.asarray(drawn.astype(out[name].dtype))
    for name, factor in factors.items():
        out[name] = (out[name] * factor).astype(out[name].dtype)
    return out
```

```python
from contextlib import ExitStack

import numpy as np

import concourse.bass as bass
from concourse import mybir

F32 = mybir.dt.float32
BF16 = mybir.dt.bfloat16
U32 = mybir.dt.uint32
ALU = mybir.AluOpType
ACT = mybir.ActivationFunctionType
AX = mybir.AxisListType

P = 128
B, T, D = 4, 1024, 128
WIN = 64
L = 32
NK = T // L
NC = NK - WIN // L
ROW = WIN + 1

H, HD = 16, 8
HP = H // 2
E, FF = 8, 512
FC = FF // P
QT = T // P
HALF = T // 2
VH = HD + 1
SCALE = 1.0 / float(np.sqrt(HD))
Q_PARTS = (0, 0, 1, 0, 1, 2)
K_PARTS = (0, 1, 0, 2, 1, 0)
M_ROW = HD * len(Q_PARTS)
EPS = 1e-5


def window_attention(nc, io, xt, w, s_weights):
    ctx = ExitStack()
    with ctx:
        def sb(name, shape, dt=F32):
            return ctx.enter_context(nc.sbuf_tensor(name, shape, dt))

        def ps(name, shape, dt=F32):
            return ctx.enter_context(nc.psum_tensor(name, shape, dt))

        def sem(name):
            return ctx.enter_context(nc.semaphore(name))

        f, v_all, x = xt["f"], xt["v_all"], xt["x"]
        ident, eps = xt["ident"], xt["eps"]
        mask = sb("mask", [P, B, L])
        wq = sb("wq", [P, D])
        bq = sb("bq", [P, 1])
        w2 = sb("w2", [P, 1])
        b0 = sb("b0", [P, 1])
        b0_row = sb("b0_row", [P, L])
        zero_row = sb("zero_row", [P, L])
        stats = sb("stats", [P, NK, 6])
        mv = sb("mv", [P, NK, 2])
        std = sb("std", [P, NK])
        rstd = sb("rstd", [P, NK])
        ft = sb("ft", [P, 2, 4 * P])
        qt = sb("qt", [P, NK + 1, P])
        qn = sb("qn", [P, P])
        vt1 = sb("vt1", [P, P])
        vt2 = sb("vt2", [P, P])
        vr = sb("vr", [P, D])
        bdg = sb("bdg", [P, 2, P])
        bdc = sb("bdc", [P, 2, P])
        tab = sb("tab", [P, 3, WIN + L])
        row = sb("row", [P, 2, ROW])
        nmax = sb("nmax", [P, 2])
        ex = sb("ex", [P, 2, ROW])
        z = sb("z", [P, 2])
        rz = sb("rz", [P, 2])
        junk = sb("junk", [P, 3, ROW])

        pf = ps("pf", [P, 2, 4 * P])
        pq = ps("pq", [P, 2, 4 * P])
        p_s = ps("p_s", [P, 512])
        p_g = ps("p_g", [P, 512])
        p_v = ps("p_v", [P, 512])
        p_t = ps("p_t", [P, 512])

        s_x = [sem(f"s_x{b}") for b in range(B)]
        s_w = sem("s_w")
        s_const, s_ident, s_mask = sem("s_const"), sem("s_ident"), sem("s_mask")
        s_stats, s_mv, s_std, s_rstd, s_f = sem("s_stats"), sem("s_mv"), sem("s_std"), sem("s_rstd"), sem("s_f")
        s_ft, s_ftc, s_pq, s_qt = sem("s_ft"), sem("s_ftc"), sem("s_pq"), sem("s_qt")
        s_init = sem("s_init")
        s_pace = sem("s_pace")
        s_vt0 = sem("s_vt0")
        s_qn = sem("s_qn")
        s_table = sem("s_table")
        s_scores = sem("s_scores")
        s_row, s_max, s_exp, s_rz, s_new, s_coef = (sem("s_row"), sem("s_max"), sem("s_exp"), sem("s_rz"),
                                                   sem("s_new"), sem("s_coef"))
        s_clear = sem("s_clear")
        s_bdc, s_pv, s_vr, s_vall, s_pt, s_vt2, s_vt1, s_g, s_bdg = (
            sem("s_bdc"), sem("s_pv"), sem("s_vr"), sem("s_vall"), sem("s_pt"), sem("s_vt2"), sem("s_vt1"),
            sem("s_g"), sem("s_bdg"))

        block = ctx.enter_context(nc.Block())

        @block.sync
        def _(sp):
            for b in range(B):
                sp.dma_start(x[L * b:L * b + L, :, :],
                             io["x"][b].rearrange("(k j) d -> j k d", j=L)).then_inc(s_x[b], 16)
            sp.dma_start(wq[:, :], io["wq_w"]).then_inc(s_w, 16)
            sp.dma_start(bq[:, :], io["wq_b"].rearrange("(d a) -> d a", a=1)).then_inc(s_w, 16)
            sp.dma_start(w2[:, :], io["w2_w"].rearrange("(d a) -> d a", a=1)).then_inc(s_w, 16)
            sp.dma_start(b0[:, :], io["w2_b"].rearrange("(d a) -> d a", a=1).broadcast_to((P, 1))).then_inc(s_w, 16)
            sp.wait_ge(s_weights, load_constants(sp, w, io, s_weights))

        @block.gpsimd
        def _(pool):
            nc.gpsimd.memset(eps[:, :], EPS).then_inc(s_const, 1)
            nc.gpsimd.memset(zero_row[:, :], 0.0).then_inc(s_const, 1)
            nc.gpsimd.memset(ident[:, :], 0.0).then_inc(s_ident, 1)
            pool.wait_ge(s_ident, 1)
            nc.gpsimd.affine_select(out=ident[:, :], in_=ident[:, :], compare_op=ALU.not_equal, fill=1.0, base=0,
                                    pattern=[[-1, P]], channel_multiplier=1).then_inc(s_ident, 1)
            nc.gpsimd.memset(mask[:, :, :], 1.0).then_inc(s_mask, 1)
            pool.wait_ge(s_mask, 1)
            nc.gpsimd.affine_select(out=mask[:, :, :], in_=mask[:, :, :], compare_op=ALU.is_ge, fill=0.0, base=0,
                                    pattern=[[-L, B], [0, L]], channel_multiplier=1).then_inc(s_mask, 1)
            pool.wait_ge(s_mask, 2)
            nc.gpsimd.affine_select(out=mask[:, :, :], in_=mask[:, :, :], compare_op=ALU.is_ge, fill=0.0, base=L - 1,
                                    pattern=[[L, B], [0, L]], channel_multiplier=-1).then_inc(s_mask, 1)
            pool.wait_ge(s_mask, 3)
            pool.wait_ge(s_f, 2)
            nc.gpsimd.tensor_copy(v_all[:, 0, :], f[:, 1, :]).then_inc(s_init, 1)
            nc.gpsimd.tensor_copy(v_all[:, 1, :], f[:, 0, :]).then_inc(s_vall, 1)
            nc.gpsimd.memset(bdc[:, 1, :], 0.0).then_inc(s_init, 1)
            nc.gpsimd.tensor_copy(bdc[:, 0, :], ident[:, :]).then_inc(s_bdc, 1)
            pool.wait_ge(s_qt, 1)
            nc.gpsimd.tensor_copy(qn[:, :], qt[:, 2, :]).then_inc(s_qn, 1)
            with pool.Fori(0, NC) as c:
                pool.wait_ge(s_vr, c + 1)
                pool.sem_inc(s_pace, 1)
                nc.gpsimd.tensor_copy(v_all[:, c + 2, :], vr[:, :]).then_inc(s_vall, 1)
                pool.wait_ge(s_scores, c + 1)
                pool.sem_inc(s_pace, 1)
                nc.gpsimd.tensor_copy(vt2[:, :], vt1[:, :]).then_inc(s_vt2, 1)
                nc.gpsimd.tensor_copy(qn[:, :], qt[:, c + 3, :]).then_inc(s_qn, 1)
                pool.wait_ge(s_coef, L * (c + 1))
                pool.wait_ge(s_pv, c + 1)
                for g in range(2):
                    last = nc.gpsimd.tensor_tensor(
                        bdc[:, g, :].rearrange("p (b j) -> p b j", b=B),
                        tab[:, 1 + g, WIN:].unsqueeze(1).broadcast_to((P, B, L)), mask[:, :, :], ALU.mult)
                last.then_inc(s_bdc, 1)

        @block.scalar
        def _(act):
            act.wait_ge(s_mv, NK)
            act.wait_ge(s_const, 2)
            nc.scalar.activation(std[:, :], mv[:, :, 1], ACT.Sqrt, bias=eps[:, :]).then_inc(s_std, 1)
            for g in range(8):
                act.wait_ge(s_ft, g + 1)
                if g >= 2:
                    act.wait_ge(s_pq, g - 1)
                if g == 2:
                    act.wait_ge(s_vt0, 2)
                nc.scalar.copy(ft[:, g % 2, :], pf[:, g % 2, :]).then_inc(s_ftc, 1)
            with act.Fori(0, NC) as c:
                for r in range(L):
                    act.wait_ge(s_max, L * c + r + 1)
                    nc.scalar.activation(ex[:, r % 2, :], row[:, r % 2, :], ACT.Exp, bias=nmax[:, r % 2:r % 2 + 1],
                                         accum_out=z[:, r % 2:r % 2 + 1]).then_inc(s_exp, 1)

        @block.vector
        def _(dve):
            for b in range(B):
                dve.wait_ge(s_x[b], 16)
            for k in range(NK):
                nc.vector.bn_stats(stats[:, k, :], x[:, k, :]).then_inc(s_stats, 1)
            for k in range(NK):
                dve.wait_ge(s_stats, k + 1)
                nc.vector.bn_aggr(mv[:, k, :], stats[:, k, :]).then_inc(s_mv, 1)
            dve.wait_ge(s_std, 1)
            nc.vector.reciprocal(rstd[:, :], std[:, :]).then_inc(s_rstd, 1)
            dve.wait_ge(s_rstd, 1)
            for k in range(NK):
                nc.vector.tensor_scalar(f[:, k, :], x[:, k, :], mv[:, k, 0:1], rstd[:, k:k + 1], ALU.subtract,
                                        ALU.mult).then_inc(s_f, 1)
            dve.wait_ge(s_w, 64)
            for g in range(8):
                dve.wait_ge(s_pq, g + 1)
                nc.vector.tensor_scalar(qt[:, 4 * g:4 * g + 4, :], pq[:, g % 2, :].rearrange("p (k i) -> p k i", k=4),
                                        bq[:, :], w2[:, :], ALU.add, ALU.mult).then_inc(s_qt, 1)
                if g == 0:
                    nc.vector.tensor_copy(vt1[:, :], ft[:, 0, 0:P]).then_inc(s_vt0, 1)
                    nc.vector.tensor_copy(vt2[:, :], ft[:, 0, P:2 * P]).then_inc(s_vt0, 1)
                    dve.wait_ge(s_vt0, 2)
            nc.vector.memset(qt[:, NK, :], 0.0).then_inc(s_init, 1)
            nc.vector.memset(tab[:, :, :], 0.0).then_inc(s_init, 1)
            dve.wait_ge(s_ident, 2)
            dve.wait_ge(s_const, 2)
            nc.vector.tensor_scalar(b0_row[:, :], zero_row[:, :], b0[:, :], None, ALU.add).then_inc(s_init, 1)
            dve.wait_ge(s_init, 5)
            for b in range(B):
                q = slice(L * b, L * b + L)
                for g in range(2):
                    nc.vector.tensor_copy(tab[q, 1 + g, L * g:L * g + L], ident[q, q]).then_inc(s_init, 1)
            dve.wait_ge(s_init, 13)
            dve.wait_ge(s_mask, 3)

            def coefficients(c, r):
                k = r % 2
                if r >= 1:
                    dve.wait_ge(s_coef, L * c + r)
                for g in (1, 2):
                    ins = nc.vector.scalar_tensor_tensor(junk[:, g, :], ex[:, k, :], rz[:, k:k + 1],
                                                         tab[:, g, r:r + ROW], ALU.mult, ALU.mult,
                                                         accum_out=tab[:, g, r + WIN:r + WIN + 1])
                ins.then_inc(s_coef, 1)

            with dve.Fori(0, NC) as c:
                dve.wait_ge(s_scores, c + 1)
                nc.vector.tensor_scalar(tab[:, 0, 0:WIN], p_s[:, 0:WIN], b0[:, :], None, ALU.add).then_inc(s_table, 1)
                nc.vector.tensor_copy(tab[:, 0, WIN:], b0_row[:, :]).then_inc(s_table, 1)
                for r in range(L):
                    k = r % 2
                    n = L * c + r
                    if r == 0:
                        dve.wait_ge(s_table, 2 * (c + 1))
                    else:
                        dve.wait_ge(s_new, n)
                    dve.sem_inc(s_pace, 1)
                    nc.vector.stream_shuffle(row[:, k, :], tab[:, 0, r:r + ROW], [r] * L).then_inc(s_row, 1)
                    dve.wait_ge(s_row, n + 1)
                    nc.vector.reduce_max(nmax[:, k:k + 1], row[:, k, :], AX.X, negate=True).then_inc(s_max, 1)
                    if r >= 1:
                        coefficients(c, r - 1)
                    else:
                        dve.wait_ge(s_bdc, c + 1)
                        nc.vector.memset(tab[:, 1:3, WIN:], 0.0).then_inc(s_clear, 1)
                        dve.wait_ge(s_clear, c + 1)
                    if r == 1:
                        dve.wait_ge(s_pv, c + 1)
                        dve.wait_ge(s_vall, c + 1)
                        nc.vector.tensor_copy(vr[:, :], p_v[:, 0:D]).then_inc(s_vr, 1)
                    if r == 4:
                        dve.wait_ge(s_pt, c + 1)
                        dve.wait_ge(s_vt2, c + 1)
                        nc.vector.tensor_copy(vt1[:, :], p_t[:, 0:P]).then_inc(s_vt1, 1)
                    if r == 8:
                        dve.wait_ge(s_g, c + 1)
                        nc.vector.tensor_tensor(
                            bdg[:, :, :].rearrange("p g (b i) -> p g b i", b=B),
                            p_g[:, 0:2 * P].rearrange("p (g b i) -> p g b i", g=2, b=B),
                            mask[:, :, :].unsqueeze(1).broadcast_to((P, 2, B, L)), ALU.mult).then_inc(s_bdg, 1)
                    dve.wait_ge(s_exp, n + 1)
                    nc.vector.reciprocal(rz[:, k:k + 1], z[:, k:k + 1]).then_inc(s_rz, 1)
                    dve.wait_ge(s_rz, n + 1)
                    nc.vector.scalar_tensor_tensor(junk[:, 0, :], ex[:, k, :], rz[:, k:k + 1], tab[:, 0, r:r + ROW],
                                                   ALU.mult, ALU.mult,
                                                   accum_out=tab[:, 0, r + WIN:r + WIN + 1]).then_inc(s_new, 1)
                coefficients(c, L - 1)
            dve.wait_ge(s_pv, NC + 1)
            nc.vector.tensor_copy(v_all[:, NC + 2, :], p_v[:, 0:D]).then_inc(s_vr, 1)

        @block.tensor
        def _(pe):
            pe.wait_ge(s_w, 64)
            pe.wait_ge(s_ident, 2)
            for g in range(8):
                pe.wait_ge(s_f, 4 * g + 4)
                if g >= 2:
                    pe.wait_ge(s_ftc, g - 1)
                for k in range(4):
                    ins = nc.tensor.transpose(pf[:, g % 2, P * k:P * k + P], f[:, 4 * g + k, :], ident[:, :])
                ins.then_inc(s_ft, 1)
                pe.wait_ge(s_ftc, g + 1)
                if g >= 2:
                    pe.wait_ge(s_qt, g - 1)
                nc.tensor.matmul(pq[:, g % 2, :], wq[:, :], ft[:, g % 2, :], start=True, stop=True).then_inc(s_pq, 1)
            pe.wait_ge(s_qn, 1)
            pe.wait_ge(s_vt0, 2)
            for b in range(B):
                q = slice(L * b, L * b + L)
                for g, vt in enumerate((vt1, vt2)):
                    ins = nc.tensor.matmul(p_s[q, L * g:L * g + L], qn[:, q], vt[:, q], start=True, stop=True)
            ins.then_inc(s_scores, 1)
            pe.wait_ge(s_init, 13)
            with pe.Fori(0, NC) as c:
                pe.wait_ge(s_bdc, c + 1)
                pe.wait_ge(s_vall, c + 1)
                for g in range(2):
                    ins = nc.tensor.matmul(p_v[:, 0:D], bdc[:, g, :], v_all[:, c + g, :], start=g == 0, stop=g == 1)
                ins.then_inc(s_pv, 1)
                pe.wait_ge(s_vr, c + 1)
                nc.tensor.transpose(p_t[:, 0:P], vr[:, :], ident[:, :]).then_inc(s_pt, 1)
                pe.wait_ge(s_vt1, c + 1)
                pe.wait_ge(s_qn, c + 2)
                for g, vt in enumerate((vt2, vt1)):
                    ins = nc.tensor.matmul(p_g[:, P * g:P * g + P], vt[:, :], qn[:, :], start=True, stop=True)
                ins.then_inc(s_g, 1)
                pe.wait_ge(s_table, 2 * (c + 1))
                for b in range(B):
                    q = slice(L * b, L * b + L)
                    nc.tensor.matmul(p_s[q, 0:L], qn[:, q], vt1[:, q], start=True, stop=True)
                pe.wait_ge(s_bdg, c + 1)
                pe.wait_ge(s_coef, L * (c + 1))
                for g in range(2):
                    ins = nc.tensor.matmul(p_s[:, L:WIN], bdg[:, g, :], tab[:, 1 + g, WIN:], start=g == 0, stop=g == 1)
                ins.then_inc(s_scores, 1)
            pe.wait_ge(s_bdc, NC + 1)
            pe.wait_ge(s_vall, NC + 1)
            for g in range(2):
                ins = nc.tensor.matmul(p_v[:, 0:D], bdc[:, g, :], v_all[:, NC + g, :], start=g == 0, stop=g == 1)
            ins.then_inc(s_pv, 1)




def middle(nc, io, xt, x1_dram, h_dram):
    ctx = ExitStack()
    with ctx:
        def sb(name, shape, dt=F32):
            return ctx.enter_context(nc.sbuf_tensor(name, shape, dt))

        def sem(name):
            return ctx.enter_context(nc.semaphore(name))

        x, f, eps = xt["x"], xt["f"], xt["eps"]
        y = xt["v_all"][:, 1:, :]
        g_row, b_row = sb("g_row", [P, D]), sb("b_row", [P, D])
        stats, mv = sb("stats2", [P, NK, 6]), sb("mv2", [P, NK, 2])
        std, rstd = sb("std2", [P, NK]), sb("rstd2", [P, NK])
        G, GK = 4, NK // 4
        m_w, m_tanh, m_y, m_stats, m_var, m_std, m_rstd, m_norm, m_scaled, m_affine, m_res, m_out = (
            sem(n) for n in ("m_w", "m_tanh", "m_y", "m_stats", "m_var", "m_std", "m_rstd", "m_norm", "m_scaled",
                             "m_affine", "m_res", "m_out"))
        block = ctx.enter_context(nc.Block())

        def ks(g):
            return slice(GK * g, GK * g + GK)

        def wide(t):
            return t[:, :].unsqueeze(1).broadcast_to((P, GK, D))

        @block.sync
        def _(sp):
            sp.dma_start(g_row[:, :], io["ln_g"].rearrange("(a d) -> a d", a=1).broadcast_to((P, D))).then_inc(m_w, 16)
            sp.dma_start(b_row[:, :], io["ln_b"].rearrange("(a d) -> a d", a=1).broadcast_to((P, D))).then_inc(m_w, 16)
            for b in range(B):
                q = slice(L * b, L * b + L)
                if b == 0:
                    sp.wait_ge(m_res, G)
                sp.dma_start(x1_dram[b].rearrange("(k j) d -> j k d", j=L), x[q, :, :]).then_inc(m_out, 16)
            for b in range(B + 1):
                q = slice(L * (b % B), L * (b % B) + L)
                if b == 0:
                    sp.wait_ge(m_norm, 3 * NK)
                sp.dma_start(h_dram[b].rearrange("(k j) d -> j k d", j=L), f[q, :, :]).then_inc(m_out, 16)
            sp.wait_ge(m_out, 16 * (2 * B + 1))

        @block.scalar
        def _(act):
            for g in range(G):
                nc.scalar.activation(y[:, ks(g), :], y[:, ks(g), :], ACT.Tanh).then_inc(m_tanh, 1)
            for n in range(3):
                for g in range(G):
                    act.wait_ge(m_var, NK * n + GK * (g + 1))
                    if n:
                        act.wait_ge(m_rstd, G * (n - 1) + g + 1)
                    nc.scalar.activation(std[:, ks(g)], mv[:, ks(g), 1], ACT.Sqrt, bias=eps[:, :]).then_inc(m_std, 1)

        @block.gpsimd
        def _(pool):
            pool.wait_ge(m_w, 32)
            for g in range(G):
                pool.wait_ge(m_norm, GK * (g + 1))
                nc.gpsimd.tensor_tensor(y[:, ks(g), :], y[:, ks(g), :], wide(g_row), ALU.mult).then_inc(m_scaled, 1)
                pool.wait_ge(m_scaled, g + 1)
                nc.gpsimd.tensor_tensor(y[:, ks(g), :], y[:, ks(g), :], wide(b_row), ALU.add).then_inc(m_affine, 1)

        @block.vector
        def _(dve):
            for g in range(G):
                dve.wait_ge(m_tanh, g + 1)
                nc.vector.scalar_tensor_tensor(y[:, ks(g), :], y[:, ks(g), :], 1.0, f[:, ks(g), :], ALU.add,
                                               ALU.mult).then_inc(m_y, 1)

            def statistics(n, g, src, ready, at):
                dve.wait_ge(ready, at)
                for k in range(GK * g, GK * g + GK):
                    nc.vector.bn_stats(stats[:, k, :], src[:, k, :]).then_inc(m_stats, 1)
                for k in range(GK * g, GK * g + GK):
                    dve.wait_ge(m_stats, NK * n + k + 1)
                    if n and k == GK * g:
                        dve.wait_ge(m_norm, NK * (n - 1) + GK * (g + 1))
                    nc.vector.bn_aggr(mv[:, k, :], stats[:, k, :]).then_inc(m_var, 1)

            def normed(n, g, out, src):
                dve.wait_ge(m_std, G * n + g + 1)
                nc.vector.reciprocal(rstd[:, ks(g)], std[:, ks(g)]).then_inc(m_rstd, 1)
                dve.wait_ge(m_rstd, G * n + g + 1)
                for k in range(GK * g, GK * g + GK):
                    nc.vector.tensor_scalar(out[:, k, :], src[:, k, :], mv[:, k, 0:1], rstd[:, k:k + 1], ALU.subtract,
                                            ALU.mult).then_inc(m_norm, 1)

            for g in range(G):
                statistics(0, g, y, m_y, g + 1)
            for g in range(G):
                normed(0, g, y, y)
            for g in range(G):
                statistics(1, g, y, m_affine, g + 1)
            for g in range(G):
                normed(1, g, y, y)
            for g in range(G):
                dve.wait_ge(m_norm, NK + GK * (g + 1))
                nc.vector.tensor_tensor(x[:, ks(g), :], x[:, ks(g), :], y[:, ks(g), :], ALU.add).then_inc(m_res, 1)
            for g in range(G):
                statistics(2, g, x, m_res, g + 1)
            for g in range(G):
                normed(2, g, f, x)


def constants(ctx, nc):
    def sb(name, shape, dt=F32):
        return ctx.enter_context(nc.sbuf_tensor(name, shape, dt))

    w = {n: sb(f"w_{n}", [P, D]) for n in ("Wq", "Wk", "Wv", "Wo")}
    w["Wg"] = sb("w_Wg", [P, E])
    w["W1"] = sb("w_W1", [P, E, FF])
    w["W2"] = sb("w_W2", [P, E, FC, D])
    w["b2"] = sb("w_b2", [E, D])
    w["b1"] = sb("w_b1", [E * FC, P])
    w["bqk"] = sb("w_bqk", [1, 4, D])
    for n in ("bv", "bo", "g1", "be1", "g2", "be2"):
        w[n] = sb(f"w_{n}", [P, D])
    w["bg"] = sb("w_bg", [P, E])
    w["cos"], w["sin"] = sb("w_cos", [P, T]), sb("w_sin", [P, T])
    return w


def load_constants(sp, w, io, arrived):
    def row(n):
        return io[n].rearrange("(a d) -> a d", a=1)

    def halves(n):
        return row(n).rearrange("a (h t e) -> a h t e", h=H, t=2)

    to, of = w["bqk"], w["bqk"][:, :, :].rearrange("a k (h t e) -> a k h t e", h=H, t=2)
    pairs = [(w[n][:, :], io[n]) for n in ("Wq", "Wk", "Wv", "Wo", "Wg")]
    pairs += [(w["W1"][:, :, :], io["W1"].rearrange("e d f -> d e f"))]
    pairs += [(w["W2"][:, e, :, :], io["W2"][e].rearrange("(c p) d -> p c d", p=P)) for e in range(E)]
    pairs += [(w["b2"][:, :], io["b2"]), (w["b1"][:, :], io["b1"].rearrange("e (c p) -> (e c) p", p=P))]
    for k, n in enumerate(("bq", "bk")):
        pairs += [(to[:, 2 * k, :], row(n))]
        pairs += [(of[:, 2 * k + 1, :, t, :], halves(n)[:, :, 1 - t, :]) for t in range(2)]
    pairs += [(w[n][:, :], row(n).broadcast_to((P, D))) for n in ("bv", "bo", "g1", "be1", "g2", "be2")]
    pairs += [(w["bg"][:, :], row("bg").broadcast_to((P, E))), (w["cos"][:, :], io["cos"]), (w["sin"][:, :], io["sin"])]
    for out, in_ in pairs:
        sp.dma_start(out, in_).then_inc(arrived, 16)
    return 16 * len(pairs)


BANK_USES = {"AT": 1, "WO": 1, "XT": 1, "GT": 1, "CT": 1, "B2": 1, "V": 1, "HID": 1, "Y": 1, "MT": 1, "OT": 1,
             "HT": 1, "QK": 2, "PRE": 1}


AHEAD = {(0, 4): [("HQ",)], (1, 4): [("HT", 0)], (1, 6): [("HT", 1)], (2, 4): [("QK", 0, 0)], (2, 12): [("QK", 0, 1)],
         (3, 4): [("QK", 1, 0)], (3, 12): [("QK", 1, 1)], (4, 2): [("PO", 0), ("PO", 1)], (4, 8): [("ST", 0, 1)],
         (5, 4): [("ST", 1, 1)], (5, 8): [("HR",)], (7, 2): [("ST", 2, 1)]}


def order(attn, moe):
    if moe:
        yield "XR",
        for name in ("AT", "WO"):
            for t in range(2):
                yield name, t
        yield "LN1",
        for t in range(2):
            yield "XT", t
        yield "GT",
        for name in ("CT", "B2"):
            for t in range(2):
                yield name, t
    if attn:
        yield "V", 0
        yield "V", 1
        if moe:
            yield "ST", 3, 0
    for hp in range(HP):
        for j in range(8):
            if moe:
                yield "HID", hp, j
            if attn:
                yield "A", 2 * hp + 2, j
        for i in range(2 * QT):
            if attn:
                yield "B", hp, i
                if i < QT:
                    yield "A", 2 * hp + 3, i
            if moe and i >= QT:
                yield "Y", hp, i - QT
            if attn:
                if i == 0 and hp:
                    yield "OC", hp - 1
                if i == 2 and hp:
                    yield "OT", hp - 1
                if i == QT + 1:
                    yield "MT", hp + 1
                yield from AHEAD.get((hp, i), ())
    if attn:
        yield "BF",
        yield "OC", HP - 1
        yield "OT", HP - 1
    if moe:
        yield "FIN",


PROLOGUE = ([("PRE",), ("HQ",), ("HT", 0), ("HT", 1), ("QK", 0, 0), ("QK", 0, 1), ("QK", 1, 0), ("QK", 1, 1),
             ("PO", 0), ("PO", 1)] + [("ST", g, 1) for g in range(4)]
            + [("A", h, j) for h in range(2) for j in range(QT)] + [("MT", 0)])
ST_DMAS = 2 * (len(Q_PARTS) + len(K_PARTS)) + 2


def uses(steps):
    return sum(BANK_USES.get(x[0], 0) for x in steps)


def passes(engine, steps_of):
    def one(steps, s, bank):
        for x in steps:
            steps_of(x, s, bank)
            bank = bank + BANK_USES.get(x[0], 0)

    first, both = uses(PROLOGUE), uses(order(True, True))
    one(PROLOGUE, -1, 0)
    one(order(True, False), 0, first)
    first += uses(order(True, False))
    with engine.Fori(1, B) as s:
        one(order(True, True), s, (s - 1) * both + first)
    one(order(False, True), B, first + (B - 1) * both)


def second_layer(nc, io, w, ident, eps, x1_dram, h_dram, parts_dram):
    ctx = ExitStack()
    with ctx:
        def sb(name, shape, dt=F32):
            return ctx.enter_context(nc.sbuf_tensor(name, shape, dt))

        def ps(name, shape, dt=F32):
            return ctx.enter_context(nc.psum_tensor(name, shape, dt))

        def sem(name):
            return ctx.enter_context(nc.semaphore(name))

        ks = sb("ks", [P, H, T], BF16)
        qs = sb("qs", [P, HP, T], BF16)
        zeros = sb("zeros", [2, 2, T], BF16)
        ones = sb("ones", [2, T], BF16)
        wp = sb("wp", [P, 2, D])
        cols = sb("cols", [P, 4 + E * FC])
        hq = sb("hq", [P, QT, D])
        ht = sb("ht", [P, T])
        rot = sb("rot", [P, 2, HALF])
        full = sb("full", [P, HALF])
        rest = sb("rest", [P, HALF])
        parts = sb("parts", [P, 2, 3, T], BF16)
        va = sb("va", [P, QT, H, VH])
        nm = sb("nm", [P, 2, 2, QT])
        m_hi, m_lo = sb("m_hi", [2 * QT, 2, P], BF16), sb("m_lo", [2 * QT, 2, P], BF16)
        pt = sb("pt", [P, 4, T])
        o_sb = sb("o_sb", [P, 512])
        rcp = sb("rcp", [P, 4, 4])
        ao = sb("ao", [P, QT, D])
        aot = sb("aot", [P, T])
        hr, xr, xa, acc = sb("hr", [P, QT, D]), sb("xr", [P, QT, D]), sb("xa", [P, QT, D]), sb("acc", [P, QT, D])
        xt = aot
        hid = sb("hid", [P, FC, T])
        stats, mv = sb("stats3", [P, QT, 6]), sb("mv3", [P, QT, 2])
        std, rstd = sb("std3", [P, QT]), sb("rstd3", [P, QT])
        logit, prob, top = sb("logit", [P, QT, E]), sb("prob", [P, QT, E]), sb("top", [P, QT, 8])
        mx, zs, idx, idx_f = sb("mx", [P, QT]), sb("zs", [P, QT]), sb("idx", [P, QT, 8], U32), sb("idx_f", [P, QT, 8])
        pick = sb("pick", [P, 2, QT, E])
        comb, ct = sb("comb", [P, QT, E]), sb("ct", [E, T])
        expert = sb("expert", [P, E])

        s1 = ps("s1", [P, T])
        s2 = [ps(f"s2{i}", [P, T]) for i in range(2)]
        p_o = ps("p_o", [P, 512])
        bank = ps("bank", [P, 512])

        s_pace = sem("s_pace2")
        s_zero, s_ones, s_setup, s_iota = sem("s_zero"), sem("s_ones"), sem("s_setup"), sem("s_iota")
        s_bank, s_free = sem("s_bank"), sem("s_free")
        s_hq, s_r, s_sp, s_split = sem("s_hq"), sem("s_r"), sem("s_sp"), sem("s_split")
        s_po = [sem(f"s_po{x}") for x in range(2)]
        s_st = [sem(f"s_st{g}") for g in range(4)]
        s_s1, s_max = sem("s_s1"), sem("s_max")
        s_mr = [sem(f"s_mr{g}") for g in range(2)]
        s_s2, s_exp, s_pv, s_oc, s_rc = sem("s_s2"), sem("s_exp"), sem("s_pv"), sem("s_oc"), sem("s_rc")
        s_mh = sem("s_mh")
        s_hr, s_hrb, s_xr = sem("s_hr"), sem("s_hrb"), sem("s_xr")
        l_stats, l_var, l_std, l_rstd, l_norm, l_scale, l_affine = (
            sem(n) for n in ("l_stats", "l_var", "l_std", "l_rstd", "l_norm", "l_scale", "l_affine"))
        s_gate, s_gexp, s_comb, s_sum, s_added, s_fin, s_out = (
            sem(n) for n in ("s_gate", "s_gexp", "s_comb", "s_sum", "s_added", "s_fin", "s_out"))
        block = ctx.enter_context(nc.Block())

        def tokens(t):
            return slice(HALF * t, HALF * t + HALF)

        def tile(q):
            return slice(P * q, P * q + P)

        def wide(t, n=QT):
            return t[:, :].unsqueeze(1).broadcast_to((P, n, t.shape[1]))

        def which(s):
            known = isinstance(s, int)
            return (0 if known and s < 0 else s), known and s < 0, known and s == 0

        def norm_index(step, s, k=0):
            return 3 * (s - 1) + (0 if step == "LN1" else 1 + k)

        @block.sync
        def _(sp):
            sp.wait_ge(s_zero, 2)
            sp.wait_ge(s_setup, 1)
            for par in range(2):
                r = 64 * par + M_ROW
                sp.dma_start(ks[r:r + 2, par::2, :],
                             ones[:, :].unsqueeze(1).broadcast_to((2, HP, T))).then_inc(s_ones, 16)

            def wait(semaphore, n):
                sp.wait_ge(semaphore, n)
                sp.sem_inc(s_pace, 1)

            def step(x, s, bank_n):
                name, b, starts, zeroth = x[0], *which(s)
                if name == "HQ":
                    sp.dma_start(hq[:, :, :], h_dram[s + 1].rearrange("(q p) d -> p q d", p=P)).then_inc(s_hq, 16)
                elif name == "HR":
                    sp.dma_start(hr[:, :, :], h_dram[s].rearrange("(q p) d -> p q d", p=P)).then_inc(s_hr, 16)
                elif name == "XR":
                    sp.dma_start(xr[:, :, :], x1_dram[s - 1].rearrange("(q p) d -> p q d", p=P)).then_inc(s_xr, 16)
                elif name == "PO":
                    wait(s_sp, 4 * (s + 1) + 2 * x[1] + 2)
                    if not starts:
                        for g in range(4):
                            wait(s_st[g], 16 * ST_DMAS * (s + 1))
                    sp.dma_start(parts_dram[x[1]].rearrange("n p t -> p n t"), parts[:, x[1], :, :])\
                        .then_inc(s_po[x[1]], 16)
                elif name == "ST":
                    g, ahead = x[1], x[2]
                    nb = s + ahead
                    for k in range(2):
                        wait(s_po[k], 16 * (nb + 1))
                    if not starts:
                        wait(s_pv, 128 * (nb - 1) + 32 * (g + 1))
                    else:
                        wait(s_ones, 32)
                    for par in range(2):
                        for k, (stack, chosen) in enumerate(((qs, Q_PARTS), (ks, K_PARTS))):
                            for n, part in enumerate(chosen):
                                rows = slice(64 * par + HD * n, 64 * par + HD * n + HD)
                                src = parts_dram[k, part].rearrange("(c r e) t -> r e c t", r=2, e=HD)
                                dst = (stack[rows, 2 * g:2 * g + 2, :] if k == 0
                                       else stack[rows, 4 * g + par:4 * g + 4:2, :])
                                sp.dma_start(dst, src[par, :, 2 * g:2 * g + 2, :]).then_inc(s_st[g], 16)
                        r = 64 * par + M_ROW
                        sp.dma_start(qs[r:r + 2, 2 * g:2 * g + 2, :], zeros[:, :, :]).then_inc(s_st[g], 16)
                elif name == "MT":
                    hp = x[1]
                    wait(s_free, bank_n + 1)
                    for k, rows in enumerate((m_hi, m_lo)):
                        for par in range(2):
                            r = 64 * par + M_ROW + k
                            sp.dma_start(qs[r:r + 1, hp % HP, :].rearrange("a (q p) -> a q p", p=P),
                                         rows[QT * par:QT * par + QT, hp % 2, :]).then_inc(s_mr[hp % 2], 16)
                elif name == "FIN":
                    wait(s_fin, s)
                    sp.dma_start(io["out"][s - 1].rearrange("(q p) d -> p q d", p=P), xa[:, :, :]).then_inc(s_out, 16)
                    wait(s_out, 16 * s)

            passes(sp, step)
            for g in range(3):
                sp.wait_ge(s_st[g], 16 * ST_DMAS * (B + 1))
            sp.wait_ge(s_mr[0], 64 * (4 * B + 1))

        @block.gpsimd
        def _(pool):
            nc.gpsimd.memset(ks[:, :, :], 0.0).then_inc(s_zero, 1)
            nc.gpsimd.memset(qs[:, :, :], 0.0).then_inc(s_zero, 1)
            nc.gpsimd.iota(expert[:, :], [[1, E]], base=0, channel_multiplier=0,
                           allow_small_or_imprecise_dtypes=True).then_inc(s_iota, 1)

            def step(x, s, bank_n):
                name, b, starts, zeroth = x[0], *which(s)
                if name == "QK":
                    k, t = x[1], x[2]
                    n = 4 * (s + 1) + 2 * k + t
                    out = [parts[:, k, i, tokens(t)] for i in range(3)]
                    if not starts:
                        pool.wait_ge(s_po[k], 16 * (s + 1))
                    pool.wait_ge(s_free, bank_n + 2)
                    pool.sem_inc(s_pace, 1)
                    nc.gpsimd.tensor_tensor(full[:, :], rot[:, 0, :], rot[:, 1, :], ALU.add).then_inc(s_r, 1)
                    pool.wait_ge(s_r, n + 1)
                    pool.sem_inc(s_pace, 1)
                    nc.gpsimd.tensor_copy(out[0], full[:, :]).then_inc(s_split, 1)
                    pool.wait_ge(s_split, 3 * n + 1)
                    nc.gpsimd.tensor_tensor(rest[:, :], full[:, :], out[0], ALU.subtract).then_inc(s_split, 1)
                    pool.wait_ge(s_split, 3 * n + 2)
                    pool.sem_inc(s_pace, 1)
                    nc.gpsimd.tensor_copy(out[1], rest[:, :]).then_inc(s_split, 1)
                    pool.wait_ge(s_split, 3 * n + 3)
                    nc.gpsimd.tensor_tensor(out[2], rest[:, :], out[1], ALU.subtract).then_inc(s_sp, 1)
                elif name == "HR":
                    pool.wait_ge(s_hr, 16 * (s + 1))
                    nc.gpsimd.tensor_tensor(hr[:, :, :], hr[:, :, :], wide(w["bo"]), ALU.add).then_inc(s_hrb, 1)
                elif name in ("LN1", "FIN"):
                    n = norm_index(name, s)
                    gain, bias = (w["g1"], w["be1"]) if name == "LN1" else (w["g2"], w["be2"])
                    a = 2 * (s - 1) + (0 if name == "LN1" else 1)
                    pool.wait_ge(l_norm, QT * (n + 1))
                    nc.gpsimd.tensor_tensor(xa[:, :, :], xa[:, :, :], wide(gain), ALU.mult).then_inc(l_scale, 1)
                    pool.wait_ge(l_scale, a + 1)
                    nc.gpsimd.tensor_tensor(xa[:, :, :], xa[:, :, :], wide(bias), ALU.add).then_inc(l_affine, 1)
                    if name == "FIN":
                        pool.wait_ge(s_xr, 16 * s)
                        pool.wait_ge(l_norm, QT * (n + 2))
                        nc.gpsimd.tensor_tensor(xa[:, :, :], xa[:, :, :], xr[:, :, :], ALU.add).then_inc(s_fin, 1)

            passes(pool, step)

        @block.scalar
        def _(act):
            def step(x, s, bank_n):
                name, b, starts, zeroth = x[0], *which(s)
                if name == "PRE":
                    act.wait_ge(s_bank, bank_n + 1)
                    nc.scalar.copy(cols[:, :], bank[:, 0:4 + E * FC]).then_inc(s_free, 1)
                elif name == "B":
                    hp, i = x[1], x[2]
                    n = 128 * s + 16 * hp + i
                    act.wait_ge(s_s2, n + 1)
                    if not (zeroth and n < 4):
                        act.wait_ge(s_pv, n - 3)
                    nc.scalar.activation(pt[:, i % 4, :], s2[i % 2][:, :], ACT.Exp, scale=SCALE).then_inc(s_exp, 1)
                elif name == "HID":
                    e, f, t = x[1], x[2] // 2, x[2] % 2
                    act.wait_ge(s_bank, bank_n + 1)
                    nc.scalar.activation(hid[:, f, tokens(t)], bank[:, :], ACT.Gelu,
                                         bias=cols[:, 4 + FC * e + f:5 + FC * e + f]).then_inc(s_free, 1)
                elif name in ("HT", "AT", "XT"):
                    act.wait_ge(s_bank, bank_n + 1)
                    to = {"HT": ht, "AT": aot, "XT": xt}[name]
                    nc.scalar.copy(to[:, tokens(x[1])], bank[:, :]).then_inc(s_free, 1)
                elif name == "CT":
                    act.wait_ge(s_bank, bank_n + 1)
                    nc.scalar.copy(ct[:, tokens(x[1])], bank[0:E, :]).then_inc(s_free, 1)
                elif name == "B2":
                    act.wait_ge(s_bank, bank_n + 1)
                    nc.scalar.copy(acc[:, 4 * x[1]:4 * x[1] + 4, :],
                                   bank[:, :].rearrange("p (q d) -> p q d", q=4)).then_inc(s_free, 1)
                elif name in ("LN1", "FIN"):
                    for k in range(1 if name == "LN1" else 2):
                        act.wait_ge(l_var, QT * (norm_index(name, s, k) + 1))
                        nc.scalar.activation(std[:, :], mv[:, :, 1], ACT.Sqrt, bias=eps[:, :]).then_inc(l_std, 1)
                elif name == "GT":
                    act.wait_ge(s_gate, 8 * (s - 1) + 2)
                    nc.scalar.activation(prob[:, :, :], logit[:, :, :], ACT.Exp).then_inc(s_gexp, 1)

            passes(act, step)

        @block.vector
        def _(dve):
            nc.vector.memset(ones[:, :], 1.0).then_inc(s_mh, 1)
            nc.vector.memset(zeros[:, :, :], 0.0).then_inc(s_mh, 1)
            dve.wait_ge(s_mh, 2)
            nc.vector.memset(va[:, :, :, HD:], 1.0).then_inc(s_setup, 1)
            nc.vector.memset(p_o[:, :], 0.0).then_inc(s_setup, 1)
            for k, n in enumerate(("Wq", "Wk")):
                a = w[n][:, :].rearrange("p (h t e) -> p h t e", h=H, t=2)
                b = wp[:, k, :].rearrange("p (h t e) -> p h t e", h=H, t=2)
                for t in range(2):
                    nc.vector.tensor_copy(b[:, :, t, :], a[:, :, 1 - t, :]).then_inc(s_setup, 1)

            def layer_norm(n):
                for q in range(QT):
                    nc.vector.bn_stats(stats[:, q, :], xa[:, q, :]).then_inc(l_stats, 1)
                for q in range(QT):
                    dve.wait_ge(l_stats, QT * n + q + 1)
                    dve.sem_inc(s_pace, 1)
                    nc.vector.bn_aggr(mv[:, q, :], stats[:, q, :]).then_inc(l_var, 1)
                dve.wait_ge(l_std, n + 1)
                nc.vector.reciprocal(rstd[:, :], std[:, :]).then_inc(l_rstd, 1)
                dve.wait_ge(l_rstd, n + 1)
                for q in range(QT):
                    nc.vector.tensor_scalar(xa[:, q, :], xa[:, q, :], mv[:, q, 0:1], rstd[:, q:q + 1], ALU.subtract,
                                            ALU.mult).then_inc(l_norm, 1)

            def step(x, s, bank_n):
                name, b, starts, zeroth = x[0], *which(s)
                if name == "A":
                    head, q = x[1], x[2]
                    n = 8 * (16 * b + head) + q
                    dve.wait_ge(s_s1, n + 1)
                    nc.vector.reduce_max(nm[:, head // 2 % 2, head % 2, q:q + 1], s1[:, :], AX.X, negate=True).then_inc(s_max, 1)
                elif name == "MT":
                    hp = x[1]
                    dve.wait_ge(s_bank, bank_n + 1)
                    if not (starts or (zeroth and hp < 2)):
                        dve.wait_ge(s_mr[hp % 2], 64 * (4 * s + hp // 2))
                    nc.vector.tensor_copy(m_hi[:, hp % 2, :], bank[0:2 * QT, 0:P]).then_inc(s_mh, 1)
                    dve.wait_ge(s_mh, 8 * b + hp + 3)
                    nc.vector.tensor_tensor(m_lo[:, hp % 2, :], bank[0:2 * QT, 0:P], m_hi[:, hp % 2, :],
                                            ALU.subtract).then_inc(s_free, 1)
                elif name == "Y":
                    e, q = x[1], x[2]
                    dve.wait_ge(s_bank, bank_n + 1)
                    nc.vector.scalar_tensor_tensor(acc[:, q, :], bank[:, 0:D], comb[:, q, e:e + 1], acc[:, q, :],
                                                   ALU.mult, ALU.add).then_inc(s_free, 1)
                elif name == "OC":
                    u = 8 * s + x[1]
                    dve.wait_ge(s_pv, 16 * (u + 1))
                    nc.vector.tensor_copy(o_sb[:, :], p_o[:, :]).then_inc(s_oc, 1)
                elif name == "OT":
                    hp = x[1]
                    u = 8 * s + hp
                    dve.wait_ge(s_bank, bank_n + 1)
                    o = bank[:, :].rearrange("p (t j c) -> p t j c", t=4, j=4)
                    nc.vector.reciprocal(rcp[:, :, :], o[:, :, :, HD]).then_inc(s_rc, 1)
                    dve.wait_ge(s_rc, 2 * u + 1)
                    for half in range(2):
                        ins = nc.vector.tensor_tensor(
                            ao[:, 4 * half:4 * half + 4, 2 * HD * hp:2 * HD * hp + 2 * HD]
                            .rearrange("p t (r e) -> p t r e", r=2),
                            o[:, :, half::2, 0:HD],
                            rcp[:, :, half::2].unsqueeze(3).broadcast_to((P, 4, 2, HD)), ALU.mult)
                        ins.then_inc(s_free if half else s_rc, 1)
                elif name == "V":
                    t = x[1]
                    dve.wait_ge(s_bank, bank_n + 1)
                    nc.vector.tensor_tensor(
                        va[:, 4 * t:4 * t + 4, :, 0:HD], bank[:, :].rearrange("p (q h e) -> p q h e", q=4, h=H),
                        w["bv"][:, :].rearrange("p (h e) -> p h e", h=H).unsqueeze(1).broadcast_to((P, 4, H, HD)),
                        ALU.add).then_inc(s_free, 1)
                elif name == "QK":
                    k, t = x[1], x[2]
                    if not (starts and k == 0 and t == 0):
                        dve.wait_ge(s_sp, 4 * (s + 1) + 2 * k + t)
                    for i, table in enumerate((w["cos"], w["sin"])):
                        dve.wait_ge(s_bank, bank_n + 1 + i)
                        nc.vector.scalar_tensor_tensor(rot[:, i, :], bank[:, :], cols[:, 2 * k + i:2 * k + i + 1],
                                                       table[:, tokens(t)], ALU.add, ALU.mult).then_inc(s_free, 1)
                elif name == "WO":
                    t = x[1]
                    dve.wait_ge(s_bank, bank_n + 1)
                    dve.wait_ge(s_hrb, s)
                    dve.wait_ge(s_xr, 16 * s)
                    nc.vector.tensor_tensor(xa[:, 4 * t:4 * t + 4, :], bank[:, :].rearrange("p (q d) -> p q d", q=4),
                                            hr[:, 4 * t:4 * t + 4, :], ALU.add).then_inc(s_free, 1)
                elif name == "LN1":
                    dve.wait_ge(s_free, bank_n)
                    layer_norm(norm_index(name, s))
                elif name == "GT":
                    c = 8 * (s - 1)
                    link = [0]

                    def chain(ins):
                        link[0] += 1
                        ins.then_inc(s_gate, 1)
                        dve.wait_ge(s_gate, c + link[0])

                    def per_tile(t):
                        return t.unsqueeze(2).broadcast_to((P, QT, E))

                    dve.wait_ge(s_bank, bank_n + 1)
                    nc.vector.tensor_tensor(logit[:, :, :], bank[:, 0:QT * E].rearrange("p (q e) -> p q e", q=QT),
                                            wide(w["bg"]), ALU.add).then_inc(s_free, 1)
                    dve.wait_ge(s_free, bank_n + 1)
                    chain(nc.vector.reduce_max(mx[:, :], logit[:, :, :], AX.X))
                    chain(nc.vector.tensor_tensor(logit[:, :, :], logit[:, :, :], per_tile(mx[:, :]), ALU.subtract))
                    dve.wait_ge(s_gexp, s)
                    chain(nc.vector.reduce_sum(zs[:, :], prob[:, :, :], AX.X))
                    chain(nc.vector.reciprocal(mx[:, :], zs[:, :]))
                    chain(nc.vector.tensor_tensor(prob[:, :, :], prob[:, :, :], per_tile(mx[:, :]), ALU.mult))
                    dve.sem_inc(s_pace, 1)
                    for q in range(QT):
                        nc.vector.max(top[:, q, :], prob[:, q, :]).then_inc(s_sum, 1)
                    for q in range(QT):
                        dve.wait_ge(s_sum, 16 * (s - 1) + q + 1)
                        dve.sem_inc(s_pace, 1)
                        nc.vector.max_index(idx[:, q, :], top[:, q, :], prob[:, q, :]).then_inc(s_sum, 1)
                    dve.wait_ge(s_sum, 16 * s)
                    chain(nc.vector.tensor_copy(idx_f[:, :, :], idx[:, :, :]))
                    chain(nc.vector.tensor_tensor(zs[:, :], top[:, :, 0], top[:, :, 1], ALU.add))
                    chain(nc.vector.reciprocal(mx[:, :], zs[:, :]))
                    for k in range(2):
                        nc.vector.tensor_tensor(pick[:, k, :, :], wide(expert), per_tile(idx_f[:, :, k]),
                                                ALU.is_equal).then_inc(s_comb, 1)
                        nc.vector.tensor_tensor(top[:, :, k], top[:, :, k], mx[:, :], ALU.mult).then_inc(s_comb, 1)
                    dve.wait_ge(s_comb, 7 * (s - 1) + 4)
                    for k in range(2):
                        nc.vector.tensor_tensor(pick[:, k, :, :], pick[:, k, :, :], per_tile(top[:, :, k]),
                                                ALU.mult).then_inc(s_comb, 1)
                    dve.wait_ge(s_comb, 7 * (s - 1) + 6)
                    nc.vector.tensor_tensor(comb[:, :, :], pick[:, 0, :, :], pick[:, 1, :, :], ALU.add)\
                        .then_inc(s_comb, 1)
                elif name == "FIN":
                    n = norm_index(name, s)
                    dve.wait_ge(s_free, bank_n)
                    nc.vector.tensor_tensor(xa[:, :, :], xa[:, :, :], acc[:, :, :], ALU.add).then_inc(s_added, 1)
                    dve.wait_ge(s_added, s)
                    layer_norm(n)
                    dve.wait_ge(l_affine, 2 * s)
                    layer_norm(n + 1)

            dve.wait_ge(s_iota, 1)
            passes(dve, step)

        @block.tensor
        def _(pe):
            late = [None]

            def weigh_values(s):
                if late[0] is None:
                    return
                hp, i = late[0]
                late[0] = None
                n = 128 * s + 16 * hp + i
                par, kt = i // QT, i % QT
                pe.wait_ge(s_exp, n + 1)
                if i == 0 and not (which(s)[2] and hp == 0):
                    pe.wait_ge(s_oc, 8 * s + hp)
                for t in range(2):
                    j = 32 * (2 * par + t)
                    ins = nc.tensor.matmul(p_o[j:j + VH, :], va[:, kt, 2 * hp + par, :], pt[:, i % 4, tokens(t)],
                                           start=kt == 0, stop=kt == QT - 1)
                ins.then_inc(s_pv, 1)

            def step(x, s, bank_n):
                name, b, starts, zeroth = x[0], *which(s)
                if name in BANK_USES and name != "PRE":
                    pe.wait_ge(s_free, bank_n)
                if name == "PRE":
                    pe.wait_ge(s_setup, 6)
                    for k in range(4):
                        nc.tensor.matmul(bank[:, k:k + 1], w["bqk"][0:1, k, :], ident[0:1, 0:1], start=True, stop=True)
                    nc.tensor.transpose(bank[:, 4:4 + E * FC], w["b1"][:, :], ident[0:E * FC, 0:E * FC])\
                        .then_inc(s_bank, 1)
                elif name == "A":
                    head, q = x[1], x[2]
                    n = 8 * (16 * b + head) + q
                    if q == 0 and head % 4 == 0:
                        pe.wait_ge(s_st[head % H // 4], 16 * ST_DMAS * (b + 1 + head // H))
                    if not (starts and n == 0):
                        pe.wait_ge(s_max, n)
                    for t in range(2):
                        ins = nc.tensor.matmul(s1[:, tokens(t)], qs[:, head % H // 2, tile(q)],
                                               ks[:, head % H, tokens(t)], start=True, stop=True)
                    ins.then_inc(s_s1, 1)
                elif name == "B":
                    hp, i = x[1], x[2]
                    head, kt = 2 * hp + i // QT, i % QT
                    n = 128 * s + 16 * hp + i
                    if i == 0:
                        pe.wait_ge(s_mr[hp % 2], 64 * (4 * s + hp // 2 + 1))
                    if not (zeroth and n < 2):
                        pe.wait_ge(s_exp, n - 1)
                    for t in range(2):
                        ins = nc.tensor.matmul(s2[i % 2][:, tokens(t)], ks[:, head, tile(kt)], qs[:, hp, tokens(t)],
                                               start=True, stop=True)
                    ins.then_inc(s_s2, 1)
                    if hp == 0 and i == 1:
                        pe.wait_ge(s_free, bank_n)
                    weigh_values(s)
                    late[0] = (hp, i)
                elif name == "BF":
                    weigh_values(s)
                elif name == "MT":
                    hp = x[1]
                    pe.wait_ge(s_max, 16 * (8 * b + hp + 1))
                    nc.tensor.transpose(bank[0:2 * QT, 0:P], nm[:, hp % 2, :, :].rearrange("p r q -> p (r q)"),
                                        ident[:, :]).then_inc(s_bank, 1)
                elif name == "OT":
                    pe.wait_ge(s_oc, 8 * s + x[1] + 1)
                    for t in range(4):
                        ins = nc.tensor.transpose(bank[:, tile(t)], o_sb[:, tile(t)], ident[:, :])
                    ins.then_inc(s_bank, 1)
                elif name == "HID":
                    e, f, t = x[1], x[2] // 2, x[2] % 2
                    nc.tensor.matmul(bank[:, :], w["W1"][:, e, tile(f)], xt[:, tokens(t)], start=True, stop=True)\
                        .then_inc(s_bank, 1)
                elif name == "Y":
                    e, q = x[1], x[2]
                    for f in range(FC):
                        ins = nc.tensor.matmul(bank[:, 0:D], hid[:, f, tile(q)], w["W2"][:, e, f, :], start=f == 0,
                                               stop=f == FC - 1)
                    ins.then_inc(s_bank, 1)
                elif name in ("HT", "AT", "XT"):
                    if name == "HT":
                        pe.wait_ge(s_hq, 16 * (s + 2))
                    if name == "XT":
                        pe.wait_ge(l_affine, 2 * (s - 1) + 1)
                    src = {"HT": hq, "AT": ao, "XT": xa}[name]
                    for q in range(4):
                        ins = nc.tensor.transpose(bank[:, tile(q)], src[:, 4 * x[1] + q, :], ident[:, :])
                    ins.then_inc(s_bank, 1)
                elif name == "QK":
                    k, t = x[1], x[2]
                    for i, wt in enumerate((w[("Wq", "Wk")[k]][:, :], wp[:, k, :])):
                        if i:
                            pe.wait_ge(s_free, bank_n + 1)
                        nc.tensor.matmul(bank[:, :], wt, ht[:, tokens(t)], start=True, stop=True).then_inc(s_bank, 1)
                elif name == "V":
                    for q in range(4):
                        ins = nc.tensor.matmul(bank[:, tile(q)], ht[:, tile(4 * x[1] + q)], w["Wv"][:, :], start=True,
                                               stop=True)
                    ins.then_inc(s_bank, 1)
                elif name == "WO":
                    for q in range(4):
                        ins = nc.tensor.matmul(bank[:, tile(q)], aot[:, tile(4 * x[1] + q)], w["Wo"][:, :], start=True,
                                               stop=True)
                    ins.then_inc(s_bank, 1)
                elif name == "GT":
                    for q in range(QT):
                        ins = nc.tensor.matmul(bank[:, E * q:E * q + E], xt[:, tile(q)], w["Wg"][:, :], start=True,
                                               stop=True)
                    ins.then_inc(s_bank, 1)
                elif name == "CT":
                    pe.wait_ge(s_comb, 7 * s)
                    for q in range(4):
                        ins = nc.tensor.transpose(bank[0:E, tile(q)], comb[:, 4 * x[1] + q, :], ident[:, :])
                    ins.then_inc(s_bank, 1)
                elif name == "B2":
                    for q in range(4):
                        ins = nc.tensor.matmul(bank[:, tile(q)], ct[:, tile(4 * x[1] + q)], w["b2"][:, :], start=True,
                                               stop=True)
                    ins.then_inc(s_bank, 1)

            passes(pe, step)


def program(nc, io):
    x1_dram = nc.dram_tensor("x1_dram", (B, T, D), F32).ap()
    h_dram = nc.dram_tensor("h_dram", (B + 1, T, D), F32).ap()
    parts_dram = nc.dram_tensor("parts_dram", (2, 3, P, T), BF16).ap()
    ctx = ExitStack()
    with ctx:
        ident = ctx.enter_context(nc.sbuf_tensor("ident", [P, P], F32))
        eps = ctx.enter_context(nc.sbuf_tensor("eps", [P, 1], F32))
        w = constants(ctx, nc)
        s_weights = ctx.enter_context(nc.semaphore("s_weights"))
        with ExitStack() as first:
            xt = {n: first.enter_context(nc.sbuf_tensor(n, [P, k, D], F32))
                  for n, k in (("x", NK), ("f", NK), ("v_all", NK + 1))}
            xt["ident"], xt["eps"] = ident, eps
            window_attention(nc, io, xt, w, s_weights)
            middle(nc, io, xt, x1_dram, h_dram)
        second_layer(nc, io, w, ident, eps, x1_dram, h_dram, parts_dram)


_INS = {"x": "L0_attn_feature", "wq_w": "L0_attn_wq_w", "wq_b": "L0_attn_wq_b", "w2_w": "L0_attn_w2_w",
        "w2_b": "L0_attn_w2_b", "ln_g": "L0_attn_ln_g", "ln_b": "L0_attn_ln_b"}
_INS.update({n: f"L0_ffn_{n}" for n in ("Wq", "bq", "Wk", "bk", "Wv", "bv", "Wo", "bo", "Wg", "bg", "W1", "b1", "W2",
                                        "b2", "g1", "be1", "g2", "be2")})


def rotation_tables():
    inv_freq = (1.0 / 10000.0 ** (np.arange(0, HD, 2, dtype=np.float32) / np.float32(HD))).astype(np.float32)
    angle = np.arange(T, dtype=np.float32)[None, :] * inv_freq[:, None]
    sign = np.repeat(np.float32([-1, 1]), HD // 2)[:, None]
    return np.tile(np.cos(angle), (2 * H, 1)), np.tile(sign * np.tile(np.sin(angle), (2, 1)), (H, 1))


def kernel(**inputs):
    import concourse.bacc as bacc
    from concourse.bass_utils import run_bass_kernel_spmd

    nc = bacc.Bacc("TRN2", target_bir_lowering=False, num_devices=1)
    arrays = {name: np.ascontiguousarray(inputs[full]) for name, full in _INS.items()}
    arrays["cos"], arrays["sin"] = rotation_tables()
    io = {name: nc.dram_tensor(f"in_{name}", a.shape, mybir.dt.from_np(a.dtype), kind="ExternalInput").ap()
          for name, a in arrays.items()}
    io["out"] = nc.dram_tensor("out_0", (B, T, D), F32, kind="ExternalOutput").ap()
    program(nc, io)
    ran = run_bass_kernel_spmd(nc, [{f"in_{name}": a for name, a in arrays.items()}], core_ids=[0])
    return ran.results[0]["out_0"]
```

```python
from contextlib import ExitStack

import numpy as np

import concourse.bass as bass
from concourse import mybir

F32 = mybir.dt.float32
BF16 = mybir.dt.bfloat16
U32 = mybir.dt.uint32
ALU = mybir.AluOpType
ACT = mybir.ActivationFunctionType
AX = mybir.AxisListType

P = 128
B, T, D = 4, 1024, 128
WIN = 64
L = 32
NK = T // L
NC = NK - WIN // L
ROW = WIN + 1

H, HD = 16, 8
HP = H // 2
E, FF = 8, 512
FC = FF // P
QT = T // P
HALF = T // 2
VH = HD + 1
SCALE = 1.0 / float(np.sqrt(HD))
Q_PARTS = (0, 0, 1, 0, 1, 2)
K_PARTS = (0, 1, 0, 2, 1, 0)
M_ROW = HD * len(Q_PARTS)
EPS = 1e-5


def window_attention(nc, io, xt, w, s_weights):
    ctx = ExitStack()
    with ctx:
        def sb(name, shape, dt=F32):
            return ctx.enter_context(nc.sbuf_tensor(name, shape, dt))

        def ps(name, shape, dt=F32):
            return ctx.enter_context(nc.psum_tensor(name, shape, dt))

        def sem(name):
            return ctx.enter_context(nc.semaphore(name))

        f, v_all, x = xt["f"], xt["v_all"], xt["x"]
        ident, eps = xt["ident"], xt["eps"]
        mask = sb("mask", [P, B, L])
        wq = sb("wq", [P, D])
        bq = sb("bq", [P, 1])
        w2 = sb("w2", [P, 1])
        b0 = sb("b0", [P, 1])
        b0_row = sb("b0_row", [P, L])
        zero_row = sb("zero_row", [P, L])
        stats = sb("stats", [P, NK, 6])
        mv = sb("mv", [P, NK, 2])
        std = sb("std", [P, NK])
        rstd = sb("rstd", [P, NK])
        ft = sb("ft", [P, 2, 4 * P])
        qt = sb("qt", [P, NK + 1, P])
        qn = sb("qn", [P, P])
        vt1 = sb("vt1", [P, P])
        vt2 = sb("vt2", [P, P])
        vr = sb("vr", [P, D])
        bdg = sb("bdg", [P, 2, P])
        bdc = sb("bdc", [P, 2, P])
        tab = sb("tab", [P, 3, WIN + L])
        row = sb("row", [P, 2, ROW + 1])
        nmax = sb("nmax", [P, 2])
        ex = sb("ex", [P, 2, ROW])
        z = sb("z", [P, 2])
        rz = sb("rz", [P, 2])
        junk = sb("junk", [P, 4, ROW])
        raw = sb("raw", [P, 3])

        pf = ps("pf", [P, 2, 4 * P])
        pq = ps("pq", [P, 2, 4 * P])
        p_s = ps("p_s", [P, 512])
        p_g = ps("p_g", [P, 512])
        p_v = ps("p_v", [P, 512])
        p_t = ps("p_t", [P, 512])

        s_x = [sem(f"s_x{b}") for b in range(B)]
        s_w = sem("s_w")
        s_const, s_ident, s_mask = sem("s_const"), sem("s_ident"), sem("s_mask")
        s_stats, s_mv, s_std, s_rstd, s_f = sem("s_stats"), sem("s_mv"), sem("s_std"), sem("s_rstd"), sem("s_f")
        s_ft, s_ftc, s_pq, s_qt = sem("s_ft"), sem("s_ftc"), sem("s_pq"), sem("s_qt")
        s_init = sem("s_init")
        s_pace, s_pace_act = sem("s_pace"), sem("s_pace_act")
        s_vt0 = sem("s_vt0")
        s_qn = sem("s_qn")
        s_table = sem("s_table")
        s_scores = sem("s_scores")
        s_row, s_max, s_exp, s_rz, s_new, s_coef = (sem("s_row"), sem("s_max"), sem("s_exp"), sem("s_rz"),
                                                   sem("s_new"), sem("s_coef"))
        s_raw, s_raw_score, s_score = sem("s_raw"), sem("s_raw_score"), sem("s_score")
        s_clear = sem("s_clear")
        s_bdc, s_pv, s_vr, s_vall, s_pt, s_vt2, s_vt1, s_g, s_bdg = (
            sem("s_bdc"), sem("s_pv"), sem("s_vr"), sem("s_vall"), sem("s_pt"), sem("s_vt2"), sem("s_vt1"),
            sem("s_g"), sem("s_bdg"))

        block = ctx.enter_context(nc.Block())

        @block.sync
        def _(sp):
            for b in range(B):
                sp.dma_start(x[L * b:L * b + L, :, :],
                             io["x"][b].rearrange("(k j) d -> j k d", j=L)).then_inc(s_x[b], 16)
            sp.dma_start(wq[:, :], io["wq_w"]).then_inc(s_w, 16)
            sp.dma_start(bq[:, :], io["wq_b"].rearrange("(d a) -> d a", a=1)).then_inc(s_w, 16)
            sp.dma_start(w2[:, :], io["w2_w"].rearrange("(d a) -> d a", a=1)).then_inc(s_w, 16)
            sp.dma_start(b0[:, :], io["w2_b"].rearrange("(d a) -> d a", a=1).broadcast_to((P, 1))).then_inc(s_w, 16)
            sp.wait_ge(s_weights, load_constants(sp, w, io, s_weights))

        @block.gpsimd
        def _(pool):
            nc.gpsimd.memset(eps[:, :], EPS).then_inc(s_const, 1)
            nc.gpsimd.memset(zero_row[:, :], 0.0).then_inc(s_const, 1)
            nc.gpsimd.memset(ident[:, :], 0.0).then_inc(s_ident, 1)
            pool.wait_ge(s_ident, 1)
            nc.gpsimd.affine_select(out=ident[:, :], in_=ident[:, :], compare_op=ALU.not_equal, fill=1.0, base=0,
                                    pattern=[[-1, P]], channel_multiplier=1).then_inc(s_ident, 1)
            nc.gpsimd.memset(mask[:, :, :], 1.0).then_inc(s_mask, 1)
            pool.wait_ge(s_mask, 1)
            nc.gpsimd.affine_select(out=mask[:, :, :], in_=mask[:, :, :], compare_op=ALU.is_ge, fill=0.0, base=0,
                                    pattern=[[-L, B], [0, L]], channel_multiplier=1).then_inc(s_mask, 1)
            pool.wait_ge(s_mask, 2)
            nc.gpsimd.affine_select(out=mask[:, :, :], in_=mask[:, :, :], compare_op=ALU.is_ge, fill=0.0, base=L - 1,
                                    pattern=[[L, B], [0, L]], channel_multiplier=-1).then_inc(s_mask, 1)
            pool.wait_ge(s_mask, 3)
            pool.wait_ge(s_f, 2)
            nc.gpsimd.tensor_copy(v_all[:, 0, :], f[:, 1, :]).then_inc(s_init, 1)
            nc.gpsimd.tensor_copy(v_all[:, 1, :], f[:, 0, :]).then_inc(s_vall, 1)
            nc.gpsimd.memset(bdc[:, 1, :], 0.0).then_inc(s_init, 1)
            nc.gpsimd.tensor_copy(bdc[:, 0, :], ident[:, :]).then_inc(s_bdc, 1)
            pool.wait_ge(s_qt, 1)
            nc.gpsimd.tensor_copy(qn[:, :], qt[:, 2, :]).then_inc(s_qn, 1)
            with pool.Fori(0, NC) as c:
                pool.wait_ge(s_vr, c + 1)
                pool.sem_inc(s_pace, 1)
                nc.gpsimd.tensor_copy(v_all[:, c + 2, :], vr[:, :]).then_inc(s_vall, 1)
                pool.wait_ge(s_scores, c + 1)
                pool.sem_inc(s_pace, 1)
                nc.gpsimd.tensor_copy(vt2[:, :], vt1[:, :]).then_inc(s_vt2, 1)
                nc.gpsimd.tensor_copy(qn[:, :], qt[:, c + 3, :]).then_inc(s_qn, 1)
                pool.wait_ge(s_coef, L * (c + 1))
                pool.wait_ge(s_pv, c + 1)
                for g in range(2):
                    last = nc.gpsimd.tensor_tensor(
                        bdc[:, g, :].rearrange("p (b j) -> p b j", b=B),
                        tab[:, 1 + g, WIN:].unsqueeze(1).broadcast_to((P, B, L)), mask[:, :, :], ALU.mult)
                last.then_inc(s_bdc, 1)

        @block.scalar
        def _(act):
            act.wait_ge(s_mv, NK)
            act.wait_ge(s_const, 2)
            nc.scalar.activation(std[:, :], mv[:, :, 1], ACT.Sqrt, bias=eps[:, :]).then_inc(s_std, 1)
            for g in range(8):
                act.wait_ge(s_ft, g + 1)
                if g >= 2:
                    act.wait_ge(s_pq, g - 1)
                if g == 2:
                    act.wait_ge(s_vt0, 2)
                nc.scalar.copy(ft[:, g % 2, :], pf[:, g % 2, :]).then_inc(s_ftc, 1)
            nc.scalar.preload_act_table(ACT.Exp)
            act.wait_ge(s_init, 14)
            with act.Fori(0, NC) as c:
                for r in range(L):
                    act.wait_ge(s_max, L * c + r + 1)
                    nc.scalar.activation(ex[:, r % 2, :], row[:, r % 2, 1:], ACT.Exp, bias=nmax[:, r % 2:r % 2 + 1],
                                         accum_out=z[:, r % 2:r % 2 + 1]).then_inc(s_exp, 1)
                    if r == 1:
                        act.wait_ge(s_vall, c + 1)
                        act.sem_inc(s_pace_act, 1)
                        act.wait_ge(s_pv, c + 1)
                        nc.scalar.copy(vr[:, :], p_v[:, 0:D]).then_inc(s_vr, 1)
                    if r == 4:
                        act.wait_ge(s_vt2, c + 1)
                        act.sem_inc(s_pace_act, 1)
                        act.wait_ge(s_pt, c + 1)
                        nc.scalar.copy(vt1[:, :], p_t[:, 0:P]).then_inc(s_vt1, 1)
                    if 8 <= r < 8 + B:
                        act.wait_ge(s_g, c + 1)
                        q = slice(L * (r - 8), L * (r - 8) + L)
                        nc.scalar.copy(bdg[q, :, q], p_g[q, 0:2 * P].rearrange("p (g i) -> p g i", g=2)[:, :, q])\
                            .then_inc(s_bdg, 1)

        @block.vector
        def _(dve):
            for b in range(B):
                dve.wait_ge(s_x[b], 16)
            for k in range(NK):
                nc.vector.bn_stats(stats[:, k, :], x[:, k, :]).then_inc(s_stats, 1)
            for k in range(NK):
                dve.wait_ge(s_stats, k + 1)
                nc.vector.bn_aggr(mv[:, k, :], stats[:, k, :]).then_inc(s_mv, 1)
            dve.wait_ge(s_std, 1)
            nc.vector.reciprocal(rstd[:, :], std[:, :]).then_inc(s_rstd, 1)
            dve.wait_ge(s_rstd, 1)
            for k in range(NK):
                nc.vector.tensor_scalar(f[:, k, :], x[:, k, :], mv[:, k, 0:1], rstd[:, k:k + 1], ALU.subtract,
                                        ALU.mult).then_inc(s_f, 1)
            dve.wait_ge(s_w, 64)
            for g in range(8):
                dve.wait_ge(s_pq, g + 1)
                nc.vector.tensor_scalar(qt[:, 4 * g:4 * g + 4, :], pq[:, g % 2, :].rearrange("p (k i) -> p k i", k=4),
                                        bq[:, :], w2[:, :], ALU.add, ALU.mult).then_inc(s_qt, 1)
                if g == 0:
                    nc.vector.tensor_copy(vt1[:, :], ft[:, 0, 0:P]).then_inc(s_vt0, 1)
                    nc.vector.tensor_copy(vt2[:, :], ft[:, 0, P:2 * P]).then_inc(s_vt0, 1)
                    dve.wait_ge(s_vt0, 2)
            nc.vector.memset(qt[:, NK, :], 0.0).then_inc(s_init, 1)
            nc.vector.memset(tab[:, :, :], 0.0).then_inc(s_init, 1)
            nc.vector.memset(bdg[:, :, :], 0.0).then_inc(s_init, 1)
            dve.wait_ge(s_ident, 2)
            dve.wait_ge(s_const, 2)
            nc.vector.tensor_scalar(b0_row[:, :], zero_row[:, :], b0[:, :], None, ALU.add).then_inc(s_init, 1)
            dve.wait_ge(s_init, 6)
            for b in range(B):
                q = slice(L * b, L * b + L)
                for g in range(2):
                    nc.vector.tensor_copy(tab[q, 1 + g, L * g:L * g + L], ident[q, q]).then_inc(s_init, 1)
            dve.wait_ge(s_init, 14)
            dve.wait_ge(s_mask, 3)

            def weighted(g, k, r, done):
                nc.vector.scalar_tensor_tensor(junk[:, g, :], ex[:, k, :], 1.0, tab[:, g, r:r + ROW], ALU.mult, ALU.mult,
                                               accum_out=raw[:, g:g + 1]).then_inc(done, 1)

            def normalised(g0, g1, k, r, done):
                nc.vector.tensor_tensor(tab[:, g0:g1, r + WIN:r + ROW], raw[:, g0:g1].unsqueeze(2),
                                        rz[:, k:k + 1].unsqueeze(1).broadcast_to((P, g1 - g0, 1)),
                                        ALU.mult).then_inc(done, 1)

            with dve.Fori(0, NC) as c:
                nc.vector.tensor_copy(tab[:, 0, WIN:], b0_row[:, :]).then_inc(s_table, 1)
                dve.wait_ge(s_scores, c + 1)
                nc.vector.tensor_scalar(tab[:, 0, 0:WIN], p_s[:, 0:WIN], b0[:, :], None, ALU.add).then_inc(s_table, 1)
                dve.wait_ge(s_table, 2 * (c + 1))
                dve.sem_inc(s_pace, 1)
                nc.vector.stream_shuffle(row[:, 0, 1:], tab[:, 0, 0:ROW], [0] * L).then_inc(s_row, 1)
                nc.vector.stream_shuffle(row[:, 1, :], tab[:, 0, 0:ROW + 1], [1] * L).then_inc(s_row, 1)
                dve.wait_ge(s_row, L * c + 1)
                nc.vector.reduce_max(nmax[:, 0:1], row[:, 0, 1:], AX.X, negate=True).then_inc(s_max, 1)
                dve.wait_ge(s_bdc, c + 1)
                nc.vector.memset(tab[:, 1:3, WIN:], 0.0).then_inc(s_clear, 1)
                dve.wait_ge(s_clear, c + 1)
                for r in range(L):
                    k, n = r % 2, L * c + r
                    last = r == L - 1
                    dve.wait_ge(s_exp, n + 1)
                    nc.vector.reciprocal(rz[:, k:k + 1], z[:, k:k + 1]).then_inc(s_rz, 1)
                    if r:
                        dve.wait_ge(s_coef, n)
                    weighted(1, k, r, s_raw)
                    if not last:
                        dve.wait_ge(s_row, L * c + r + 2)
                        dve.wait_ge(s_rz, n + 1)
                        nc.vector.scalar_tensor_tensor(junk[:, 3, :], ex[:, k, :], rz[:, k:k + 1],
                                                       row[:, 1 - k, 0:ROW], ALU.mult, ALU.mult,
                                                       accum_out=row[:, 1 - k, WIN:ROW]).then_inc(s_new, 1)
                        weighted(0, k, r, s_raw_score)
                        dve.wait_ge(s_new, (L - 1) * c + r + 1)
                        nc.vector.reduce_max(nmax[:, 1 - k:2 - k], row[:, 1 - k, 1:], AX.X, negate=True)\
                            .then_inc(s_max, 1)
                        dve.wait_ge(s_raw_score, (L - 1) * c + r + 1)
                        normalised(0, 1, k, r, s_score)
                    weighted(2, k, r, s_raw)
                    if r < L - 2:
                        dve.wait_ge(s_score, (L - 1) * c + r + 1)
                        dve.sem_inc(s_pace, 1)
                        nc.vector.stream_shuffle(row[:, k, :], tab[:, 0, r + 1:r + 2 + ROW], [r + 2] * L)\
                            .then_inc(s_row, 1)
                    dve.wait_ge(s_raw, 2 * n + 2)
                    normalised(1, 3, k, r, s_coef)
            dve.wait_ge(s_pv, NC + 1)
            nc.vector.tensor_copy(v_all[:, NC + 2, :], p_v[:, 0:D]).then_inc(s_vr, 1)

        @block.tensor
        def _(pe):
            pe.wait_ge(s_w, 64)
            pe.wait_ge(s_ident, 2)
            for g in range(8):
                pe.wait_ge(s_f, 4 * g + 4)
                if g >= 2:
                    pe.wait_ge(s_ftc, g - 1)
                for k in range(4):
                    ins = nc.tensor.transpose(pf[:, g % 2, P * k:P * k + P], f[:, 4 * g + k, :], ident[:, :])
                ins.then_inc(s_ft, 1)
                pe.wait_ge(s_ftc, g + 1)
                if g >= 2:
                    pe.wait_ge(s_qt, g - 1)
                nc.tensor.matmul(pq[:, g % 2, :], wq[:, :], ft[:, g % 2, :], start=True, stop=True).then_inc(s_pq, 1)
            pe.wait_ge(s_qn, 1)
            pe.wait_ge(s_vt0, 2)
            for b in range(B):
                q = slice(L * b, L * b + L)
                for g, vt in enumerate((vt1, vt2)):
                    ins = nc.tensor.matmul(p_s[q, L * g:L * g + L], qn[:, q], vt[:, q], start=True, stop=True)
            ins.then_inc(s_scores, 1)
            pe.wait_ge(s_init, 14)
            with pe.Fori(0, NC) as c:
                pe.wait_ge(s_bdc, c + 1)
                pe.wait_ge(s_vall, c + 1)
                for g in range(2):
                    ins = nc.tensor.matmul(p_v[:, 0:D], bdc[:, g, :], v_all[:, c + g, :], start=g == 0, stop=g == 1)
                ins.then_inc(s_pv, 1)
                pe.wait_ge(s_vr, c + 1)
                nc.tensor.transpose(p_t[:, 0:P], vr[:, :], ident[:, :]).then_inc(s_pt, 1)
                pe.wait_ge(s_vt1, c + 1)
                pe.wait_ge(s_qn, c + 2)
                for g, vt in enumerate((vt2, vt1)):
                    ins = nc.tensor.matmul(p_g[:, P * g:P * g + P], vt[:, :], qn[:, :], start=True, stop=True)
                ins.then_inc(s_g, 1)
                pe.wait_ge(s_table, 2 * (c + 1))
                for b in range(B):
                    q = slice(L * b, L * b + L)
                    nc.tensor.matmul(p_s[q, 0:L], qn[:, q], vt1[:, q], start=True, stop=True)
                pe.wait_ge(s_bdg, B * (c + 1))
                pe.wait_ge(s_coef, L * (c + 1))
                for g in range(2):
                    ins = nc.tensor.matmul(p_s[:, L:WIN], bdg[:, g, :], tab[:, 1 + g, WIN:], start=g == 0, stop=g == 1)
                ins.then_inc(s_scores, 1)
            pe.wait_ge(s_bdc, NC + 1)
            pe.wait_ge(s_vall, NC + 1)
            for g in range(2):
                ins = nc.tensor.matmul(p_v[:, 0:D], bdc[:, g, :], v_all[:, NC + g, :], start=g == 0, stop=g == 1)
            ins.then_inc(s_pv, 1)




def middle(nc, io, xt, x1_dram, h_dram):
    ctx = ExitStack()
    with ctx:
        def sb(name, shape, dt=F32):
            return ctx.enter_context(nc.sbuf_tensor(name, shape, dt))

        def sem(name):
            return ctx.enter_context(nc.semaphore(name))

        x, f, eps = xt["x"], xt["f"], xt["eps"]
        y = xt["v_all"][:, 1:, :]
        g_row, b_row = sb("g_row", [P, D]), sb("b_row", [P, D])
        stats, mv = sb("stats2", [P, NK, 6]), sb("mv2", [P, NK, 2])
        std, rstd = sb("std2", [P, NK]), sb("rstd2", [P, NK])
        G, GK = 4, NK // 4
        m_w, m_tanh, m_y, m_stats, m_var, m_std, m_rstd, m_norm, m_scaled, m_affine, m_res, m_out = (
            sem(n) for n in ("m_w", "m_tanh", "m_y", "m_stats", "m_var", "m_std", "m_rstd", "m_norm", "m_scaled",
                             "m_affine", "m_res", "m_out"))
        block = ctx.enter_context(nc.Block())

        def ks(g):
            return slice(GK * g, GK * g + GK)

        def wide(t):
            return t[:, :].unsqueeze(1).broadcast_to((P, GK, D))

        @block.sync
        def _(sp):
            sp.dma_start(g_row[:, :], io["ln_g"].rearrange("(a d) -> a d", a=1).broadcast_to((P, D))).then_inc(m_w, 16)
            sp.dma_start(b_row[:, :], io["ln_b"].rearrange("(a d) -> a d", a=1).broadcast_to((P, D))).then_inc(m_w, 16)
            for b in range(B):
                q = slice(L * b, L * b + L)
                if b == 0:
                    sp.wait_ge(m_res, G)
                sp.dma_start(x1_dram[b].rearrange("(k j) d -> j k d", j=L), x[q, :, :]).then_inc(m_out, 16)
            for b in range(B + 1):
                q = slice(L * (b % B), L * (b % B) + L)
                if b == 0:
                    sp.wait_ge(m_norm, 3 * NK)
                sp.dma_start(h_dram[b].rearrange("(k j) d -> j k d", j=L), f[q, :, :]).then_inc(m_out, 16)
            sp.wait_ge(m_out, 16 * (2 * B + 1))

        @block.scalar
        def _(act):
            for g in range(G):
                nc.scalar.activation(y[:, ks(g), :], y[:, ks(g), :], ACT.Tanh).then_inc(m_tanh, 1)
            for n in range(3):
                for g in range(G):
                    act.wait_ge(m_var, NK * n + GK * (g + 1))
                    if n:
                        act.wait_ge(m_rstd, G * (n - 1) + g + 1)
                    nc.scalar.activation(std[:, ks(g)], mv[:, ks(g), 1], ACT.Sqrt, bias=eps[:, :]).then_inc(m_std, 1)

        @block.gpsimd
        def _(pool):
            pool.wait_ge(m_w, 32)
            for g in range(G):
                pool.wait_ge(m_norm, GK * (g + 1))
                nc.gpsimd.tensor_tensor(y[:, ks(g), :], y[:, ks(g), :], wide(g_row), ALU.mult).then_inc(m_scaled, 1)
                pool.wait_ge(m_scaled, g + 1)
                nc.gpsimd.tensor_tensor(y[:, ks(g), :], y[:, ks(g), :], wide(b_row), ALU.add).then_inc(m_affine, 1)

        @block.vector
        def _(dve):
            for g in range(G):
                dve.wait_ge(m_tanh, g + 1)
                nc.vector.scalar_tensor_tensor(y[:, ks(g), :], y[:, ks(g), :], 1.0, f[:, ks(g), :], ALU.add,
                                               ALU.mult).then_inc(m_y, 1)

            def statistics(n, g, src, ready, at):
                dve.wait_ge(ready, at)
                for k in range(GK * g, GK * g + GK):
                    nc.vector.bn_stats(stats[:, k, :], src[:, k, :]).then_inc(m_stats, 1)
                for k in range(GK * g, GK * g + GK):
                    dve.wait_ge(m_stats, NK * n + k + 1)
                    if n and k == GK * g:
                        dve.wait_ge(m_norm, NK * (n - 1) + GK * (g + 1))
                    nc.vector.bn_aggr(mv[:, k, :], stats[:, k, :]).then_inc(m_var, 1)

            def normed(n, g, out, src):
                dve.wait_ge(m_std, G * n + g + 1)
                nc.vector.reciprocal(rstd[:, ks(g)], std[:, ks(g)]).then_inc(m_rstd, 1)
                dve.wait_ge(m_rstd, G * n + g + 1)
                for k in range(GK * g, GK * g + GK):
                    nc.vector.tensor_scalar(out[:, k, :], src[:, k, :], mv[:, k, 0:1], rstd[:, k:k + 1], ALU.subtract,
                                            ALU.mult).then_inc(m_norm, 1)

            for g in range(G):
                statistics(0, g, y, m_y, g + 1)
            for g in range(G):
                normed(0, g, y, y)
            for g in range(G):
                statistics(1, g, y, m_affine, g + 1)
            for g in range(G):
                normed(1, g, y, y)
            for g in range(G):
                dve.wait_ge(m_norm, NK + GK * (g + 1))
                nc.vector.tensor_tensor(x[:, ks(g), :], x[:, ks(g), :], y[:, ks(g), :], ALU.add).then_inc(m_res, 1)
            for g in range(G):
                statistics(2, g, x, m_res, g + 1)
            for g in range(G):
                normed(2, g, f, x)


def constants(ctx, nc):
    def sb(name, shape, dt=F32):
        return ctx.enter_context(nc.sbuf_tensor(name, shape, dt))

    w = {n: sb(f"w_{n}", [P, D]) for n in ("Wq", "Wk", "Wv", "Wo")}
    w["Wg"] = sb("w_Wg", [P, E])
    w["W1"] = sb("w_W1", [P, E, FF])
    w["W2"] = sb("w_W2", [P, E, FC, D])
    w["b2"] = sb("w_b2", [E, D])
    w["b1"] = sb("w_b1", [E * FC, P])
    w["bqk"] = sb("w_bqk", [1, 4, D])
    for n in ("bv", "bo", "g1", "be1", "g2", "be2"):
        w[n] = sb(f"w_{n}", [P, D])
    w["bg"] = sb("w_bg", [P, E])
    w["cos"], w["sin"] = sb("w_cos", [P, T]), sb("w_sin", [P, T])
    return w


def load_constants(sp, w, io, arrived):
    def row(n):
        return io[n].rearrange("(a d) -> a d", a=1)

    def halves(n):
        return row(n).rearrange("a (h t e) -> a h t e", h=H, t=2)

    to, of = w["bqk"], w["bqk"][:, :, :].rearrange("a k (h t e) -> a k h t e", h=H, t=2)
    pairs = [(w[n][:, :], io[n]) for n in ("Wq", "Wk", "Wv", "Wo", "Wg")]
    pairs += [(w["W1"][:, :, :], io["W1"].rearrange("e d f -> d e f"))]
    pairs += [(w["W2"][:, e, :, :], io["W2"][e].rearrange("(c p) d -> p c d", p=P)) for e in range(E)]
    pairs += [(w["b2"][:, :], io["b2"]), (w["b1"][:, :], io["b1"].rearrange("e (c p) -> (e c) p", p=P))]
    for k, n in enumerate(("bq", "bk")):
        pairs += [(to[:, 2 * k, :], row(n))]
        pairs += [(of[:, 2 * k + 1, :, t, :], halves(n)[:, :, 1 - t, :]) for t in range(2)]
    pairs += [(w[n][:, :], row(n).broadcast_to((P, D))) for n in ("bv", "bo", "g1", "be1", "g2", "be2")]
    pairs += [(w["bg"][:, :], row("bg").broadcast_to((P, E))), (w["cos"][:, :], io["cos"]), (w["sin"][:, :], io["sin"])]
    for out, in_ in pairs:
        sp.dma_start(out, in_).then_inc(arrived, 16)
    return 16 * len(pairs)


BANK_USES = {"AT": 1, "WO": 1, "XT": 1, "GL": 1, "CT": 1, "B2": 1, "V": 1, "HID": 1, "Y": 1, "MT": 1, "OT": 1,
             "HT": 1, "QK": 2, "PRE": 1}


AHEAD = {(0, 4): [("HQ",)], (1, 4): [("HT", 0)], (1, 6): [("HT", 1)], (2, 4): [("QK", 0, 0)], (2, 12): [("QK", 0, 1)],
         (3, 4): [("QK", 1, 0)], (3, 12): [("QK", 1, 1)], (4, 2): [("PO", 0), ("PO", 1)], (4, 8): [("ST", 0, 1)],
         (5, 4): [("ST", 1, 1)], (5, 8): [("HR",)], (7, 2): [("ST", 2, 1)]}

AFTER = {(0, -8): [("AT", 0)], (0, -7): [("AT", 1)], (0, -6): [("WO", 0)], (0, -5): [("WO", 1)],
         (0, -4): [("LNS", 0)], (0, -2): [("LNN", 0)], (0, 8): [("XT", 0)], (0, 9): [("XT", 1)],
         (0, 11): [("GL", 0)], (0, 12): [("GL", 1)], (0, 13): [("GA",)], (0, 15): [("GB",)],
         (1, 0): [("GC",)], (1, 3): [("CT", 0)], (1, 4): [("CT", 1)], (1, 5): [("B2", 0)], (1, 6): [("B2", 1)],
         (7, -6): [("ADD",)], (7, -4): [("LNS", 1)], (7, -1): [("LNN", 1)], (7, 6): [("LNS", 2)],
         (7, 9): [("LNN", 2)]}

EXPERTS = {1: (0,), 2: (1,), 3: (2, 3), 4: (4,), 5: (5, 6), 6: (7,)}


def order(attn, moe):
    if moe:
        yield "XR",
    if not attn:
        for name in ("AT", "WO"):
            for t in range(2):
                yield name, t
        yield "LNS", 0
        yield "LNN", 0
        for name in ("XT", "GL"):
            for t in range(2):
                yield name, t
        yield "GA",
        for e in range(E):
            for j in range(2 * FC):
                yield "HID", e, j
            if e == 0:
                yield "GB",
                yield "GC",
                for name in ("CT", "B2"):
                    for t in range(2):
                        yield name, t
            for q in range(QT):
                yield "Y", e, q
        yield "ADD",
        for k in (1, 2):
            yield "LNS", k
            yield "LNN", k
        yield "OUT",
        return
    yield "V", 0
    yield "V", 1
    if moe:
        yield "ST", 3, 0
    for hp in range(HP):
        experts = EXPERTS.get(hp, ()) if moe else ()
        for j in range(8):
            if experts:
                yield "HID", experts[0], j
            yield "A", 2 * hp + 2, j
            if moe:
                yield from AFTER.get((hp, j - 8), ())
        for i in range(2 * QT):
            if len(experts) == 2 and i == QT:
                for j in range(2 * FC):
                    yield "HID", experts[1], j
            yield "B", hp, i
            if i < QT:
                yield "A", 2 * hp + 3, i
            if experts and (i >= QT or len(experts) == 2):
                yield "Y", experts[-1 if i >= QT else 0], i % QT
            if i == 0 and hp:
                yield "OC", hp - 1
            if i == 2 and hp:
                yield "OT", hp - 1
            if i == QT:
                yield "MN", hp + 1
            if i == QT + 1:
                yield "MT", hp + 1
            yield from AHEAD.get((hp, i), ())
            if moe:
                yield from AFTER.get((hp, i), ())
    yield "BF",
    yield "OC", HP - 1
    yield "OT", HP - 1
    if moe:
        yield "OUT",


PROLOGUE = ([("PRE",), ("HQ",), ("HT", 0), ("HT", 1), ("QK", 0, 0), ("QK", 0, 1), ("QK", 1, 0), ("QK", 1, 1),
             ("PO", 0), ("PO", 1)] + [("ST", g, 1) for g in range(4)]
            + [("A", h, j) for h in range(2) for j in range(QT)] + [("MN", 0), ("MT", 0)])
ST_DMAS = 2 * (len(Q_PARTS) + len(K_PARTS)) + 2


def uses(steps):
    return sum(BANK_USES.get(x[0], 0) for x in steps)


class Fill:

    def __init__(self, base, n):
        self.base, self.n = base, n

    def slot(self, k=0):
        return (self.n + k) % 2

    def turn(self, k=0):
        return self.base + (self.n + k) // 2


def passes(engine, steps_of):
    def one(steps, s, base, n):
        for x in steps:
            steps_of(x, s, Fill(base, n))
            n += BANK_USES.get(x[0], 0)

    first, both = uses(PROLOGUE), uses(order(True, True))
    assert both % 2 == 0
    one(PROLOGUE, -1, 0, 0)
    one(order(True, False), 0, 0, first)
    first += uses(order(True, False))
    with engine.Fori(1, B) as s:
        one(order(True, True), s, (s - 1) * (both // 2), first)
    one(order(False, True), B, (B - 1) * (both // 2), first)


def second_layer(nc, io, w, ident, eps, x1_dram, h_dram, parts_dram):
    ctx = ExitStack()
    with ctx:
        def sb(name, shape, dt=F32):
            return ctx.enter_context(nc.sbuf_tensor(name, shape, dt))

        def ps(name, shape, dt=F32):
            return ctx.enter_context(nc.psum_tensor(name, shape, dt))

        def sem(name):
            return ctx.enter_context(nc.semaphore(name))

        ks = sb("ks", [P, H, T], BF16)
        qs = sb("qs", [P, HP, T], BF16)
        zeros = sb("zeros", [2, 2, T], BF16)
        ones = sb("ones", [2, T], BF16)
        wp = sb("wp", [P, 2, D])
        cols = sb("cols", [P, 4 + E * FC])
        hq = sb("hq", [P, QT, D])
        ht = sb("ht", [P, T])
        rot = sb("rot", [P, 2, HALF])
        full = sb("full", [P, HALF])
        rest = sb("rest", [P, HALF])
        parts = sb("parts", [P, 2, 3, T], BF16)
        va = sb("va", [P, QT, H, VH])
        nm_half = sb("nm_half", [P, 2, 2, 2, QT])
        nm = sb("nm", [P, 2, 2, QT])
        m_hi, m_lo = sb("m_hi", [2 * QT, 2, P], BF16), sb("m_lo", [2 * QT, 2, P], BF16)
        pt = sb("pt", [P, 4, T])
        o_sb = sb("o_sb", [P, 512])
        rcp = sb("rcp", [P, 4, 4])
        ao = sb("ao", [P, QT, D])
        aot = sb("aot", [P, T])
        hr, xr, xa, acc = sb("hr", [P, QT, D]), sb("xr", [P, QT, D]), sb("xa", [P, QT, D]), sb("acc", [P, QT, D])
        xt = aot
        hid = sb("hid", [P, FC, T])
        stats, mv = sb("stats3", [P, QT, 6]), sb("mv3", [P, QT, 2])
        std, rstd = sb("std3", [P, QT]), sb("rstd3", [P, QT])
        logit, prob, top = sb("logit", [P, QT, E]), sb("prob", [P, QT, E]), sb("top", [P, QT, 8])
        mx, zs, idx, idx_f = sb("mx", [P, QT]), sb("zs", [P, QT]), sb("idx", [P, QT, 8], U32), sb("idx_f", [P, QT, 8])
        pick = sb("pick", [P, 2, QT, E])
        comb, ct = sb("comb", [P, QT, E]), sb("ct", [E, T])
        expert = sb("expert", [P, E])

        s1 = [ps(f"s1{i}", [P, HALF]) for i in range(2)]
        s2 = [ps(f"s2{i}", [P, HALF]) for i in range(3)]
        p_o = ps("p_o", [P, 512])
        banks = [ps(f"bank{i}", [P, 512]) for i in range(2)]

        s_pace, s_pace_act = sem("s_pace2"), sem("s_pace_act2")
        s_zero, s_ones, s_setup, s_iota = sem("s_zero"), sem("s_ones"), sem("s_setup"), sem("s_iota")
        s_bank = [sem(f"s_bank{i}") for i in range(2)]
        s_free = [sem(f"s_free{i}") for i in range(2)]
        s_hq, s_r, s_sp, s_split = sem("s_hq"), sem("s_r"), sem("s_sp"), sem("s_split")
        s_po = [sem(f"s_po{x}") for x in range(2)]
        s_st = [sem(f"s_st{g}") for g in range(4)]
        s_s1, s_max, s_nm = sem("s_s1"), sem("s_max"), sem("s_nm")
        s_mr = [sem(f"s_mr{g}") for g in range(2)]
        s_s2, s_exp, s_pv, s_oc, s_rc = sem("s_s2"), sem("s_exp"), sem("s_pv"), sem("s_oc"), sem("s_rc")
        s_mh = sem("s_mh")
        s_hr, s_hrb, s_xr = sem("s_hr"), sem("s_hrb"), sem("s_xr")
        l_stats, l_var, l_std, l_rstd, l_norm, l_scale, l_affine = (
            sem(n) for n in ("l_stats", "l_var", "l_std", "l_rstd", "l_norm", "l_scale", "l_affine"))
        s_gate, s_gexp, s_comb, s_sum, s_added, s_fin, s_out = (
            sem(n) for n in ("s_gate", "s_gexp", "s_comb", "s_sum", "s_added", "s_fin", "s_out"))
        block = ctx.enter_context(nc.Block())

        def tokens(t):
            return slice(HALF * t, HALF * t + HALF)

        def tile(q):
            return slice(P * q, P * q + P)

        def wide(t, n=QT):
            return t[:, :].unsqueeze(1).broadcast_to((P, n, t.shape[1]))

        def which(s):
            known = isinstance(s, int)
            return (0 if known and s < 0 else s), known and s < 0, known and s == 0

        def norm_index(s, k):
            return 3 * (s - 1) + k

        def filled(engine, fill, k=0):
            engine.wait_ge(s_bank[fill.slot(k)], fill.turn(k) + 1)

        def taken(engine, fill, k=0):
            engine.wait_ge(s_free[fill.slot(k)], fill.turn(k) + 1)

        def drained(engine, fill):
            taken(engine, fill, -2)
            taken(engine, fill, -1)

        def last_in_slot(m):
            return m - 3 if m >= 3 else max(x for x in range(256) if x % 3 == m) - 256

        @block.sync
        def _(sp):
            sp.wait_ge(s_zero, 2)
            sp.wait_ge(s_setup, 1)
            for par in range(2):
                r = 64 * par + M_ROW
                sp.dma_start(ks[r:r + 2, par::2, :],
                             ones[:, :].unsqueeze(1).broadcast_to((2, HP, T))).then_inc(s_ones, 16)

            def wait(semaphore, n):
                sp.wait_ge(semaphore, n)
                sp.sem_inc(s_pace, 1)

            def step(x, s, fill):
                name, b, starts, zeroth = x[0], *which(s)
                bank, free = banks[fill.slot()], s_free[fill.slot()]
                if name == "HQ":
                    sp.dma_start(hq[:, :, :], h_dram[s + 1].rearrange("(q p) d -> p q d", p=P)).then_inc(s_hq, 16)
                elif name == "HR":
                    sp.dma_start(hr[:, :, :], h_dram[s].rearrange("(q p) d -> p q d", p=P)).then_inc(s_hr, 16)
                elif name == "XR":
                    sp.dma_start(xr[:, :, :], x1_dram[s - 1].rearrange("(q p) d -> p q d", p=P)).then_inc(s_xr, 16)
                elif name == "PO":
                    wait(s_sp, 4 * (s + 1) + 2 * x[1] + 2)
                    if not starts:
                        for g in range(4):
                            wait(s_st[g], 16 * ST_DMAS * (s + 1))
                    sp.dma_start(parts_dram[x[1]].rearrange("n p t -> p n t"), parts[:, x[1], :, :])\
                        .then_inc(s_po[x[1]], 16)
                elif name == "ST":
                    g, ahead = x[1], x[2]
                    nb = s + ahead
                    for k in range(2):
                        wait(s_po[k], 16 * (nb + 1))
                    if not starts:
                        wait(s_pv, 128 * (nb - 1) + 32 * (g + 1))
                    else:
                        wait(s_ones, 32)
                    for par in range(2):
                        for k, (stack, chosen) in enumerate(((qs, Q_PARTS), (ks, K_PARTS))):
                            for n, part in enumerate(chosen):
                                rows = slice(64 * par + HD * n, 64 * par + HD * n + HD)
                                src = parts_dram[k, part].rearrange("(c r e) t -> r e c t", r=2, e=HD)
                                dst = (stack[rows, 2 * g:2 * g + 2, :] if k == 0
                                       else stack[rows, 4 * g + par:4 * g + 4:2, :])
                                sp.dma_start(dst, src[par, :, 2 * g:2 * g + 2, :]).then_inc(s_st[g], 16)
                        r = 64 * par + M_ROW
                        sp.dma_start(qs[r:r + 2, 2 * g:2 * g + 2, :], zeros[:, :, :]).then_inc(s_st[g], 16)
                elif name == "MT":
                    hp = x[1]
                    wait(s_free[fill.slot()], fill.turn() + 1)
                    for k, rows in enumerate((m_hi, m_lo)):
                        for par in range(2):
                            r = 64 * par + M_ROW + k
                            sp.dma_start(qs[r:r + 1, hp % HP, :].rearrange("a (q p) -> a q p", p=P),
                                         rows[QT * par:QT * par + QT, hp % 2, :]).then_inc(s_mr[hp % 2], 16)
                elif name == "OUT":
                    wait(s_fin, s)
                    sp.dma_start(io["out"][s - 1].rearrange("(q p) d -> p q d", p=P), xa[:, :, :]).then_inc(s_out, 16)
                    wait(s_out, 16 * s)

            passes(sp, step)
            for g in range(3):
                sp.wait_ge(s_st[g], 16 * ST_DMAS * (B + 1))
            sp.wait_ge(s_mr[0], 64 * (4 * B + 1))

        @block.gpsimd
        def _(pool):
            nc.gpsimd.memset(ks[:, :, :], 0.0).then_inc(s_zero, 1)
            nc.gpsimd.memset(qs[:, :, :], 0.0).then_inc(s_zero, 1)
            nc.gpsimd.iota(expert[:, :], [[1, E]], base=0, channel_multiplier=0,
                           allow_small_or_imprecise_dtypes=True).then_inc(s_iota, 1)

            def step(x, s, fill):
                name, b, starts, zeroth = x[0], *which(s)
                bank, free = banks[fill.slot()], s_free[fill.slot()]
                if name == "QK":
                    k, t = x[1], x[2]
                    n = 4 * (s + 1) + 2 * k + t
                    out = [parts[:, k, i, tokens(t)] for i in range(3)]
                    if not starts:
                        pool.wait_ge(s_po[k], 16 * (s + 1))
                    taken(pool, fill)
                    pool.sem_inc(s_pace, 1)
                    taken(pool, fill, 1)
                    pool.sem_inc(s_pace, 1)
                    nc.gpsimd.tensor_tensor(full[:, :], rot[:, 0, :], rot[:, 1, :], ALU.add).then_inc(s_r, 1)
                    pool.wait_ge(s_r, n + 1)
                    pool.sem_inc(s_pace, 1)
                    nc.gpsimd.tensor_copy(out[0], full[:, :]).then_inc(s_split, 1)
                    pool.wait_ge(s_split, 3 * n + 1)
                    nc.gpsimd.tensor_tensor(rest[:, :], full[:, :], out[0], ALU.subtract).then_inc(s_split, 1)
                    pool.wait_ge(s_split, 3 * n + 2)
                    pool.sem_inc(s_pace, 1)
                    nc.gpsimd.tensor_copy(out[1], rest[:, :]).then_inc(s_split, 1)
                    pool.wait_ge(s_split, 3 * n + 3)
                    nc.gpsimd.tensor_tensor(out[2], rest[:, :], out[1], ALU.subtract).then_inc(s_sp, 1)
                elif name == "HR":
                    pool.wait_ge(s_hr, 16 * (s + 1))
                    nc.gpsimd.tensor_tensor(hr[:, :, :], hr[:, :, :], wide(w["bo"]), ALU.add).then_inc(s_hrb, 1)
                elif name == "LNN" and x[1] < 2:
                    gain, bias = ((w["g1"], w["be1"]), (w["g2"], w["be2"]))[x[1]]
                    a = 2 * (s - 1) + x[1]
                    pool.wait_ge(l_norm, QT * (norm_index(s, x[1]) + 1))
                    nc.gpsimd.tensor_tensor(xa[:, :, :], xa[:, :, :], wide(gain), ALU.mult).then_inc(l_scale, 1)
                    pool.wait_ge(l_scale, a + 1)
                    nc.gpsimd.tensor_tensor(xa[:, :, :], xa[:, :, :], wide(bias), ALU.add).then_inc(l_affine, 1)
                elif name == "LNN":
                    pool.wait_ge(s_xr, 16 * s)
                    pool.wait_ge(l_norm, QT * (norm_index(s, 2) + 1))
                    nc.gpsimd.tensor_tensor(xa[:, :, :], xa[:, :, :], xr[:, :, :], ALU.add).then_inc(s_fin, 1)

            passes(pool, step)

        @block.scalar
        def _(act):
            def step(x, s, fill):
                name, b, starts, zeroth = x[0], *which(s)
                bank, free = banks[fill.slot()], s_free[fill.slot()]
                if name == "PRE":
                    filled(act, fill)
                    nc.scalar.copy(cols[:, :], bank[:, 0:4 + E * FC]).then_inc(free, 1)
                elif name == "B":
                    hp, i = x[1], x[2]
                    n = 128 * s + 16 * hp + i
                    if not (zeroth and n < 4):
                        act.wait_ge(s_pv, n - 3)
                        act.sem_inc(s_pace_act, 1)
                    for t in range(2):
                        act.wait_ge(s_s2, 2 * n + t + 1)
                        nc.scalar.activation(pt[:, i % 4, tokens(t)], s2[(32 * hp + 2 * i + t) % 3][:, :], ACT.Exp,
                                             scale=SCALE).then_inc(s_exp, 1)
                elif name == "HID":
                    e, f, t = x[1], x[2] % FC, x[2] // FC
                    filled(act, fill)
                    nc.scalar.activation(hid[:, f, tokens(t)], bank[:, :], ACT.Gelu,
                                         bias=cols[:, 4 + FC * e + f:5 + FC * e + f]).then_inc(free, 1)
                elif name in ("HT", "AT", "XT"):
                    filled(act, fill)
                    to = {"HT": ht, "AT": aot, "XT": xt}[name]
                    nc.scalar.copy(to[:, tokens(x[1])], bank[:, :]).then_inc(free, 1)
                elif name == "CT":
                    filled(act, fill)
                    nc.scalar.copy(ct[:, tokens(x[1])], bank[0:E, :]).then_inc(free, 1)
                elif name == "B2":
                    filled(act, fill)
                    nc.scalar.copy(acc[:, 4 * x[1]:4 * x[1] + 4, :],
                                   bank[:, :].rearrange("p (q d) -> p q d", q=4)).then_inc(free, 1)
                elif name == "LNS":
                    act.wait_ge(l_var, QT * (norm_index(s, x[1]) + 1))
                    nc.scalar.activation(std[:, :], mv[:, :, 1], ACT.Sqrt, bias=eps[:, :]).then_inc(l_std, 1)
                elif name == "GA":
                    act.wait_ge(s_gate, 8 * (s - 1) + 2)
                    nc.scalar.activation(prob[:, :, :], logit[:, :, :], ACT.Exp).then_inc(s_gexp, 1)

            passes(act, step)

        @block.vector
        def _(dve):
            nc.vector.memset(ones[:, :], 1.0).then_inc(s_mh, 1)
            nc.vector.memset(zeros[:, :, :], 0.0).then_inc(s_mh, 1)
            dve.wait_ge(s_mh, 2)
            nc.vector.memset(va[:, :, :, HD:], 1.0).then_inc(s_setup, 1)
            nc.vector.memset(p_o[:, :], 0.0).then_inc(s_setup, 1)
            for k, n in enumerate(("Wq", "Wk")):
                a = w[n][:, :].rearrange("p (h t e) -> p h t e", h=H, t=2)
                b = wp[:, k, :].rearrange("p (h t e) -> p h t e", h=H, t=2)
                for t in range(2):
                    nc.vector.tensor_copy(b[:, :, t, :], a[:, :, 1 - t, :]).then_inc(s_setup, 1)

            def statistics(n):
                for q in range(QT):
                    nc.vector.bn_stats(stats[:, q, :], xa[:, q, :]).then_inc(l_stats, 1)
                for q in range(QT):
                    dve.wait_ge(l_stats, QT * n + q + 1)
                    dve.sem_inc(s_pace, 1)
                    nc.vector.bn_aggr(mv[:, q, :], stats[:, q, :]).then_inc(l_var, 1)

            def normed(n):
                dve.wait_ge(l_std, n + 1)
                nc.vector.reciprocal(rstd[:, :], std[:, :]).then_inc(l_rstd, 1)
                dve.wait_ge(l_rstd, n + 1)
                for q in range(QT):
                    nc.vector.tensor_scalar(xa[:, q, :], xa[:, q, :], mv[:, q, 0:1], rstd[:, q:q + 1], ALU.subtract,
                                            ALU.mult).then_inc(l_norm, 1)

            link = [0]
            at = {}

            def chain(s, ins):
                link[0] = link[0] % 8 + 1
                ins.then_inc(s_gate, 1)
                dve.wait_ge(s_gate, 8 * (s - 1) + link[0])

            def per_tile(t):
                return t.unsqueeze(2).broadcast_to((P, QT, E))

            def step(x, s, fill):
                name, b, starts, zeroth = x[0], *which(s)
                bank, free = banks[fill.slot()], s_free[fill.slot()]
                at[x] = fill
                if name == "A":
                    head, q = x[1], x[2]
                    n = 8 * (16 * b + head) + q
                    for t in range(2):
                        dve.wait_ge(s_s1, 2 * n + t + 1)
                        nc.vector.reduce_max(nm_half[:, t, head // 2 % 2, head % 2, q:q + 1], s1[t][:, :], AX.X,
                                             negate=True).then_inc(s_max, 1)
                elif name == "MN":
                    hp = x[1]
                    dve.wait_ge(s_max, 32 * (8 * b + hp + 1))
                    nc.vector.tensor_tensor(nm[:, hp % 2, :, :], nm_half[:, 0, hp % 2, :, :], nm_half[:, 1, hp % 2, :, :],
                                            ALU.min).then_inc(s_nm, 1)
                elif name == "MT":
                    hp = x[1]
                    filled(dve, fill)
                    if not (starts or (zeroth and hp < 2)):
                        dve.wait_ge(s_mr[hp % 2], 64 * (4 * s + hp // 2))
                    nc.vector.tensor_copy(m_hi[:, hp % 2, :], bank[0:2 * QT, 0:P]).then_inc(s_mh, 1)
                    dve.wait_ge(s_mh, 8 * b + hp + 3)
                    nc.vector.tensor_tensor(m_lo[:, hp % 2, :], bank[0:2 * QT, 0:P], m_hi[:, hp % 2, :],
                                            ALU.subtract).then_inc(free, 1)
                elif name == "Y":
                    e, q = x[1], x[2]
                    filled(dve, fill)
                    nc.vector.scalar_tensor_tensor(acc[:, q, :], bank[:, 0:D], comb[:, q, e:e + 1], acc[:, q, :],
                                                   ALU.mult, ALU.add).then_inc(free, 1)
                elif name == "OC":
                    u = 8 * s + x[1]
                    dve.wait_ge(s_pv, 16 * (u + 1))
                    nc.vector.tensor_copy(o_sb[:, :], p_o[:, :]).then_inc(s_oc, 1)
                elif name == "OT":
                    hp = x[1]
                    u = 8 * s + hp
                    filled(dve, fill)
                    o = bank[:, :].rearrange("p (t j c) -> p t j c", t=4, j=4)
                    nc.vector.reciprocal(rcp[:, :, :], o[:, :, :, HD]).then_inc(s_rc, 1)
                    dve.wait_ge(s_rc, 2 * u + 1)
                    for half in range(2):
                        ins = nc.vector.tensor_tensor(
                            ao[:, 4 * half:4 * half + 4, 2 * HD * hp:2 * HD * hp + 2 * HD]
                            .rearrange("p t (r e) -> p t r e", r=2),
                            o[:, :, half::2, 0:HD],
                            rcp[:, :, half::2].unsqueeze(3).broadcast_to((P, 4, 2, HD)), ALU.mult)
                        ins.then_inc(free if half else s_rc, 1)
                elif name == "V":
                    t = x[1]
                    filled(dve, fill)
                    nc.vector.tensor_tensor(
                        va[:, 4 * t:4 * t + 4, :, 0:HD], bank[:, :].rearrange("p (q h e) -> p q h e", q=4, h=H),
                        w["bv"][:, :].rearrange("p (h e) -> p h e", h=H).unsqueeze(1).broadcast_to((P, 4, H, HD)),
                        ALU.add).then_inc(free, 1)
                elif name == "QK":
                    k, t = x[1], x[2]
                    if not (starts and k == 0 and t == 0):
                        dve.wait_ge(s_sp, 4 * (s + 1) + 2 * k + t)
                    for i, table in enumerate((w["cos"], w["sin"])):
                        filled(dve, fill, i)
                        nc.vector.scalar_tensor_tensor(rot[:, i, :], banks[fill.slot(i)][:, :], cols[:, 2 * k + i:2 * k + i + 1],
                                                       table[:, tokens(t)], ALU.add, ALU.mult)\
                            .then_inc(s_free[fill.slot(i)], 1)
                elif name == "WO":
                    t = x[1]
                    filled(dve, fill)
                    dve.wait_ge(s_hrb, s)
                    dve.wait_ge(s_xr, 16 * s)
                    nc.vector.tensor_tensor(xa[:, 4 * t:4 * t + 4, :], bank[:, :].rearrange("p (q d) -> p q d", q=4),
                                            hr[:, 4 * t:4 * t + 4, :], ALU.add).then_inc(free, 1)
                elif name == "LNS":
                    k = x[1]
                    if k == 0:
                        for t in range(2):
                            taken(dve, at["WO", t])
                    elif k == 1:
                        dve.wait_ge(s_added, s)
                    else:
                        dve.wait_ge(l_affine, 2 * s)
                    statistics(norm_index(s, k))
                elif name == "LNN":
                    normed(norm_index(s, x[1]))
                elif name == "ADD":
                    for q in (QT - 2, QT - 1):
                        taken(dve, at["Y", E - 1, q])
                    nc.vector.tensor_tensor(xa[:, :, :], xa[:, :, :], acc[:, :, :], ALU.add).then_inc(s_added, 1)
                elif name == "GL":
                    filled(dve, fill)
                    nc.vector.tensor_tensor(logit[:, 4 * x[1]:4 * x[1] + 4, :],
                                            bank[:, 0:4 * E].rearrange("p (q e) -> p q e", q=4),
                                            wide(w["bg"], 4), ALU.add).then_inc(free, 1)
                elif name == "GA":
                    for t in range(2):
                        taken(dve, at["GL", t])
                    chain(s, nc.vector.reduce_max(mx[:, :], logit[:, :, :], AX.X))
                    chain(s, nc.vector.tensor_tensor(logit[:, :, :], logit[:, :, :], per_tile(mx[:, :]), ALU.subtract))
                elif name == "GB":
                    dve.wait_ge(s_gexp, s)
                    chain(s, nc.vector.reduce_sum(zs[:, :], prob[:, :, :], AX.X))
                    chain(s, nc.vector.reciprocal(mx[:, :], zs[:, :]))
                    chain(s, nc.vector.tensor_tensor(prob[:, :, :], prob[:, :, :], per_tile(mx[:, :]), ALU.mult))
                    dve.sem_inc(s_pace, 1)
                    for q in range(QT):
                        nc.vector.max(top[:, q, :], prob[:, q, :]).then_inc(s_sum, 1)
                elif name == "GC":
                    for q in range(QT):
                        dve.wait_ge(s_sum, 16 * (s - 1) + q + 1)
                        dve.sem_inc(s_pace, 1)
                        nc.vector.max_index(idx[:, q, :], top[:, q, :], prob[:, q, :]).then_inc(s_sum, 1)
                    dve.wait_ge(s_sum, 16 * s)
                    chain(s, nc.vector.tensor_copy(idx_f[:, :, :], idx[:, :, :]))
                    chain(s, nc.vector.tensor_tensor(zs[:, :], top[:, :, 0], top[:, :, 1], ALU.add))
                    chain(s, nc.vector.reciprocal(mx[:, :], zs[:, :]))
                    for k in range(2):
                        nc.vector.tensor_tensor(pick[:, k, :, :], wide(expert), per_tile(idx_f[:, :, k]),
                                                ALU.is_equal).then_inc(s_comb, 1)
                        nc.vector.tensor_tensor(top[:, :, k], top[:, :, k], mx[:, :], ALU.mult).then_inc(s_comb, 1)
                    dve.wait_ge(s_comb, 7 * (s - 1) + 4)
                    for k in range(2):
                        nc.vector.tensor_tensor(pick[:, k, :, :], pick[:, k, :, :], per_tile(top[:, :, k]),
                                                ALU.mult).then_inc(s_comb, 1)
                    dve.wait_ge(s_comb, 7 * (s - 1) + 6)
                    nc.vector.tensor_tensor(comb[:, :, :], pick[:, 0, :, :], pick[:, 1, :, :], ALU.add)\
                        .then_inc(s_comb, 1)

            dve.wait_ge(s_iota, 1)
            passes(dve, step)

        @block.tensor
        def _(pe):
            at = {}
            late = [None]

            def weigh_values(s):
                if late[0] is None:
                    return
                hp, i = late[0]
                late[0] = None
                n = 128 * s + 16 * hp + i
                par, kt = i // QT, i % QT
                pe.wait_ge(s_exp, 2 * n + 2)
                if i == 0 and not (which(s)[2] and hp == 0):
                    pe.wait_ge(s_oc, 8 * s + hp)
                for t in range(2):
                    j = 32 * (2 * par + t)
                    ins = nc.tensor.matmul(p_o[j:j + VH, :], va[:, kt, 2 * hp + par, :], pt[:, i % 4, tokens(t)],
                                           start=kt == 0, stop=kt == QT - 1)
                ins.then_inc(s_pv, 1)

            def step(x, s, fill):
                name, b, starts, zeroth = x[0], *which(s)
                bank, full_bank = banks[fill.slot()], s_bank[fill.slot()]
                at[x] = fill
                if name in BANK_USES and fill.n >= 2:
                    taken(pe, fill, -2)
                if name == "PRE":
                    pe.wait_ge(s_setup, 6)
                    for k in range(4):
                        nc.tensor.matmul(bank[:, k:k + 1], w["bqk"][0:1, k, :], ident[0:1, 0:1], start=True, stop=True)
                    nc.tensor.transpose(bank[:, 4:4 + E * FC], w["b1"][:, :], ident[0:E * FC, 0:E * FC])\
                        .then_inc(full_bank, 1)
                elif name == "A":
                    head, q = x[1], x[2]
                    n = 8 * (16 * b + head) + q
                    if q == 0 and head % 4 == 0:
                        pe.wait_ge(s_st[head % H // 4], 16 * ST_DMAS * (b + 1 + head // H))
                    for t in range(2):
                        if not (starts and n == 0):
                            pe.wait_ge(s_max, 2 * n + t - 1)
                        nc.tensor.matmul(s1[t][:, :], qs[:, head % H // 2, tile(q)],
                                         ks[:, head % H, tokens(t)], start=True, stop=True).then_inc(s_s1, 1)
                elif name == "B":
                    hp, i = x[1], x[2]
                    head, kt = 2 * hp + i // QT, i % QT
                    n = 128 * s + 16 * hp + i
                    if i == 0:
                        pe.wait_ge(s_mr[hp % 2], 64 * (4 * s + hp // 2 + 1))
                    for t in range(2):
                        m = 32 * hp + 2 * i + t
                        if not (zeroth and m < 3):
                            pe.wait_ge(s_exp, 256 * s + last_in_slot(m) + 1)
                        nc.tensor.matmul(s2[m % 3][:, :], ks[:, head, tile(kt)], qs[:, hp, tokens(t)], start=True,
                                         stop=True).then_inc(s_s2, 1)
                    if hp == 0 and i == 1:
                        taken(pe, at["V", 0])
                        taken(pe, at["V", 1])
                    weigh_values(s)
                    late[0] = (hp, i)
                elif name == "BF":
                    weigh_values(s)
                elif name == "MT":
                    hp = x[1]
                    pe.wait_ge(s_nm, 8 * b + hp + 1)
                    nc.tensor.transpose(bank[0:2 * QT, 0:P], nm[:, hp % 2, :, :].rearrange("p r q -> p (r q)"),
                                        ident[:, :]).then_inc(full_bank, 1)
                elif name == "OT":
                    pe.wait_ge(s_oc, 8 * s + x[1] + 1)
                    for t in range(4):
                        ins = nc.tensor.transpose(bank[:, tile(t)], o_sb[:, tile(t)], ident[:, :])
                    ins.then_inc(full_bank, 1)
                elif name == "HID":
                    e, f, t = x[1], x[2] % FC, x[2] // FC
                    nc.tensor.matmul(bank[:, :], w["W1"][:, e, tile(f)], xt[:, tokens(t)], start=True, stop=True)\
                        .then_inc(full_bank, 1)
                elif name == "Y":
                    e, q = x[1], x[2]
                    if q == 0:
                        taken(pe, at["HID", e, 2 * FC - 1])
                    for f in range(FC):
                        ins = nc.tensor.matmul(bank[:, 0:D], hid[:, f, tile(q)], w["W2"][:, e, f, :], start=f == 0,
                                               stop=f == FC - 1)
                    ins.then_inc(full_bank, 1)
                elif name in ("HT", "AT", "XT"):
                    if name == "HT":
                        pe.wait_ge(s_hq, 16 * (s + 2))
                    if name == "XT":
                        pe.wait_ge(l_affine, 2 * (s - 1) + 1)
                    if x == ("AT", 0):
                        drained(pe, fill)
                    src = {"HT": hq, "AT": ao, "XT": xa}[name]
                    for q in range(4):
                        ins = nc.tensor.transpose(bank[:, tile(q)], src[:, 4 * x[1] + q, :], ident[:, :])
                    ins.then_inc(full_bank, 1)
                elif name == "QK":
                    k, t = x[1], x[2]
                    taken(pe, at["HT", t])
                    for i, wt in enumerate((w[("Wq", "Wk")[k]][:, :], wp[:, k, :])):
                        if i:
                            taken(pe, fill, -1)
                        nc.tensor.matmul(banks[fill.slot(i)][:, :], wt, ht[:, tokens(t)], start=True, stop=True)\
                            .then_inc(s_bank[fill.slot(i)], 1)
                elif name == "V":
                    for q in range(4):
                        ins = nc.tensor.matmul(bank[:, tile(q)], ht[:, tile(4 * x[1] + q)], w["Wv"][:, :], start=True,
                                               stop=True)
                    ins.then_inc(full_bank, 1)
                elif name == "WO":
                    taken(pe, at["AT", x[1]])
                    for q in range(4):
                        ins = nc.tensor.matmul(bank[:, tile(q)], aot[:, tile(4 * x[1] + q)], w["Wo"][:, :], start=True,
                                               stop=True)
                    ins.then_inc(full_bank, 1)
                elif name == "GL":
                    taken(pe, at["XT", x[1]])
                    for q in range(4):
                        ins = nc.tensor.matmul(bank[:, E * q:E * q + E], xt[:, tile(4 * x[1] + q)], w["Wg"][:, :],
                                               start=True, stop=True)
                    ins.then_inc(full_bank, 1)
                elif name == "CT":
                    pe.wait_ge(s_comb, 7 * s)
                    for q in range(4):
                        ins = nc.tensor.transpose(bank[0:E, tile(q)], comb[:, 4 * x[1] + q, :], ident[:, :])
                    ins.then_inc(full_bank, 1)
                elif name == "B2":
                    taken(pe, at["CT", x[1]])
                    for q in range(4):
                        ins = nc.tensor.matmul(bank[:, tile(q)], ct[:, tile(4 * x[1] + q)], w["b2"][:, :], start=True,
                                               stop=True)
                    ins.then_inc(full_bank, 1)

            passes(pe, step)


def program(nc, io):
    x1_dram = nc.dram_tensor("x1_dram", (B, T, D), F32).ap()
    h_dram = nc.dram_tensor("h_dram", (B + 1, T, D), F32).ap()
    parts_dram = nc.dram_tensor("parts_dram", (2, 3, P, T), BF16).ap()
    ctx = ExitStack()
    with ctx:
        ident = ctx.enter_context(nc.sbuf_tensor("ident", [P, P], F32))
        eps = ctx.enter_context(nc.sbuf_tensor("eps", [P, 1], F32))
        w = constants(ctx, nc)
        s_weights = ctx.enter_context(nc.semaphore("s_weights"))
        with ExitStack() as first:
            xt = {n: first.enter_context(nc.sbuf_tensor(n, [P, k, D], F32))
                  for n, k in (("x", NK), ("f", NK), ("v_all", NK + 1))}
            xt["ident"], xt["eps"] = ident, eps
            window_attention(nc, io, xt, w, s_weights)
            middle(nc, io, xt, x1_dram, h_dram)
        second_layer(nc, io, w, ident, eps, x1_dram, h_dram, parts_dram)


_INS = {"x": "L0_attn_feature", "wq_w": "L0_attn_wq_w", "wq_b": "L0_attn_wq_b", "w2_w": "L0_attn_w2_w",
        "w2_b": "L0_attn_w2_b", "ln_g": "L0_attn_ln_g", "ln_b": "L0_attn_ln_b"}
_INS.update({n: f"L0_ffn_{n}" for n in ("Wq", "bq", "Wk", "bk", "Wv", "bv", "Wo", "bo", "Wg", "bg", "W1", "b1", "W2",
                                        "b2", "g1", "be1", "g2", "be2")})


def rotation_tables():
    inv_freq = (1.0 / 10000.0 ** (np.arange(0, HD, 2, dtype=np.float32) / np.float32(HD))).astype(np.float32)
    angle = np.arange(T, dtype=np.float32)[None, :] * inv_freq[:, None]
    sign = np.repeat(np.float32([-1, 1]), HD // 2)[:, None]
    return np.tile(np.cos(angle), (2 * H, 1)), np.tile(sign * np.tile(np.sin(angle), (2, 1)), (H, 1))


def kernel(**inputs):
    import concourse.bacc as bacc
    from concourse.bass_utils import run_bass_kernel_spmd

    nc = bacc.Bacc("TRN2", target_bir_lowering=False, num_devices=1)
    arrays = {name: np.ascontiguousarray(inputs[full]) for name, full in _INS.items()}
    arrays["cos"], arrays["sin"] = rotation_tables()
    io = {name: nc.dram_tensor(f"in_{name}", a.shape, mybir.dt.from_np(a.dtype), kind="ExternalInput").ap()
          for name, a in arrays.items()}
    io["out"] = nc.dram_tensor("out_0", (B, T, D), F32, kind="ExternalOutput").ap()
    program(nc, io)
    ran = run_bass_kernel_spmd(nc, [{f"in_{name}": a for name, a in arrays.items()}], core_ids=[0])
    return ran.results[0]["out_0"]
```

```python
from contextlib import ExitStack

import numpy as np

import concourse.bass as bass
from concourse import mybir

F32 = mybir.dt.float32
BF16 = mybir.dt.bfloat16
U32 = mybir.dt.uint32
ALU = mybir.AluOpType
ACT = mybir.ActivationFunctionType
AX = mybir.AxisListType

P = 128
B, T, D = 4, 1024, 128
WIN = 64
L = 32
NK = T // L
NC = NK - WIN // L
ROW = WIN + 1

H, HD = 16, 8
HP = H // 2
E, FF = 8, 512
FC = FF // P
QT = T // P
HALF = T // 2
VH = HD + 1
SCALE = 1.0 / float(np.sqrt(HD))
CHOSEN = ((0, 0, 1, 0, 1, 2), (0, 1, 0, 2, 1, 0))
PARTS = len(CHOSEN[0])
M_ROW = HD * PARTS
EPS = 1e-5


def window_attention(nc, io, xt, w, stacks, s_weights):
    ctx = ExitStack()
    with ctx:
        def sb(name, shape, dt=F32):
            return ctx.enter_context(nc.sbuf_tensor(name, shape, dt))

        def ps(name, shape, dt=F32):
            return ctx.enter_context(nc.psum_tensor(name, shape, dt))

        def sem(name):
            return ctx.enter_context(nc.semaphore(name))

        f, v_all, x = xt["f"], xt["v_all"], xt["x"]
        ident, eps = xt["ident"], xt["eps"]
        mask = sb("mask", [P, B, L])
        wq = sb("wq", [P, D])
        bq = sb("bq", [P, 1])
        w2 = sb("w2", [P, 1])
        b0 = sb("b0", [P, 1])
        b0_row = sb("b0_row", [P, L])
        zero_row = sb("zero_row", [P, L])
        stats = sb("stats", [P, NK, 6])
        mv = sb("mv", [P, NK, 2])
        std = sb("std", [P, NK])
        rstd = sb("rstd", [P, NK])
        ft = sb("ft", [P, 2, 4 * P])
        qt = sb("qt", [P, NK + 1, P])
        qn = sb("qn", [P, P])
        vt1 = sb("vt1", [P, P])
        vt2 = sb("vt2", [P, P])
        vr = sb("vr", [P, D])
        bdg = sb("bdg", [P, 2, P])
        bdc = sb("bdc", [P, 2, P])
        tab = sb("tab", [P, 3, WIN + L])
        row = sb("row", [P, 2, ROW + 1])
        nmax = sb("nmax", [P, 2])
        ex = sb("ex", [P, 2, ROW])
        z = sb("z", [P, 2])
        rz = sb("rz", [P, 2])
        junk = sb("junk", [P, 4, ROW])
        raw = sb("raw", [P, 3])

        pf = ps("pf", [P, 2, 4 * P])
        pq = ps("pq", [P, 2, 4 * P])
        p_s = ps("p_s", [P, 512])
        p_g = ps("p_g", [P, 512])
        p_v = ps("p_v", [P, 512])
        p_t = ps("p_t", [P, 512])

        s_x = [sem(f"s_x{b}") for b in range(B)]
        s_w = sem("s_w")
        s_const, s_ident, s_mask = sem("s_const"), sem("s_ident"), sem("s_mask")
        s_stats, s_mv, s_std, s_rstd, s_f = sem("s_stats"), sem("s_mv"), sem("s_std"), sem("s_rstd"), sem("s_f")
        s_ft, s_ftc, s_pq, s_qt = sem("s_ft"), sem("s_ftc"), sem("s_pq"), sem("s_qt")
        s_init = sem("s_init")
        s_pace, s_pace_act = sem("s_pace"), sem("s_pace_act")
        s_vt0 = sem("s_vt0")
        s_stacks = sem("s_stacks")
        s_qn = sem("s_qn")
        s_table = sem("s_table")
        s_scores = sem("s_scores")
        s_row, s_max, s_exp, s_rz, s_new, s_coef = (sem("s_row"), sem("s_max"), sem("s_exp"), sem("s_rz"),
                                                   sem("s_new"), sem("s_coef"))
        s_raw, s_raw_score, s_score = sem("s_raw"), sem("s_raw_score"), sem("s_score")
        s_clear = sem("s_clear")
        s_bdc, s_pv, s_vr, s_vall, s_pt, s_vt2, s_vt1, s_g, s_bdg = (
            sem("s_bdc"), sem("s_pv"), sem("s_vr"), sem("s_vall"), sem("s_pt"), sem("s_vt2"), sem("s_vt1"),
            sem("s_g"), sem("s_bdg"))

        block = ctx.enter_context(nc.Block())

        @block.sync
        def _(sp):
            for b in range(B):
                sp.dma_start(x[L * b:L * b + L, :, :],
                             io["x"][b].rearrange("(k j) d -> j k d", j=L)).then_inc(s_x[b], 16)
            sp.dma_start(wq[:, :], io["wq_w"]).then_inc(s_w, 16)
            sp.dma_start(bq[:, :], io["wq_b"].rearrange("(d a) -> d a", a=1)).then_inc(s_w, 16)
            sp.dma_start(w2[:, :], io["w2_w"].rearrange("(d a) -> d a", a=1)).then_inc(s_w, 16)
            sp.dma_start(b0[:, :], io["w2_b"].rearrange("(d a) -> d a", a=1).broadcast_to((P, 1))).then_inc(s_w, 16)
            loaded = load_constants(sp, w, io, s_weights)
            sp.wait_ge(s_stacks, 4)
            for par in range(2):
                r = 64 * par + M_ROW
                sp.dma_start(stacks["ks"][r:r + 2, par::2, :],
                             stacks["ones"][:, :].unsqueeze(1).broadcast_to((2, HP, T))).then_inc(s_weights, 16)
            sp.wait_ge(s_weights, loaded + 32)

        @block.gpsimd
        def _(pool):
            nc.gpsimd.memset(eps[:, :], EPS).then_inc(s_const, 1)
            nc.gpsimd.memset(zero_row[:, :], 0.0).then_inc(s_const, 1)
            nc.gpsimd.memset(ident[:, :], 0.0).then_inc(s_ident, 1)
            pool.wait_ge(s_ident, 1)
            nc.gpsimd.affine_select(out=ident[:, :], in_=ident[:, :], compare_op=ALU.not_equal, fill=1.0, base=0,
                                    pattern=[[-1, P]], channel_multiplier=1).then_inc(s_ident, 1)
            nc.gpsimd.memset(mask[:, :, :], 1.0).then_inc(s_mask, 1)
            pool.wait_ge(s_mask, 1)
            nc.gpsimd.affine_select(out=mask[:, :, :], in_=mask[:, :, :], compare_op=ALU.is_ge, fill=0.0, base=0,
                                    pattern=[[-L, B], [0, L]], channel_multiplier=1).then_inc(s_mask, 1)
            pool.wait_ge(s_mask, 2)
            nc.gpsimd.affine_select(out=mask[:, :, :], in_=mask[:, :, :], compare_op=ALU.is_ge, fill=0.0, base=L - 1,
                                    pattern=[[L, B], [0, L]], channel_multiplier=-1).then_inc(s_mask, 1)
            pool.wait_ge(s_mask, 3)
            pool.wait_ge(s_f, 2)
            nc.gpsimd.tensor_copy(v_all[:, 0, :], f[:, 1, :]).then_inc(s_init, 1)
            nc.gpsimd.tensor_copy(v_all[:, 1, :], f[:, 0, :]).then_inc(s_vall, 1)
            nc.gpsimd.memset(bdc[:, 1, :], 0.0).then_inc(s_init, 1)
            nc.gpsimd.tensor_copy(bdc[:, 0, :], ident[:, :]).then_inc(s_bdc, 1)
            pool.wait_ge(s_qt, 1)
            nc.gpsimd.tensor_copy(qn[:, :], qt[:, 2, :]).then_inc(s_qn, 1)
            for name, value in (("ks", 0.0), ("qs", 0.0), ("zeros", 0.0), ("ones", 1.0)):
                t = stacks[name]
                nc.gpsimd.memset(t[:, :, :] if name != "ones" else t[:, :], value).then_inc(s_stacks, 1)
            with pool.Fori(0, NC) as c:
                pool.wait_ge(s_vr, c + 1)
                pool.sem_inc(s_pace, 1)
                nc.gpsimd.tensor_copy(v_all[:, c + 2, :], vr[:, :]).then_inc(s_vall, 1)
                pool.wait_ge(s_scores, c + 1)
                pool.sem_inc(s_pace, 1)
                nc.gpsimd.tensor_copy(vt2[:, :], vt1[:, :]).then_inc(s_vt2, 1)
                nc.gpsimd.tensor_copy(qn[:, :], qt[:, c + 3, :]).then_inc(s_qn, 1)
                pool.wait_ge(s_coef, L * (c + 1))
                pool.wait_ge(s_pv, c + 1)
                for g in range(2):
                    last = nc.gpsimd.tensor_tensor(
                        bdc[:, g, :].rearrange("p (b j) -> p b j", b=B),
                        tab[:, 1 + g, WIN:].unsqueeze(1).broadcast_to((P, B, L)), mask[:, :, :], ALU.mult)
                last.then_inc(s_bdc, 1)

        @block.scalar
        def _(act):
            act.wait_ge(s_mv, NK)
            act.wait_ge(s_const, 2)
            nc.scalar.activation(std[:, :], mv[:, :, 1], ACT.Sqrt, bias=eps[:, :]).then_inc(s_std, 1)
            for g in range(8):
                act.wait_ge(s_ft, g + 1)
                if g >= 2:
                    act.wait_ge(s_pq, g - 1)
                if g == 2:
                    act.wait_ge(s_vt0, 2)
                nc.scalar.copy(ft[:, g % 2, :], pf[:, g % 2, :]).then_inc(s_ftc, 1)
            nc.scalar.preload_act_table(ACT.Exp)
            act.wait_ge(s_init, 14)
            with act.Fori(0, NC) as c:
                for r in range(L):
                    act.wait_ge(s_max, L * c + r + 1)
                    nc.scalar.activation(ex[:, r % 2, :], row[:, r % 2, 1:], ACT.Exp, bias=nmax[:, r % 2:r % 2 + 1],
                                         accum_out=z[:, r % 2:r % 2 + 1]).then_inc(s_exp, 1)
                    if r == 1:
                        act.wait_ge(s_vall, c + 1)
                        act.sem_inc(s_pace_act, 1)
                        act.wait_ge(s_pv, c + 1)
                        nc.scalar.copy(vr[:, :], p_v[:, 0:D]).then_inc(s_vr, 1)
                    if r == 4:
                        act.wait_ge(s_vt2, c + 1)
                        act.sem_inc(s_pace_act, 1)
                        act.wait_ge(s_pt, c + 1)
                        nc.scalar.copy(vt1[:, :], p_t[:, 0:P]).then_inc(s_vt1, 1)
                    if 8 <= r < 8 + B:
                        act.wait_ge(s_g, c + 1)
                        q = slice(L * (r - 8), L * (r - 8) + L)
                        nc.scalar.copy(bdg[q, :, q], p_g[q, 0:2 * P].rearrange("p (g i) -> p g i", g=2)[:, :, q])\
                            .then_inc(s_bdg, 1)

        @block.vector
        def _(dve):
            for b in range(B):
                dve.wait_ge(s_x[b], 16)
            for k in range(NK):
                nc.vector.bn_stats(stats[:, k, :], x[:, k, :]).then_inc(s_stats, 1)
            for k in range(NK):
                dve.wait_ge(s_stats, k + 1)
                nc.vector.bn_aggr(mv[:, k, :], stats[:, k, :]).then_inc(s_mv, 1)
            dve.wait_ge(s_std, 1)
            nc.vector.reciprocal(rstd[:, :], std[:, :]).then_inc(s_rstd, 1)
            dve.wait_ge(s_rstd, 1)
            for k in range(NK):
                nc.vector.tensor_scalar(f[:, k, :], x[:, k, :], mv[:, k, 0:1], rstd[:, k:k + 1], ALU.subtract,
                                        ALU.mult).then_inc(s_f, 1)
            dve.wait_ge(s_w, 64)
            for g in range(8):
                dve.wait_ge(s_pq, g + 1)
                nc.vector.tensor_scalar(qt[:, 4 * g:4 * g + 4, :], pq[:, g % 2, :].rearrange("p (k i) -> p k i", k=4),
                                        bq[:, :], w2[:, :], ALU.add, ALU.mult).then_inc(s_qt, 1)
                if g == 0:
                    nc.vector.tensor_copy(vt1[:, :], ft[:, 0, 0:P]).then_inc(s_vt0, 1)
                    nc.vector.tensor_copy(vt2[:, :], ft[:, 0, P:2 * P]).then_inc(s_vt0, 1)
                    dve.wait_ge(s_vt0, 2)
            nc.vector.memset(qt[:, NK, :], 0.0).then_inc(s_init, 1)
            nc.vector.memset(tab[:, :, :], 0.0).then_inc(s_init, 1)
            nc.vector.memset(bdg[:, :, :], 0.0).then_inc(s_init, 1)
            dve.wait_ge(s_ident, 2)
            dve.wait_ge(s_const, 2)
            nc.vector.tensor_scalar(b0_row[:, :], zero_row[:, :], b0[:, :], None, ALU.add).then_inc(s_init, 1)
            dve.wait_ge(s_init, 6)
            for b in range(B):
                q = slice(L * b, L * b + L)
                for g in range(2):
                    nc.vector.tensor_copy(tab[q, 1 + g, L * g:L * g + L], ident[q, q]).then_inc(s_init, 1)
            dve.wait_ge(s_init, 14)
            dve.wait_ge(s_mask, 3)

            def weighted(g, k, r, done):
                nc.vector.scalar_tensor_tensor(junk[:, g, :], ex[:, k, :], 1.0, tab[:, g, r:r + ROW], ALU.mult,
                                               ALU.mult, accum_out=raw[:, g:g + 1]).then_inc(done, 1)

            def normalised(g0, g1, k, r, done):
                nc.vector.tensor_tensor(tab[:, g0:g1, r + WIN:r + ROW], raw[:, g0:g1].unsqueeze(2),
                                        rz[:, k:k + 1].unsqueeze(1).broadcast_to((P, g1 - g0, 1)),
                                        ALU.mult).then_inc(done, 1)

            with dve.Fori(0, NC) as c:
                nc.vector.tensor_copy(tab[:, 0, WIN:], b0_row[:, :]).then_inc(s_table, 1)
                dve.wait_ge(s_scores, c + 1)
                nc.vector.tensor_scalar(tab[:, 0, 0:WIN], p_s[:, 0:WIN], b0[:, :], None, ALU.add).then_inc(s_table, 1)
                dve.wait_ge(s_table, 2 * (c + 1))
                dve.sem_inc(s_pace, 1)
                nc.vector.stream_shuffle(row[:, 0, 1:], tab[:, 0, 0:ROW], [0] * L).then_inc(s_row, 1)
                nc.vector.stream_shuffle(row[:, 1, :], tab[:, 0, 0:ROW + 1], [1] * L).then_inc(s_row, 1)
                dve.wait_ge(s_row, L * c + 1)
                nc.vector.reduce_max(nmax[:, 0:1], row[:, 0, 1:], AX.X, negate=True).then_inc(s_max, 1)
                dve.wait_ge(s_bdc, c + 1)
                nc.vector.memset(tab[:, 1:3, WIN:], 0.0).then_inc(s_clear, 1)
                dve.wait_ge(s_clear, c + 1)
                for r in range(L):
                    k, n = r % 2, L * c + r
                    last = r == L - 1
                    dve.wait_ge(s_exp, n + 1)
                    nc.vector.reciprocal(rz[:, k:k + 1], z[:, k:k + 1]).then_inc(s_rz, 1)
                    if not last:
                        weighted(0, k, r, s_raw_score)
                        dve.wait_ge(s_row, L * c + r + 2)
                        dve.wait_ge(s_rz, n + 1)
                        nc.vector.scalar_tensor_tensor(junk[:, 3, :], ex[:, k, :], rz[:, k:k + 1],
                                                       row[:, 1 - k, 0:ROW], ALU.mult, ALU.mult,
                                                       accum_out=row[:, 1 - k, WIN:ROW]).then_inc(s_new, 1)
                    if r:
                        dve.wait_ge(s_coef, n)
                    weighted(1, k, r, s_raw)
                    if not last:
                        dve.wait_ge(s_new, (L - 1) * c + r + 1)
                        nc.vector.reduce_max(nmax[:, 1 - k:2 - k], row[:, 1 - k, 1:], AX.X, negate=True)\
                            .then_inc(s_max, 1)
                        dve.wait_ge(s_raw_score, (L - 1) * c + r + 1)
                        normalised(0, 1, k, r, s_score)
                    weighted(2, k, r, s_raw)
                    if r < L - 2:
                        dve.wait_ge(s_score, (L - 1) * c + r + 1)
                        dve.sem_inc(s_pace, 1)
                        nc.vector.stream_shuffle(row[:, k, :], tab[:, 0, r + 1:r + 2 + ROW], [r + 2] * L)\
                            .then_inc(s_row, 1)
                    dve.wait_ge(s_raw, 2 * n + 2)
                    normalised(1, 3, k, r, s_coef)
            dve.wait_ge(s_pv, NC + 1)
            nc.vector.tensor_copy(v_all[:, NC + 2, :], p_v[:, 0:D]).then_inc(s_vr, 1)

        @block.tensor
        def _(pe):
            pe.wait_ge(s_w, 64)
            pe.wait_ge(s_ident, 2)
            for g in range(8):
                pe.wait_ge(s_f, 4 * g + 4)
                if g >= 2:
                    pe.wait_ge(s_ftc, g - 1)
                for k in range(4):
                    ins = nc.tensor.transpose(pf[:, g % 2, P * k:P * k + P], f[:, 4 * g + k, :], ident[:, :])
                ins.then_inc(s_ft, 1)
                pe.wait_ge(s_ftc, g + 1)
                if g >= 2:
                    pe.wait_ge(s_qt, g - 1)
                nc.tensor.matmul(pq[:, g % 2, :], wq[:, :], ft[:, g % 2, :], start=True, stop=True).then_inc(s_pq, 1)
            pe.wait_ge(s_qn, 1)
            pe.wait_ge(s_vt0, 2)
            for b in range(B):
                q = slice(L * b, L * b + L)
                for g, vt in enumerate((vt1, vt2)):
                    ins = nc.tensor.matmul(p_s[q, L * g:L * g + L], qn[:, q], vt[:, q], start=True, stop=True)
            ins.then_inc(s_scores, 1)
            pe.wait_ge(s_init, 14)
            with pe.Fori(0, NC) as c:
                pe.wait_ge(s_bdc, c + 1)
                pe.wait_ge(s_vall, c + 1)
                for g in range(2):
                    ins = nc.tensor.matmul(p_v[:, 0:D], bdc[:, g, :], v_all[:, c + g, :], start=g == 0, stop=g == 1)
                ins.then_inc(s_pv, 1)
                pe.wait_ge(s_vr, c + 1)
                nc.tensor.transpose(p_t[:, 0:P], vr[:, :], ident[:, :]).then_inc(s_pt, 1)
                pe.wait_ge(s_vt1, c + 1)
                pe.wait_ge(s_qn, c + 2)
                for g, vt in enumerate((vt2, vt1)):
                    ins = nc.tensor.matmul(p_g[:, P * g:P * g + P], vt[:, :], qn[:, :], start=True, stop=True)
                ins.then_inc(s_g, 1)
                pe.wait_ge(s_bdg, B * (c + 1))
                pe.wait_ge(s_table, 2 * (c + 1))
                for b in range(B):
                    q = slice(L * b, L * b + L)
                    nc.tensor.matmul(p_s[q, 0:L], qn[:, q], vt1[:, q], start=True, stop=True)
                pe.wait_ge(s_coef, L * (c + 1))
                for g in range(2):
                    ins = nc.tensor.matmul(p_s[:, L:WIN], bdg[:, g, :], tab[:, 1 + g, WIN:], start=g == 0, stop=g == 1)
                ins.then_inc(s_scores, 1)
            pe.wait_ge(s_bdc, NC + 1)
            pe.wait_ge(s_vall, NC + 1)
            for g in range(2):
                ins = nc.tensor.matmul(p_v[:, 0:D], bdc[:, g, :], v_all[:, NC + g, :], start=g == 0, stop=g == 1)
            ins.then_inc(s_pv, 1)




def middle(nc, io, xt, x1_dram, h_dram):
    ctx = ExitStack()
    with ctx:
        def sb(name, shape, dt=F32):
            return ctx.enter_context(nc.sbuf_tensor(name, shape, dt))

        def sem(name):
            return ctx.enter_context(nc.semaphore(name))

        x, f, eps = xt["x"], xt["f"], xt["eps"]
        y = xt["v_all"][:, 1:, :]
        g_row, b_row = sb("g_row", [P, D]), sb("b_row", [P, D])
        stats, mv = sb("stats2", [P, NK, 6]), sb("mv2", [P, NK, 2])
        std, rstd, shift = sb("std2", [P, NK]), sb("rstd2", [P, NK]), sb("shift2", [P, NK])
        G, GK = 4, NK // 4
        m_w, m_tanh, m_y, m_stats, m_var, m_std, m_rstd, m_shift, m_norm, m_scaled, m_affine, m_res, m_out = (
            sem(n) for n in ("m_w", "m_tanh", "m_y", "m_stats", "m_var", "m_std", "m_rstd", "m_shift", "m_norm",
                             "m_scaled", "m_affine", "m_res", "m_out"))
        block = ctx.enter_context(nc.Block())

        def ks(g):
            return slice(GK * g, GK * g + GK)

        def wide(t):
            return t[:, :].unsqueeze(1).broadcast_to((P, GK, D))

        def pipelined(first, second):
            for g in range(G + 1):
                if g < G:
                    first(g)
                if g:
                    second(g - 1)

        @block.sync
        def _(sp):
            sp.dma_start(g_row[:, :], io["ln_g"].rearrange("(a d) -> a d", a=1).broadcast_to((P, D))).then_inc(m_w, 16)
            sp.dma_start(b_row[:, :], io["ln_b"].rearrange("(a d) -> a d", a=1).broadcast_to((P, D))).then_inc(m_w, 16)

            def out(to, batches, src, g):
                for b in range(batches):
                    q = slice(L * (b % B), L * (b % B) + L)
                    sp.dma_start(to[b].rearrange("(k j) d -> j k d", j=L)[:, ks(g), :], src[q, ks(g), :])\
                        .then_inc(m_out, 16)

            def first(g):
                sp.wait_ge(m_res, g + 1)
                out(x1_dram, B, x, g)

            def second(g):
                sp.wait_ge(m_norm, 2 * NK + GK * (g + 1))
                out(h_dram, B + 1, f, g)

            pipelined(first, second)
            sp.wait_ge(m_out, 16 * (2 * B + 1) * G)

        @block.scalar
        def _(act):
            for g in range(G):
                nc.scalar.activation(y[:, ks(g), :], y[:, ks(g), :], ACT.Tanh).then_inc(m_tanh, 1)
            for n in range(3):
                src, out = (x, f) if n == 2 else (y, y)

                def deviation(g):
                    act.wait_ge(m_var, NK * n + GK * (g + 1))
                    nc.scalar.activation(std[:, ks(g)], mv[:, ks(g), 1], ACT.Sqrt, bias=eps[:, :]).then_inc(m_std, 1)

                def apply(g):
                    act.wait_ge(m_shift, G * n + g + 1)
                    for k in range(GK * g, GK * g + GK):
                        nc.scalar.activation(out[:, k, :], src[:, k, :], ACT.Identity, bias=shift[:, k:k + 1],
                                             scale=rstd[:, k:k + 1]).then_inc(m_norm, 1)

                pipelined(deviation, apply)

        @block.gpsimd
        def _(pool):
            pool.wait_ge(m_w, 32)
            for g in range(G):
                pool.wait_ge(m_norm, GK * (g + 1))
                nc.gpsimd.tensor_tensor(y[:, ks(g), :], y[:, ks(g), :], wide(g_row), ALU.mult).then_inc(m_scaled, 1)

        @block.vector
        def _(dve):
            for n in range(3):
                def statistics(g):
                    if n == 0:
                        dve.wait_ge(m_tanh, g + 1)
                        nc.vector.scalar_tensor_tensor(y[:, ks(g), :], y[:, ks(g), :], 1.0, f[:, ks(g), :], ALU.add,
                                                       ALU.mult).then_inc(m_y, 1)
                        dve.wait_ge(m_y, g + 1)
                    elif n == 1:
                        dve.wait_ge(m_scaled, g + 1)
                        nc.vector.tensor_tensor(y[:, ks(g), :], y[:, ks(g), :], wide(b_row), ALU.add)\
                            .then_inc(m_affine, 1)
                        dve.wait_ge(m_affine, g + 1)
                    else:
                        dve.wait_ge(m_norm, NK + GK * (g + 1))
                        nc.vector.tensor_tensor(x[:, ks(g), :], x[:, ks(g), :], y[:, ks(g), :], ALU.add)\
                            .then_inc(m_res, 1)
                        dve.wait_ge(m_res, g + 1)
                    src = x if n == 2 else y
                    for k in range(GK * g, GK * g + GK):
                        nc.vector.bn_stats(stats[:, k, :], src[:, k, :]).then_inc(m_stats, 1)
                    for k in range(GK * g, GK * g + GK):
                        dve.wait_ge(m_stats, NK * n + k + 1)
                        nc.vector.bn_aggr(mv[:, k, :], stats[:, k, :]).then_inc(m_var, 1)

                def factors(g):
                    dve.wait_ge(m_std, G * n + g + 1)
                    nc.vector.reciprocal(rstd[:, ks(g)], std[:, ks(g)]).then_inc(m_rstd, 1)
                    dve.wait_ge(m_rstd, G * n + g + 1)
                    nc.vector.scalar_tensor_tensor(shift[:, ks(g)], mv[:, ks(g), 0], -1.0, rstd[:, ks(g)], ALU.mult,
                                                   ALU.mult).then_inc(m_shift, 1)

                pipelined(statistics, factors)


def constants(ctx, nc):
    def sb(name, shape, dt=F32):
        return ctx.enter_context(nc.sbuf_tensor(name, shape, dt))

    w = {n: sb(f"w_{n}", [P, D]) for n in ("Wq", "Wk", "Wv", "Wo")}
    w["Wg"] = sb("w_Wg", [P, E])
    w["W1"] = sb("w_W1", [P, E, FF])
    w["W2"] = sb("w_W2", [P, E, FC, D])
    w["b2"] = sb("w_b2", [E, D])
    w["b1"] = sb("w_b1", [E * FC, P])
    w["bqk"] = sb("w_bqk", [1, 4, D])
    for n in ("bv", "bo", "g1", "be1", "g2", "be2"):
        w[n] = sb(f"w_{n}", [P, D])
    w["bg"] = sb("w_bg", [P, E])
    w["cos"], w["sin"] = sb("w_cos", [P, T]), sb("w_sin", [P, T])
    return w


def load_constants(sp, w, io, arrived):
    def row(n):
        return io[n].rearrange("(a d) -> a d", a=1)

    def halves(n):
        return row(n).rearrange("a (h t e) -> a h t e", h=H, t=2)

    to, of = w["bqk"], w["bqk"][:, :, :].rearrange("a k (h t e) -> a k h t e", h=H, t=2)
    pairs = [(w[n][:, :], io[n]) for n in ("Wq", "Wk", "Wv", "Wo", "Wg")]
    pairs += [(w["W1"][:, :, :], io["W1"].rearrange("e d f -> d e f"))]
    pairs += [(w["W2"][:, e, :, :], io["W2"][e].rearrange("(c p) d -> p c d", p=P)) for e in range(E)]
    pairs += [(w["b2"][:, :], io["b2"]), (w["b1"][:, :], io["b1"].rearrange("e (c p) -> (e c) p", p=P))]
    for k, n in enumerate(("bq", "bk")):
        pairs += [(to[:, 2 * k, :], row(n))]
        pairs += [(of[:, 2 * k + 1, :, t, :], halves(n)[:, :, 1 - t, :]) for t in range(2)]
    pairs += [(w[n][:, :], row(n).broadcast_to((P, D))) for n in ("bv", "bo", "g1", "be1", "g2", "be2")]
    pairs += [(w["bg"][:, :], row("bg").broadcast_to((P, E))), (w["cos"][:, :], io["cos"]), (w["sin"][:, :], io["sin"])]
    for out, in_ in pairs:
        sp.dma_start(out, in_).then_inc(arrived, 16)
    return 16 * len(pairs)



BANK_USES = {"AT": 1, "WO": 1, "XT": 1, "GL": 1, "CT": 1, "B2": 1, "V": 1, "HID": 1, "Y": 1, "MT": 1, "OT": 1,
             "HT": 1, "QK": 2, "PRE": 1}


AHEAD = {(0, 4): [("HQ",)], (0, 9): [("HT", 0)], (0, 11): [("HT", 1)], (2, 4): [("QK", 0, 0)], (2, 12): [("QK", 0, 1)],
         (3, 4): [("QK", 1, 0)], (3, 12): [("QK", 1, 1)], (4, 2): [("PO", 0), ("PO", 1)], (4, 8): [("ST", 0, 1)],
         (5, 4): [("ST", 1, 1)], (5, 8): [("HR",)], (7, 2): [("ST", 2, 1)]}

AFTER = {(0, 4): [("AT", 0)], (0, 5): [("AT", 1), ("WO", 0)], (0, 6): [("WO", 1)],
         (0, 7): [("LNS", 0)], (0, 10): [("LND", 0), ("LNN", 0)], (0, 14): [("XT", 0)], (0, 15): [("XT", 1)],
         (1, -6): [("GL", 0), ("GL", 1)], (1, -4): [("GA",)], (1, 0): [("GE",), ("GB",)], (1, 2): [("GC",)],
         (1, 5): [("CT", 0)], (1, 6): [("CT", 1), ("B2", 0)], (1, 7): [("B2", 1)],
         (7, 0): [("ADD",)], (7, 1): [("LNS", 1)], (7, 5): [("LND", 1), ("LNN", 1)],
         (7, 8): [("LNS", 2)], (7, 13): [("LND", 2), ("LNN", 2)]}

EXPERTS = {1: (0,), 2: (1,), 3: (2, 3), 4: (4,), 5: (5, 6), 6: (7,)}

FIRST_READY, READY = 3, 4


def in_turn(first, end):
    steps = [("A", h, q, t) for h in range(first, end) for q in range(QT) for t in range(2)]
    return [(*x, k) for k, x in enumerate(steps)]


def order(attn, moe):
    if moe:
        yield "XR",
    if not attn:
        yield "PV", -1, 2 * QT - 1
        yield "OC", -1
        yield "OT", -1
        for name in ("AT", "WO"):
            for t in range(2):
                yield name, t
        for name in ("LNS", "LND", "LNN"):
            yield name, 0
        for name in ("XT", "GL"):
            for t in range(2):
                yield name, t
        yield "GA",
        yield "GE",
        for e in range(E):
            for j in range(2 * FC):
                yield "HID", e, j
            if e == 0:
                yield "GB",
                yield "GC",
                for name in ("CT", "B2"):
                    for t in range(2):
                        yield name, t
            for q in range(QT):
                yield "Y", e, q
        yield "ADD",
        for k in (1, 2):
            for name in ("LNS", "LND", "LNN"):
                yield name, k
        yield "OUT",
        return
    if moe:
        yield "ST", 3, 0

    halves = in_turn(READY if moe else FIRST_READY, H + READY)
    complete = []

    def maxima(n):
        for _ in range(n):
            x = halves.pop(0)
            yield x
            if x[1] % 2 and x[2:4] == (QT - 1, 1):
                complete.append([("MN", x[1] // 2), ("MT", x[1] // 2)])

    def sent():
        if complete:
            yield complete[0].pop(0)
            if not complete[0]:
                complete.pop(0)

    for hp in range(HP):
        experts = EXPERTS.get(hp, ()) if moe else ()
        due = 0
        for j in range(2 * FC if experts else 0):
            yield "HID", experts[0], j
            yield from sent()
            yield from maxima(2)
            yield from AFTER.get((hp, j - 8), ())
        for i in range(2 * QT):
            if len(experts) == 2 and i == QT:
                for j in range(2 * FC):
                    yield "HID", experts[1], j
                    yield from sent()
                    yield from maxima(2)
            weighed = bool(experts) and (i >= QT or len(experts) == 2)
            if i % 2 == 0:
                if not moe:
                    due = 4 + (i % 8 == 6)
                elif hp == 0:
                    due = 3 if i < 10 else int(i < 12)
                elif not experts or (hp == 1 and i < QT):
                    due = 0
                else:
                    due = 2 if weighed else 4
            for t in range(2):
                yield "B", hp, i, t
                n = int(due > 0 and not (i % 2 and t))
                yield from maxima(n)
                due -= n
                if weighed and t == 0:
                    yield "Y", experts[-1 if i >= QT else 0], i % QT
            yield from sent()
            if i > 1 and i % 2:
                yield "PV", hp, i - 2
            elif i == 1 and (hp or moe):
                yield "PV", hp - 1, 2 * QT - 1
            if i % 2:
                yield from maxima(due)
            if i == 1 and not hp:
                yield "V", 0
                yield "V", 1
            if i == 1 and (hp or moe):
                yield "OC", hp - 1
            if i == 3 and (hp or moe):
                yield "OT", hp - 1
            yield from AHEAD.get((hp, i), ())
            if moe:
                yield from AFTER.get((hp, i), ())
    assert not halves
    while complete:
        yield from sent()
    if moe:
        yield "OUT",


PROLOGUE = ([("PRE",), ("HQ",), ("HT", 0), ("HT", 1), ("QK", 0, 0), ("QK", 0, 1), ("PO", 0), ("QK", 1, 0),
             ("QK", 1, 1), ("PO", 1)] + [("ST", g, 1) for g in range(4)]
            + in_turn(0, FIRST_READY)[:4 * QT] + [("MN", 0), ("MT", 0)]
            + in_turn(0, FIRST_READY)[4 * QT:])
ST_DMAS = 6


def uses(steps):
    return sum(BANK_USES.get(x[0], 0) for x in steps)


class Fill:

    def __init__(self, base, n):
        self.base, self.n = base, n

    def slot(self, k=0):
        return (self.n + k) % 2

    def turn(self, k=0):
        return self.base + (self.n + k) // 2


def passes(engine, steps_of):
    def one(steps, s, base, n):
        for x in steps:
            steps_of(x, s, Fill(base, n))
            n += BANK_USES.get(x[0], 0)

    first, both = uses(PROLOGUE), uses(order(True, True))
    assert both % 2 == 0
    one(PROLOGUE, -1, 0, 0)
    one(order(True, False), 0, 0, first)
    first += uses(order(True, False))
    with engine.Fori(1, B) as s:
        one(order(True, True), s, (s - 1) * (both // 2), first)
    one(order(False, True), B, (B - 1) * (both // 2), first)


def second_layer(nc, io, w, stacks, ident, eps, x1_dram, h_dram, parts_dram):
    ctx = ExitStack()
    with ctx:
        def sb(name, shape, dt=F32):
            return ctx.enter_context(nc.sbuf_tensor(name, shape, dt))

        def ps(name, shape, dt=F32):
            return ctx.enter_context(nc.psum_tensor(name, shape, dt))

        def sem(name):
            return ctx.enter_context(nc.semaphore(name))

        ks, qs, zeros = stacks["ks"], stacks["qs"], stacks["zeros"]
        wp = sb("wp", [P, 2, D])
        cols = sb("cols", [P, 4 + E * FC])
        hq = sb("hq", [P, QT, D])
        ht = sb("ht", [P, T])
        rot = sb("rot", [P, 2, HALF])
        full = sb("full", [P, HALF])
        rest = sb("rest", [P, HALF])
        parts = sb("parts", [P, 2, 3, T], BF16)
        va = sb("va", [P, QT, H, VH])
        nm_half = sb("nm_half", [P, 2, 2, 2, QT])
        nm = sb("nm", [P, 2, 2, QT])
        m_hi, m_lo = sb("m_hi", [2 * QT, 2, P], BF16), sb("m_lo", [2 * QT, 2, P], BF16)
        pt = sb("pt", [P, 4, T])
        o_sb = sb("o_sb", [P, 512])
        rcp = sb("rcp", [P, 4, 4])
        ao = sb("ao", [P, QT, D])
        aot = sb("aot", [P, T])
        hr, xr, xa, acc = sb("hr", [P, QT, D]), sb("xr", [P, QT, D]), sb("xa", [P, QT, D]), sb("acc", [P, QT, D])
        xt = aot
        hid = sb("hid", [P, FC, T])
        stats, mv = sb("stats3", [P, QT, 6]), sb("mv3", [P, QT, 2])
        std, rstd = sb("std3", [P, QT]), sb("rstd3", [P, QT])
        logit, prob, top = sb("logit", [P, QT, E]), sb("prob", [P, QT, E]), sb("top", [P, QT, 8])
        mx, zs, idx, idx_f = sb("mx", [P, QT]), sb("zs", [P, QT]), sb("idx", [P, QT, 8], U32), sb("idx_f", [P, QT, 8])
        pick = sb("pick", [P, 2, QT, E])
        comb, ct = sb("comb", [P, QT, E]), sb("ct", [E, T])
        expert = sb("expert", [P, E])

        s1 = [ps(f"s1{i}", [P, HALF]) for i in range(3)]
        s2 = [ps(f"s2{i}", [P, HALF]) for i in range(2)]
        p_o = ps("p_o", [P, 512])
        banks = [ps(f"bank{i}", [P, 512]) for i in range(2)]

        s_pace, s_pace_act = sem("s_pace2"), sem("s_pace_act2")
        s_setup, s_iota = sem("s_setup"), sem("s_iota")
        s_bank = [sem(f"s_bank{i}") for i in range(2)]
        s_free = [sem(f"s_free{i}") for i in range(2)]
        s_hq, s_r, s_sp, s_split = sem("s_hq"), sem("s_r"), sem("s_sp"), sem("s_split")
        s_po = [sem(f"s_po{x}") for x in range(2)]
        s_st = [sem(f"s_st{g}") for g in range(4)]
        s_s1, s_max, s_nm = sem("s_s1"), sem("s_max"), sem("s_nm")
        s_mr = [sem(f"s_mr{g}") for g in range(2)]
        s_s2, s_exp, s_pv, s_oc, s_rc = sem("s_s2"), sem("s_exp"), sem("s_pv"), sem("s_oc"), sem("s_rc")
        s_mh = sem("s_mh")
        s_hr, s_hrb, s_xr = sem("s_hr"), sem("s_hrb"), sem("s_xr")
        l_stats, l_var, l_std, l_rstd, l_norm, l_scale, l_affine = (
            sem(n) for n in ("l_stats", "l_var", "l_std", "l_rstd", "l_norm", "l_scale", "l_affine"))
        s_gate, s_gexp, s_comb, s_sum, s_added, s_fin, s_out = (
            sem(n) for n in ("s_gate", "s_gexp", "s_comb", "s_sum", "s_added", "s_fin", "s_out"))
        block = ctx.enter_context(nc.Block())

        def tokens(t):
            return slice(HALF * t, HALF * t + HALF)

        def tile(q):
            return slice(P * q, P * q + P)

        def wide(t, n=QT):
            return t[:, :].unsqueeze(1).broadcast_to((P, n, t.shape[1]))

        def which(s):
            known = isinstance(s, int)
            return (0 if known and s < 0 else s), known and s < 0, known and s == 0

        def norm_index(s, k):
            return 3 * (s - 1) + k

        def filled(engine, fill, k=0):
            engine.wait_ge(s_bank[fill.slot(k)], fill.turn(k) + 1)

        def taken(engine, fill, k=0):
            engine.wait_ge(s_free[fill.slot(k)], fill.turn(k) + 1)

        def drained(engine, fill):
            taken(engine, fill, -2)
            taken(engine, fill, -1)

        def split(engine, compute, k, t, s, fill):
            n = 4 * (s + 1) + 2 * k + t
            out = [parts[:, k, i, tokens(t)] for i in range(3)]
            if not (isinstance(s, int) and s < 0):
                engine.wait_ge(s_po[k], 16 * PARTS * (s + 1))
            taken(engine, fill)
            engine.sem_inc(s_pace, 1)
            taken(engine, fill, 1)
            engine.sem_inc(s_pace, 1)
            compute.tensor_tensor(full[:, :], rot[:, 0, :], rot[:, 1, :], ALU.add).then_inc(s_r, 1)
            engine.wait_ge(s_r, n + 1)
            engine.sem_inc(s_pace, 1)
            compute.tensor_copy(out[0], full[:, :]).then_inc(s_split, 1)
            engine.wait_ge(s_split, 3 * n + 1)
            compute.tensor_tensor(rest[:, :], full[:, :], out[0], ALU.subtract).then_inc(s_split, 1)
            engine.wait_ge(s_split, 3 * n + 2)
            engine.sem_inc(s_pace, 1)
            compute.tensor_copy(out[1], rest[:, :]).then_inc(s_split, 1)
            engine.wait_ge(s_split, 3 * n + 3)
            compute.tensor_tensor(out[2], rest[:, :], out[1], ALU.subtract).then_inc(s_sp, 1)

        @block.sync
        def _(sp):
            def wait(semaphore, n):
                sp.wait_ge(semaphore, n)
                sp.sem_inc(s_pace, 1)

            def step(x, s, fill):
                name, b, starts, zeroth = x[0], *which(s)
                bank, free = banks[fill.slot()], s_free[fill.slot()]
                if name == "HQ":
                    sp.dma_start(hq[:, :, :], h_dram[s + 1].rearrange("(q p) d -> p q d", p=P)).then_inc(s_hq, 16)
                elif name == "HR":
                    sp.dma_start(hr[:, :, :], h_dram[s].rearrange("(q p) d -> p q d", p=P)).then_inc(s_hr, 16)
                elif name == "XR":
                    sp.dma_start(xr[:, :, :], x1_dram[s - 1].rearrange("(q p) d -> p q d", p=P)).then_inc(s_xr, 16)
                elif name == "PO":
                    wait(s_sp, 4 * (s + 1) + 2 * x[1] + 2)
                    if not starts:
                        for g in range(4):
                            wait(s_st[g], 16 * ST_DMAS * (s + 1))
                    for n, part in enumerate(CHOSEN[x[1]]):
                        to = parts_dram[x[1]][:, HD * n:HD * n + HD, :]
                        sp.dma_start(to, parts[:, x[1], part, :]).then_inc(s_po[x[1]], 16)
                elif name == "ST":
                    g, ahead = x[1], x[2]
                    nb = s + ahead
                    for k in range(2):
                        wait(s_po[k], 16 * PARTS * (nb + 1))
                    if not starts:
                        wait(s_pv, 64 * (nb - 1) + 16 * (g + 1))
                    for par in range(2):
                        rows = slice(64 * par, 64 * par + M_ROW)
                        for k, dst in enumerate((qs[rows, 2 * g:2 * g + 2, :], ks[rows, 4 * g + par:4 * g + 4:2, :])):
                            heads = parts_dram[k][4 * g + par:4 * g + 4:2]
                            sp.dma_start(dst, heads.rearrange("h m t -> m h t")).then_inc(s_st[g], 16)
                        r = 64 * par + M_ROW
                        sp.dma_start(qs[r:r + 2, 2 * g:2 * g + 2, :], zeros[:, :, :]).then_inc(s_st[g], 16)
                elif name == "MT":
                    hp = x[1]
                    wait(s_free[fill.slot()], fill.turn() + 1)
                    for k, rows in enumerate((m_hi, m_lo)):
                        for par in range(2):
                            r = 64 * par + M_ROW + k
                            sp.dma_start(qs[r:r + 1, hp % HP, :].rearrange("a (q p) -> a q p", p=P),
                                         rows[QT * par:QT * par + QT, hp % 2, :]).then_inc(s_mr[hp % 2], 16)
                elif name == "OUT":
                    wait(s_fin, s)
                    sp.dma_start(io["out"][s - 1].rearrange("(q p) d -> p q d", p=P), xa[:, :, :]).then_inc(s_out, 16)
                    wait(s_out, 16 * s)

            passes(sp, step)
            for g in range(3):
                sp.wait_ge(s_st[g], 16 * ST_DMAS * (B + 1))
            sp.wait_ge(s_mr[0], 64 * (4 * B + 1))
            sp.wait_ge(s_mr[1], 64 * (4 * B + 1))

        @block.gpsimd
        def _(pool):
            nc.gpsimd.iota(expert[:, :], [[1, E]], base=0, channel_multiplier=0,
                           allow_small_or_imprecise_dtypes=True).then_inc(s_iota, 1)

            def step(x, s, fill):
                name, b, starts, zeroth = x[0], *which(s)
                bank, free = banks[fill.slot()], s_free[fill.slot()]
                if name == "QK" and not starts:
                    split(pool, nc.gpsimd, x[1], x[2], s, fill)
                elif name == "HR":
                    pool.wait_ge(s_hr, 16 * (s + 1))
                    nc.gpsimd.tensor_tensor(hr[:, :, :], hr[:, :, :], wide(w["bo"]), ALU.add).then_inc(s_hrb, 1)

            passes(pool, step)

        @block.scalar
        def _(act):
            def step(x, s, fill):
                name, b, starts, zeroth = x[0], *which(s)
                bank, free = banks[fill.slot()], s_free[fill.slot()]
                if name == "PRE":
                    filled(act, fill)
                    nc.scalar.copy(cols[:, :], bank[:, 0:4 + E * FC]).then_inc(free, 1)
                elif name == "B":
                    hp, i, t = x[1:]
                    n = 128 * s + 16 * hp + i
                    if i % 2 == 0 and t == 0 and not (zeroth and hp == 0 and i < 4):
                        act.wait_ge(s_pv, 64 * s + 8 * hp + i // 2 - 1)
                        act.sem_inc(s_pace_act, 1)
                    act.wait_ge(s_s2, 2 * n + t + 1)
                    nc.scalar.activation(pt[:, i % 4, tokens(t)], s2[t][:, :], ACT.Exp,
                                         scale=SCALE).then_inc(s_exp, 1)
                elif name == "HID":
                    e, f, t = x[1], x[2] % FC, x[2] // FC
                    filled(act, fill)
                    nc.scalar.activation(hid[:, f, tokens(t)], bank[:, :], ACT.Gelu,
                                         bias=cols[:, 4 + FC * e + f:5 + FC * e + f]).then_inc(free, 1)
                elif name in ("HT", "AT", "XT"):
                    filled(act, fill)
                    to = {"HT": ht, "AT": aot, "XT": xt}[name]
                    nc.scalar.copy(to[:, tokens(x[1])], bank[:, :]).then_inc(free, 1)
                elif name == "CT":
                    filled(act, fill)
                    nc.scalar.copy(ct[:, tokens(x[1])], bank[0:E, :]).then_inc(free, 1)
                elif name == "B2":
                    filled(act, fill)
                    nc.scalar.copy(acc[:, 4 * x[1]:4 * x[1] + 4, :],
                                   bank[:, :].rearrange("p (q d) -> p q d", q=4)).then_inc(free, 1)
                elif name == "LND":
                    act.wait_ge(l_var, QT * (norm_index(s, x[1]) + 1))
                    nc.scalar.activation(std[:, :], mv[:, :, 1], ACT.Sqrt, bias=eps[:, :]).then_inc(l_std, 1)
                elif name == "GE":
                    act.wait_ge(s_gate, 8 * (s - 1) + 2)
                    nc.scalar.activation(prob[:, :, :], logit[:, :, :], ACT.Exp).then_inc(s_gexp, 1)

            passes(act, step)

        @block.vector
        def _(dve):
            nc.vector.memset(va[:, :, :, HD:], 1.0).then_inc(s_setup, 1)
            nc.vector.memset(p_o[:, :], 0.0).then_inc(s_setup, 1)
            for k, n in enumerate(("Wq", "Wk")):
                a = w[n][:, :].rearrange("p (h t e) -> p h t e", h=H, t=2)
                b = wp[:, k, :].rearrange("p (h t e) -> p h t e", h=H, t=2)
                for t in range(2):
                    nc.vector.tensor_copy(b[:, :, t, :], a[:, :, 1 - t, :]).then_inc(s_setup, 1)

            def statistics(n):
                for q in range(QT):
                    nc.vector.bn_stats(stats[:, q, :], xa[:, q, :]).then_inc(l_stats, 1)
                for q in range(QT):
                    dve.wait_ge(l_stats, QT * n + q + 1)
                    dve.sem_inc(s_pace, 1)
                    nc.vector.bn_aggr(mv[:, q, :], stats[:, q, :]).then_inc(l_var, 1)

            def normed(n):
                dve.wait_ge(l_std, n + 1)
                nc.vector.reciprocal(rstd[:, :], std[:, :]).then_inc(l_rstd, 1)
                dve.wait_ge(l_rstd, n + 1)
                for q in range(QT):
                    nc.vector.tensor_scalar(xa[:, q, :], xa[:, q, :], mv[:, q, 0:1], rstd[:, q:q + 1], ALU.subtract,
                                            ALU.mult).then_inc(l_norm, 1)

            link = [0]
            at = {}

            def chain(s, ins):
                link[0] = link[0] % 8 + 1
                ins.then_inc(s_gate, 1)
                dve.wait_ge(s_gate, 8 * (s - 1) + link[0])

            def per_tile(t):
                return t.unsqueeze(2).broadcast_to((P, QT, E))

            def step(x, s, fill):
                name, b, starts, zeroth = x[0], *which(s)
                bank, free = banks[fill.slot()], s_free[fill.slot()]
                at[x] = fill
                if name == "A":
                    head, q, t, k = x[1:]
                    n = 8 * (16 * b + head) + q
                    dve.wait_ge(s_s1, 2 * n + t + 1)
                    nc.vector.reduce_max(nm_half[:, t, head // 2 % 2, head % 2, q:q + 1], s1[k % 3][:, :], AX.X,
                                         negate=True).then_inc(s_max, 1)
                elif name == "MN":
                    hp = x[1]
                    dve.wait_ge(s_max, 32 * (8 * b + hp + 1))
                    k = hp % 2
                    nc.vector.tensor_tensor(nm[:, k, :, :], nm_half[:, 0, k, :, :], nm_half[:, 1, k, :, :],
                                            ALU.min).then_inc(s_nm, 1)
                elif name == "MT":
                    hp = x[1]
                    filled(dve, fill)
                    if not (starts or (zeroth and hp < 2)):
                        dve.wait_ge(s_mr[hp % 2], 64 * (4 * s + hp // 2))
                    nc.vector.tensor_copy(m_hi[:, hp % 2, :], bank[0:2 * QT, 0:P]).then_inc(s_mh, 1)
                    dve.wait_ge(s_mh, 8 * b + hp + 1)
                    nc.vector.tensor_tensor(m_lo[:, hp % 2, :], bank[0:2 * QT, 0:P], m_hi[:, hp % 2, :],
                                            ALU.subtract).then_inc(free, 1)
                elif name == "Y":
                    e, q = x[1], x[2]
                    filled(dve, fill)
                    nc.vector.scalar_tensor_tensor(acc[:, q, :], bank[:, 0:D], comb[:, q, e:e + 1], acc[:, q, :],
                                                   ALU.mult, ALU.add).then_inc(free, 1)
                elif name == "OC":
                    u = 8 * s + x[1]
                    dve.wait_ge(s_pv, 8 * (u + 1))
                    nc.vector.tensor_copy(o_sb[:, :], p_o[:, :]).then_inc(s_oc, 1)
                elif name == "OT":
                    hp = x[1]
                    u = 8 * s + hp
                    filled(dve, fill)
                    o = bank[:, :].rearrange("p (t j c) -> p t j c", t=4, j=4)
                    nc.vector.reciprocal(rcp[:, :, :], o[:, :, :, HD]).then_inc(s_rc, 1)
                    dve.wait_ge(s_rc, 2 * u + 1)
                    for half in range(2):
                        ins = nc.vector.tensor_tensor(
                            ao[:, 4 * half:4 * half + 4, 2 * HD * (hp % HP):2 * HD * (hp % HP) + 2 * HD]
                            .rearrange("p t (r e) -> p t r e", r=2),
                            o[:, :, half::2, 0:HD],
                            rcp[:, :, half::2].unsqueeze(3).broadcast_to((P, 4, 2, HD)), ALU.mult)
                        ins.then_inc(free if half else s_rc, 1)
                elif name == "V":
                    t = x[1]
                    filled(dve, fill)
                    nc.vector.tensor_tensor(
                        va[:, 4 * t:4 * t + 4, :, 0:HD], bank[:, :].rearrange("p (q h e) -> p q h e", q=4, h=H),
                        w["bv"][:, :].rearrange("p (h e) -> p h e", h=H).unsqueeze(1).broadcast_to((P, 4, H, HD)),
                        ALU.add).then_inc(free, 1)
                elif name == "QK":
                    k, t = x[1], x[2]
                    if not (starts and k == 0 and t == 0):
                        dve.wait_ge(s_sp, 4 * (s + 1) + 2 * k + t)
                    for i, table in enumerate((w["cos"], w["sin"])):
                        filled(dve, fill, i)
                        nc.vector.scalar_tensor_tensor(rot[:, i, :], banks[fill.slot(i)][:, :],
                                                       cols[:, 2 * k + i:2 * k + i + 1], table[:, tokens(t)],
                                                       ALU.add, ALU.mult).then_inc(s_free[fill.slot(i)], 1)
                    if starts:
                        split(dve, nc.vector, k, t, s, fill)
                elif name == "WO":
                    t = x[1]
                    filled(dve, fill)
                    dve.wait_ge(s_hrb, s)
                    dve.wait_ge(s_xr, 16 * s)
                    nc.vector.tensor_tensor(xa[:, 4 * t:4 * t + 4, :], bank[:, :].rearrange("p (q d) -> p q d", q=4),
                                            hr[:, 4 * t:4 * t + 4, :], ALU.add).then_inc(free, 1)
                elif name == "LNS":
                    k = x[1]
                    if k == 0:
                        for t in range(2):
                            taken(dve, at["WO", t])
                    elif k == 1:
                        dve.wait_ge(s_added, s)
                    else:
                        dve.wait_ge(l_affine, 2 * s)
                    statistics(norm_index(s, k))
                elif name == "LNN":
                    k = x[1]
                    n = norm_index(s, k)
                    normed(n)
                    if k == 2:
                        dve.wait_ge(s_xr, 16 * s)
                        dve.wait_ge(l_norm, QT * (n + 1))
                        nc.vector.tensor_tensor(xa[:, :, :], xa[:, :, :], xr[:, :, :], ALU.add).then_inc(s_fin, 1)
                    else:
                        gain, bias = ((w["g1"], w["be1"]), (w["g2"], w["be2"]))[k]
                        dve.wait_ge(l_norm, QT * (n + 1))
                        nc.vector.tensor_tensor(xa[:, :, :], xa[:, :, :], wide(gain), ALU.mult).then_inc(l_scale, 1)
                        dve.wait_ge(l_scale, 2 * (s - 1) + k + 1)
                        nc.vector.tensor_tensor(xa[:, :, :], xa[:, :, :], wide(bias), ALU.add).then_inc(l_affine, 1)
                elif name == "ADD":
                    for q in (QT - 2, QT - 1):
                        taken(dve, at["Y", E - 1, q])
                    nc.vector.tensor_tensor(xa[:, :, :], xa[:, :, :], acc[:, :, :], ALU.add).then_inc(s_added, 1)
                elif name == "GL":
                    filled(dve, fill)
                    nc.vector.tensor_tensor(logit[:, 4 * x[1]:4 * x[1] + 4, :],
                                            bank[:, 0:4 * E].rearrange("p (q e) -> p q e", q=4),
                                            wide(w["bg"], 4), ALU.add).then_inc(free, 1)
                elif name == "GA":
                    for t in range(2):
                        taken(dve, at["GL", t])
                    chain(s, nc.vector.reduce_max(mx[:, :], logit[:, :, :], AX.X))
                    chain(s, nc.vector.tensor_tensor(logit[:, :, :], logit[:, :, :], per_tile(mx[:, :]), ALU.subtract))
                elif name == "GB":
                    dve.wait_ge(s_gexp, s)
                    chain(s, nc.vector.reduce_sum(zs[:, :], prob[:, :, :], AX.X))
                    chain(s, nc.vector.reciprocal(mx[:, :], zs[:, :]))
                    chain(s, nc.vector.tensor_tensor(prob[:, :, :], prob[:, :, :], per_tile(mx[:, :]), ALU.mult))
                    dve.sem_inc(s_pace, 1)
                    for q in range(QT):
                        nc.vector.max(top[:, q, :], prob[:, q, :]).then_inc(s_sum, 1)
                elif name == "GC":
                    for q in range(QT):
                        dve.wait_ge(s_sum, 16 * (s - 1) + q + 1)
                        dve.sem_inc(s_pace, 1)
                        nc.vector.max_index(idx[:, q, :], top[:, q, :], prob[:, q, :]).then_inc(s_sum, 1)
                    dve.wait_ge(s_sum, 16 * s)
                    chain(s, nc.vector.tensor_copy(idx_f[:, :, :], idx[:, :, :]))
                    chain(s, nc.vector.tensor_tensor(zs[:, :], top[:, :, 0], top[:, :, 1], ALU.add))
                    chain(s, nc.vector.reciprocal(mx[:, :], zs[:, :]))
                    for k in range(2):
                        nc.vector.tensor_tensor(pick[:, k, :, :], wide(expert), per_tile(idx_f[:, :, k]),
                                                ALU.is_equal).then_inc(s_comb, 1)
                        nc.vector.tensor_tensor(top[:, :, k], top[:, :, k], mx[:, :], ALU.mult).then_inc(s_comb, 1)
                    dve.wait_ge(s_comb, 7 * (s - 1) + 4)
                    for k in range(2):
                        nc.vector.tensor_tensor(pick[:, k, :, :], pick[:, k, :, :], per_tile(top[:, :, k]),
                                                ALU.mult).then_inc(s_comb, 1)
                    dve.wait_ge(s_comb, 7 * (s - 1) + 6)
                    nc.vector.tensor_tensor(comb[:, :, :], pick[:, 0, :, :], pick[:, 1, :, :], ALU.add)\
                        .then_inc(s_comb, 1)

            dve.wait_ge(s_iota, 1)
            passes(dve, step)

        @block.tensor
        def _(pe):
            at = {}

            def weigh_values(s, hp, i):
                kt = i // 2
                pe.wait_ge(s_exp, 2 * (128 * s + 16 * hp + i) + 2)
                if kt == 0 and not (which(s)[2] and hp == 0):
                    pe.wait_ge(s_oc, 8 * s + hp)
                for par in range(2):
                    for t in range(2):
                        j = 32 * (2 * par + t)
                        ins = nc.tensor.matmul(p_o[j:j + VH, :], va[:, kt, 2 * (hp % HP) + par, :],
                                               pt[:, (i - 1 + par) % 4, tokens(t)], start=kt == 0, stop=kt == QT - 1)
                ins.then_inc(s_pv, 1)

            def step(x, s, fill):
                name, b, starts, zeroth = x[0], *which(s)
                bank, full_bank = banks[fill.slot()], s_bank[fill.slot()]
                at[x] = fill
                if name in BANK_USES and fill.n >= 2:
                    taken(pe, fill, -2)
                if name == "PRE":
                    pe.wait_ge(s_setup, 6)
                    for k in range(4):
                        nc.tensor.matmul(bank[:, k:k + 1], w["bqk"][0:1, k, :], ident[0:1, 0:1], start=True, stop=True)
                    nc.tensor.transpose(bank[:, 4:4 + E * FC], w["b1"][:, :], ident[0:E * FC, 0:E * FC])\
                        .then_inc(full_bank, 1)
                elif name == "A":
                    head, q, t, k = x[1:]
                    n = 8 * (16 * b + head) + q
                    if q == 0 and t == 0 and head % 4 == 0:
                        pe.wait_ge(s_st[head % H // 4], 16 * ST_DMAS * (b + 1 + head // H))
                    if k >= 3:
                        pe.wait_ge(s_max, 2 * n + t - 2)
                    elif not starts:
                        pe.wait_ge(s_max, 2 * n + t - k)
                    nc.tensor.matmul(s1[k % 3][:, :], qs[:, head % H // 2, tile(q)],
                                     ks[:, head % H, tokens(t)], start=True, stop=True).then_inc(s_s1, 1)
                elif name == "B":
                    hp, i, t = x[1:]
                    head, kt = 2 * hp + i % 2, i // 2
                    if i == 0 and t == 0:
                        pe.wait_ge(s_mr[hp % 2], 64 * (4 * s + hp // 2 + 1))
                    m = 32 * hp + 2 * i + t
                    if not (zeroth and m < 2):
                        pe.wait_ge(s_exp, 256 * s + m - 1)
                    nc.tensor.matmul(s2[t][:, :], ks[:, head, tile(kt)], qs[:, hp, tokens(t)], start=True,
                                     stop=True).then_inc(s_s2, 1)
                elif name == "PV":
                    if x[1:] == (0, 1):
                        taken(pe, at["V", 0])
                        taken(pe, at["V", 1])
                    weigh_values(s, *x[1:])
                elif name == "MT":
                    hp = x[1]
                    pe.wait_ge(s_nm, 8 * b + hp + 1)
                    nc.tensor.transpose(bank[0:2 * QT, 0:P], nm[:, hp % 2, :, :].rearrange("p r q -> p (r q)"),
                                        ident[:, :]).then_inc(full_bank, 1)
                elif name == "OT":
                    pe.wait_ge(s_oc, 8 * s + x[1] + 1)
                    for t in range(4):
                        ins = nc.tensor.transpose(bank[:, tile(t)], o_sb[:, tile(t)], ident[:, :])
                    ins.then_inc(full_bank, 1)
                elif name == "HID":
                    e, f, t = x[1], x[2] % FC, x[2] // FC
                    nc.tensor.matmul(bank[:, :], w["W1"][:, e, tile(f)], xt[:, tokens(t)], start=True, stop=True)\
                        .then_inc(full_bank, 1)
                elif name == "Y":
                    e, q = x[1], x[2]
                    if q == 0:
                        taken(pe, at["HID", e, 2 * FC - 1])
                    for f in range(FC):
                        ins = nc.tensor.matmul(bank[:, 0:D], hid[:, f, tile(q)], w["W2"][:, e, f, :], start=f == 0,
                                               stop=f == FC - 1)
                    ins.then_inc(full_bank, 1)
                elif name in ("HT", "AT", "XT"):
                    if name == "HT":
                        pe.wait_ge(s_hq, 16 * (s + 2))
                    if name == "XT":
                        pe.wait_ge(l_affine, 2 * (s - 1) + 1)
                    if x == ("AT", 0):
                        drained(pe, fill)
                    src = {"HT": hq, "AT": ao, "XT": xa}[name]
                    for q in range(4):
                        ins = nc.tensor.transpose(bank[:, tile(q)], src[:, 4 * x[1] + q, :], ident[:, :])
                    ins.then_inc(full_bank, 1)
                elif name == "QK":
                    k, t = x[1], x[2]
                    taken(pe, at["HT", t])
                    for i, wt in enumerate((w[("Wq", "Wk")[k]][:, :], wp[:, k, :])):
                        if i:
                            taken(pe, fill, -1)
                        nc.tensor.matmul(banks[fill.slot(i)][:, :], wt, ht[:, tokens(t)], start=True, stop=True)\
                            .then_inc(s_bank[fill.slot(i)], 1)
                elif name == "V":
                    for q in range(4):
                        ins = nc.tensor.matmul(bank[:, tile(q)], ht[:, tile(4 * x[1] + q)], w["Wv"][:, :], start=True,
                                               stop=True)
                    ins.then_inc(full_bank, 1)
                elif name == "WO":
                    taken(pe, at["AT", x[1]])
                    for q in range(4):
                        ins = nc.tensor.matmul(bank[:, tile(q)], aot[:, tile(4 * x[1] + q)], w["Wo"][:, :], start=True,
                                               stop=True)
                    ins.then_inc(full_bank, 1)
                elif name == "GL":
                    taken(pe, at["XT", x[1]])
                    for q in range(4):
                        ins = nc.tensor.matmul(bank[:, E * q:E * q + E], xt[:, tile(4 * x[1] + q)], w["Wg"][:, :],
                                               start=True, stop=True)
                    ins.then_inc(full_bank, 1)
                elif name == "CT":
                    pe.wait_ge(s_comb, 7 * s)
                    for q in range(4):
                        ins = nc.tensor.transpose(bank[0:E, tile(q)], comb[:, 4 * x[1] + q, :], ident[:, :])
                    ins.then_inc(full_bank, 1)
                elif name == "B2":
                    taken(pe, at["CT", x[1]])
                    for q in range(4):
                        ins = nc.tensor.matmul(bank[:, tile(q)], ct[:, tile(4 * x[1] + q)], w["b2"][:, :], start=True,
                                               stop=True)
                    ins.then_inc(full_bank, 1)

            passes(pe, step)


def program(nc, io):
    x1_dram = nc.dram_tensor("x1_dram", (B, T, D), F32).ap()
    h_dram = nc.dram_tensor("h_dram", (B + 1, T, D), F32).ap()
    parts_dram = nc.dram_tensor("parts_dram", (2, H, PARTS * HD, T), BF16).ap()
    ctx = ExitStack()
    with ctx:
        ident = ctx.enter_context(nc.sbuf_tensor("ident", [P, P], F32))
        eps = ctx.enter_context(nc.sbuf_tensor("eps", [P, 1], F32))
        w = constants(ctx, nc)
        stacks = {n: ctx.enter_context(nc.sbuf_tensor(n, shape, BF16))
                  for n, shape in (("ks", [P, H, T]), ("qs", [P, HP, T]), ("zeros", [2, 2, T]), ("ones", [2, T]))}
        s_weights = ctx.enter_context(nc.semaphore("s_weights"))
        with ExitStack() as first:
            xt = {n: first.enter_context(nc.sbuf_tensor(n, [P, k, D], F32))
                  for n, k in (("x", NK), ("f", NK), ("v_all", NK + 1))}
            xt["ident"], xt["eps"] = ident, eps
            window_attention(nc, io, xt, w, stacks, s_weights)
            middle(nc, io, xt, x1_dram, h_dram)
        second_layer(nc, io, w, stacks, ident, eps, x1_dram, h_dram, parts_dram)


_INS = {"x": "L0_attn_feature", "wq_w": "L0_attn_wq_w", "wq_b": "L0_attn_wq_b", "w2_w": "L0_attn_w2_w",
        "w2_b": "L0_attn_w2_b", "ln_g": "L0_attn_ln_g", "ln_b": "L0_attn_ln_b"}
_INS.update({n: f"L0_ffn_{n}" for n in ("Wq", "bq", "Wk", "bk", "Wv", "bv", "Wo", "bo", "Wg", "bg", "W1", "b1", "W2",
                                        "b2", "g1", "be1", "g2", "be2")})


def rotation_tables():
    inv_freq = (1.0 / 10000.0 ** (np.arange(0, HD, 2, dtype=np.float32) / np.float32(HD))).astype(np.float32)
    angle = np.arange(T, dtype=np.float32)[None, :] * inv_freq[:, None]
    sign = np.repeat(np.float32([-1, 1]), HD // 2)[:, None]
    return np.tile(np.cos(angle), (2 * H, 1)), np.tile(sign * np.tile(np.sin(angle), (2, 1)), (H, 1))


def kernel(**inputs):
    import concourse.bacc as bacc
    from concourse.bass_utils import run_bass_kernel_spmd

    nc = bacc.Bacc("TRN2", target_bir_lowering=False, num_devices=1)
    arrays = {name: np.ascontiguousarray(inputs[full]) for name, full in _INS.items()}
    arrays["cos"], arrays["sin"] = rotation_tables()
    io = {name: nc.dram_tensor(f"in_{name}", a.shape, mybir.dt.from_np(a.dtype), kind="ExternalInput").ap()
          for name, a in arrays.items()}
    io["out"] = nc.dram_tensor("out_0", (B, T, D), F32, kind="ExternalOutput").ap()
    program(nc, io)
    ran = run_bass_kernel_spmd(nc, [{f"in_{name}": a for name, a in arrays.items()}], core_ids=[0])
    return ran.results[0]["out_0"]
```
